# Optimizing a Trainium2 kernel written in Bass

```python
import numpy as np
import jax
import jax.numpy as jnp

def _softmax(x, axis=-1):
    return jax.nn.softmax(x, axis=axis)

def _gelu(x):
    return jax.nn.gelu(x, approximate=True)

def _silu(x):
    return jax.nn.silu(x)

def _sigmoid(x):
    return jax.nn.sigmoid(x)

def _layernorm(x, axis=-1, eps=1e-05):
    m = jnp.mean(x, axis=axis, keepdims=True)
    v = jnp.var(x, axis=axis, keepdims=True)
    return (x - m) / jnp.sqrt(v + eps)

def _scatter_add(tgt, idx, src, axis=0):
    return tgt.at[idx].add(src)

def _segment_sum(src, seg, n):
    return jax.ops.segment_sum(src, seg, n)
kernel_name = 'mk_gnn_resnorm_d2_gnn_r32_ec4ff2'

def setup_inputs(seed: int=0):
    np.random.seed(seed)
    _w = jnp.asarray

    def _rec_inputs():
        import jax
        import jax.numpy as jnp
        _gk = jax.random.key(seed)
        x = -0.000202 + 1 * jax.random.normal(jax.random.fold_in(_gk, 1), (50000, 128), jnp.float32)
        _s = jax.random.randint(jax.random.fold_in(_gk, 2), (12500,), 0, 50000, jnp.int32)
        _d = jax.random.randint(jax.random.fold_in(_gk, 3), (12500,), 0, 50000, jnp.int32)
        _loop = jnp.arange(50000, dtype=jnp.int32)
        src = jnp.concatenate([_s, _d, _loop])
        dst = jnp.concatenate([_d, _s, _loop])
        _o = jnp.argsort(dst, stable=True)
        src = src[_o]
        dst = dst[_o]
        return (x, src, dst)
    x, src, dst = _rec_inputs()

    def _L0_gnn_setup():
        import jax, jax.numpy as jnp
        import numpy as np
        N_NODES = 50000
        N_EDGES = 18750
        D = 128
        D_OUT = 128
        key = jax.random.key(seed)
        ks = jax.random.split(key, 6)
        features = jax.random.normal(ks[0], (N_NODES, D), dtype=jnp.float32)
        edge_index = jax.random.randint(ks[1], (2, N_EDGES), 0, N_NODES, dtype=jnp.int64)

        def xavier(k, shape):
            gain = float(np.sqrt(2.0))
            fan_out, fan_in = shape
            bound = gain * float(np.sqrt(6.0 / (fan_in + fan_out)))
            return jax.random.uniform(k, shape, jnp.float32, -bound, bound)
        W_neigh = xavier(ks[2], (D, D))
        b_neigh = jnp.zeros((D,), jnp.float32)
        W_edge = xavier(ks[3], (D, 2 * D))
        b_edge = jnp.zeros((D,), jnp.float32)
        W_lin = xavier(ks[4], (D_OUT, 2 * D))
        b_lin = jnp.zeros((D_OUT,), jnp.float32)
        return {'features': features, 'edge_index': edge_index, 'W_neigh': W_neigh, 'b_neigh': b_neigh, 'W_edge': W_edge, 'b_edge': b_edge, 'W_lin': W_lin, 'b_lin': b_lin}
    _L0_gnn_all = _L0_gnn_setup()
    _L0_gnn_in = {k: v for k, v in _L0_gnn_all.items() if k in ('W_neigh', 'b_neigh', 'W_edge', 'b_edge', 'W_lin', 'b_lin')}
    del _L0_gnn_all

    def _L1_gnn_setup():
        import jax, jax.numpy as jnp
        import numpy as np
        N, E, D_IN, D_OUT = (50000, 25000, 128, 128)
        key = jax.random.key(seed)
        ks = jax.random.split(key, 16)
        row = jax.random.randint(ks[0], (E,), 0, N, dtype=jnp.int32)
        off = jax.random.randint(ks[1], (E,), 1, N, dtype=jnp.int32)
        col = (row + off) % N
        edge_index = jnp.stack([row, col], axis=0)
        s_in = 1.0 / np.sqrt(D_IN)
        s_out = 1.0 / np.sqrt(D_OUT)
        u = lambda k, shape, s: jax.random.uniform(k, shape, jnp.float32, -s, s)
        return {'x': jax.random.normal(ks[2], (N, D_IN), jnp.float32), 'edge_index': edge_index, 'W_hp': u(ks[3], (D_OUT, D_IN), s_in), 'b_hp': u(ks[4], (D_OUT,), s_in), 'W_lp': u(ks[5], (D_OUT, D_IN), s_in), 'b_lp': u(ks[6], (D_OUT,), s_in), 'W_i': u(ks[7], (D_OUT, D_IN), s_in), 'b_i': u(ks[8], (D_OUT,), s_in), 'wlin_h': u(ks[9], (D_OUT,), s_out), 'blin_h': u(ks[10], (), s_out), 'wlin_l': u(ks[11], (D_OUT,), s_out), 'blin_l': u(ks[12], (), s_out), 'wlin_i': u(ks[13], (D_OUT,), s_out), 'blin_i': u(ks[14], (), s_out)}
    _L1_gnn_all = _L1_gnn_setup()
    _L1_gnn_in = {k: v for k, v in _L1_gnn_all.items() if k in ('W_hp', 'b_hp', 'W_lp', 'b_lp', 'W_i', 'b_i', 'wlin_h', 'blin_h', 'wlin_l', 'blin_l', 'wlin_i', 'blin_i')}
    del _L1_gnn_all
    return {'x': x, 'src': src, 'dst': dst, 'L0_gnn_W_neigh': _L0_gnn_in['W_neigh'], 'L0_gnn_b_neigh': _L0_gnn_in['b_neigh'], 'L0_gnn_W_edge': _L0_gnn_in['W_edge'], 'L0_gnn_b_edge': _L0_gnn_in['b_edge'], 'L0_gnn_W_lin': _L0_gnn_in['W_lin'], 'L0_gnn_b_lin': _L0_gnn_in['b_lin'], 'L1_gnn_W_hp': _L1_gnn_in['W_hp'], 'L1_gnn_b_hp': _L1_gnn_in['b_hp'], 'L1_gnn_W_lp': _L1_gnn_in['W_lp'], 'L1_gnn_b_lp': _L1_gnn_in['b_lp'], 'L1_gnn_W_i': _L1_gnn_in['W_i'], 'L1_gnn_b_i': _L1_gnn_in['b_i'], 'L1_gnn_wlin_h': _L1_gnn_in['wlin_h'], 'L1_gnn_blin_h': _L1_gnn_in['blin_h'], 'L1_gnn_wlin_l': _L1_gnn_in['wlin_l'], 'L1_gnn_blin_l': _L1_gnn_in['blin_l'], 'L1_gnn_wlin_i': _L1_gnn_in['wlin_i'], 'L1_gnn_blin_i': _L1_gnn_in['blin_i']}

def reference(x, src, dst, L0_gnn_W_neigh, L0_gnn_b_neigh, L0_gnn_W_edge, L0_gnn_b_edge, L0_gnn_W_lin, L0_gnn_b_lin, L1_gnn_W_hp, L1_gnn_b_hp, L1_gnn_W_lp, L1_gnn_b_lp, L1_gnn_W_i, L1_gnn_b_i, L1_gnn_wlin_h, L1_gnn_blin_h, L1_gnn_wlin_l, L1_gnn_blin_l, L1_gnn_wlin_i, L1_gnn_blin_i):
    import jax
    import jax.numpy as jnp

    def _L0_gnn_ref(features, edge_index, W_neigh, b_neigh, W_edge, b_edge, W_lin, b_lin):
        import jax, jax.numpy as jnp
        import numpy as np
        N_NODES = 50000
        N_EDGES = 18750
        D = 128
        D_OUT = 128
        n = features.shape[0]
        dst = edge_index[0]
        src = edge_index[1]
        h = features @ W_neigh.T + b_neigh
        h_src = h[src]
        edge_feats = jnp.abs(h[dst] - h_src)
        new_h = jnp.concatenate([h_src, edge_feats], axis=-1) @ W_edge.T + b_edge
        seg_sum = jax.ops.segment_sum(new_h, dst, num_segments=n)
        cnt = jax.ops.segment_sum(jnp.ones((dst.shape[0],), jnp.float32), dst, num_segments=n)[:, None]
        s = (h + seg_sum) / jnp.maximum(cnt, 1.0)
        z = jnp.concatenate([features, s], axis=-1) @ W_lin.T + b_lin
        return z

    def _L1_gnn_ref(x, edge_index, W_hp, b_hp, W_lp, b_lp, W_i, b_i, wlin_h, blin_h, wlin_l, blin_l, wlin_i, blin_i):
        import jax, jax.numpy as jnp
        import numpy as np
        N, E, D_IN, D_OUT = (50000, 25000, 128, 128)
        n = x.shape[0]
        row, col = (edge_index[0], edge_index[1])
        loop = jnp.arange(n, dtype=row.dtype)
        rf = jnp.concatenate([row, loop])
        cf = jnp.concatenate([col, loop])
        w = jnp.ones(rf.shape[0], x.dtype)
        deg = jax.ops.segment_sum(w, cf, num_segments=n)
        dinv = jnp.where(deg > 0, deg ** (-0.5), 0.0).astype(x.dtype)
        w = dinv[rf] * w * dinv[cf]

        def agg(h):
            return jax.ops.segment_sum(w[:, None] * h[rf], cf, num_segments=n)
        h_hp = x @ W_hp.T + b_hp
        H_hp = jax.nn.relu(h_hp - agg(h_hp))
        h_lp = x @ W_lp.T + b_lp
        H_lp = jax.nn.relu(agg(h_lp))
        H_i = jax.nn.relu(x @ W_i.T + b_i)
        a_h = jax.nn.sigmoid(H_hp @ wlin_h + blin_h)
        a_l = jax.nn.sigmoid(H_lp @ wlin_l + blin_l)
        a_i = jax.nn.sigmoid(H_i @ wlin_i + blin_i)
        return a_h[:, None] * H_hp + a_l[:, None] * H_lp + a_i[:, None] * H_i
    edge_index = jnp.stack([src, dst])
    x = _layernorm(x + _L0_gnn_ref(x, edge_index, L0_gnn_W_neigh, L0_gnn_b_neigh, L0_gnn_W_edge, L0_gnn_b_edge, L0_gnn_W_lin, L0_gnn_b_lin), axis=-1)
    x = _layernorm(x + _L1_gnn_ref(x, edge_index, L1_gnn_W_hp, L1_gnn_b_hp, L1_gnn_W_lp, L1_gnn_b_lp, L1_gnn_W_i, L1_gnn_b_i, L1_gnn_wlin_h, L1_gnn_blin_h, L1_gnn_wlin_l, L1_gnn_blin_l, L1_gnn_wlin_i, L1_gnn_blin_i), axis=-1)
    return x

_drawn_inputs = setup_inputs


def setup_inputs(seed=0):
    import zlib

    import numpy as np

    out = dict(_drawn_inputs(seed))
    spreads = {'L0_gnn_b_neigh': (0.0, 0.1), 'L0_gnn_b_edge': (0.0, 0.1), 'L0_gnn_b_lin': (0.0, 0.1)}
    factors = {'L1_gnn_b_hp': 64.0,
     'L1_gnn_b_lp': 3.204,
     'L1_gnn_b_i': 3.038,
     'L1_gnn_wlin_h': 43.343,
     'L1_gnn_wlin_l': 4.191,
     'L1_gnn_wlin_i': 4.001}
    for name, (base, spread) in spreads.items():
        noise = np.random.default_rng([zlib.crc32(name.encode()), seed]).standard_normal(out[name].shape)
        drawn = base * np.exp(spread * noise) if base else spread * noise
        out[name] = jnp.asarray(drawn.astype(out[name].dtype))
    for name, factor in factors.items():
        out[name] = (out[name] * factor).astype(out[name].dtype)
    return out
```

```python
def build(nc, x_d, src_d, dst_d, wn_d, bn_d, we_d, be_d, wl_d, bl_d,
          whp_d, bhp_d, wlp_d, blp_d, wi_d, bi_d, wvh_d, bvh_d, wvl_d, bvl_d, wvi_d, bvi_d, out_d):
    from contextlib import ExitStack
    import concourse.bass as bass
    from concourse import mybir

    f32, f16, i32 = mybir.dt.float32, mybir.dt.float16, mybir.dt.int32
    ALU, ACT, AX = mybir.AluOpType, mybir.ActivationFunctionType, mybir.AxisListType
    P = 128
    N, D = x_d.shape
    E = src_d.shape[0]
    TG = 4
    NG = -(-N // (P * TG))
    NT = NG * TG
    NPAD = NT * P
    CB = 4
    NC = -(-E // P)
    NCP = -(-NC // CB) * CB
    NB = -(-NC // P)
    W = D + 1
    OOB = 60000
    HALF = 2048
    EPS = 1e-5
    assert NPAD + P > N and OOB > N and N * P < 2 ** 24

    h1_d = nc.dram_tensor("h1_scratch", (N, W), f32).ap()
    rows_d = nc.dram_tensor("rows_scratch", (2, NPAD), f32).ap()
    acc0_d = nc.dram_tensor("acc0_scratch", (NPAD + P, 2 * D), f32).ap()
    acc1_d = nc.dram_tensor("acc1_scratch", (NPAD + P, W), f32).ap()

    ctx = ExitStack()
    with ctx:
        def sb(name, shape, dt=f32):
            return ctx.enter_context(nc.sbuf_tensor(name, shape, dt))

        def sem(name):
            return ctx.enter_context(nc.semaphore(name))

        psum = ctx.enter_context(nc.psum_tensor("psum", [P, 8 * 512], f32))

        def bank(b, n=1):
            return psum[:, 512 * b:512 * (b + n)]

        ident = sb("ident", [P, P])
        ident16 = sb("ident16", [P, P], f16)
        neg_ident = sb("neg_ident", [P, P])
        iota_i = sb("iota_i", [P, NCP], i32)
        iota = sb("iota", [P, P])
        iota_t = sb("iota_t", [P, NT], f16)
        part = sb("part", [P, 1])
        before = sb("before", [P, P])
        before16 = sb("before16", [P, P], f16)
        notbefore16 = sb("notbefore16", [P, P], f16)
        after = sb("after", [P, P])
        row0 = sb("row0", [P, P])
        ones = sb("ones", [P, P])
        minus_half = sb("minus_half", [P, TG])
        zeros = sb("zeros", [P, TG, 2 * D])

        wn = sb("wn", [P, D])
        we = sb("we", [P, 2 * D])
        wl = sb("wl", [P, 2 * D])
        w1 = sb("w1", [P, 3, D])
        wnT = sb("wnT", [P, D])
        wl2T = sb("wl2T", [P, D])
        wz = sb("wz", [P, 2 * D])
        wmid = sb("wmid", [P, D])
        wsum = sb("wsum", [P, D])
        wabs = sb("wabs", [P, D])
        wx = sb("wx", [P, 2 * D])
        wg = sb("wg", [P, 2 * D])
        bcol = sb("bcol", [P, 2])
        bias3 = sb("bias3", [3, D])
        brow = sb("brow", [1, 2, D])
        bx = sb("bx", [1, 2 * D])
        vec_row = sb("vec_row", [1, 5 * D + 3])
        vec = sb("vec", [P, 5 * D + 3])
        ones_row = sb("ones_row", [1, P])

        sort_area = sb("sort_area", [P, 13 * NCP])

        s_raw = sb("s_raw", [P, NB, P], i32)
        d_raw = sb("d_raw", [P, NB, P], i32)
        nat_area = sb("nat_area", [P, 2 * NB * P])
        s_nat = nat_area[:, 0:NB * P].rearrange("p (b n) -> p b n", b=NB)
        d_nat = nat_area[:, NB * P:2 * NB * P].rearrange("p (b n) -> p b n", b=NB)
        t0_raw = sb("t0_raw", [P, NB], i32)
        t0_col = sb("t0_col", [P, 2, NB])
        s_i = sb("s_i", [P, NCP], i32)
        d_i = sb("d_i", [P, NCP], i32)
        tmp_i = sb("tmp_i", [P, NCP], i32)
        tmp2_i = sb("tmp2_i", [P, NCP], i32)
        td = sb("td", [P, NCP])
        ld = sb("ld", [P, NCP])
        hi = sort_area[:, 0 * NCP:1 * NCP]
        lo = sort_area[:, 1 * NCP:2 * NCP]
        valid = sb("valid", [P, NCP])
        selfe = sort_area[:, 2 * NCP:3 * NCP]
        other = sort_area[:, 3 * NCP:4 * NCP]
        in0 = sb("in0", [P, NCP])
        in1 = sb("in1", [P, NCP])
        t0 = sort_area[:, 4 * NCP:5 * NCP]
        cols = sort_area[:, 5 * NCP:6 * NCP]
        n_first = sort_area[:, 6 * NCP:7 * NCP]
        o_first = sort_area[:, 7 * NCP:8 * NCP]
        pre = sort_area[:, 8 * NCP:9 * NCP]
        nxt = sort_area[:, 9 * NCP:10 * NCP]
        start = sort_area[:, 10 * NCP:11 * NCP]
        rank = sort_area[:, 11 * NCP:12 * NCP]
        ta = sb("ta", [P, NCP])
        tb = sb("tb", [P, NCP])
        bad = sort_area[:, 12 * NCP:13 * NCP]
        place_v = sb("place_v", [P, NCP, 4], f16)
        count_v = sb("count_v", [P, NCP, 4], f16)
        place_oh = sb("place_oh", [P, 2, CB, P], f16)
        local_oh = sb("local_oh", [P, 2, CB, P], f16)
        fields = sb("fields", [P, 8, P], f16)
        fieldsT = sb("fieldsT", [P, 8, P], f16)
        fold = sb("fold", [P, 2, NT], f16)

        slot_hi = sb("slot_hi", [P, NT])
        slot_lo = sb("slot_lo", [P, NT])
        slot_i = sb("slot_i", [P, NT], i32)
        slot_j = sb("slot_j", [P, NT], i32)
        slot_k = sb("slot_k", [P, NT], i32)
        slot_f = sb("slot_f", [P, NT])
        occ = sb("occ", [P, NT])
        idx0 = sb("idx0", [P, NT], i32)
        loc0 = sb("loc0", [P, NT])
        idx1 = sb("idx1", [P, NT], i32)
        loc1 = sb("loc1", [P, NT])
        n_self = sb("n_self", [P, NT])
        n_in = sb("n_in", [P, NT])
        n_out = sb("n_out", [P, NT])
        dinv = sb("dinv", [P, NT])
        self_w = sb("self_w", [P, NT])
        rc = sb("rc", [P, NT])
        some = sb("some", [P, NT])
        statT = sb("statT", [P, 2, 4, P])
        sort_f = sb("sort_f", [P, NT, 4])
        sort_s = sb("sort_s", [P, 2, CB, 4])
        tile_oh = sb("tile_oh", [P, CB, NT], f16)
        src_oh = sb("src_oh", [P, CB, P], f16)
        rank_oh = sb("rank_oh", [P, CB, P], f16)
        hi_oh = sb("hi_oh", [P, CB, P], f16)
        lo_oh = sb("lo_oh", [P, CB, P], f16)
        junk = sb("junk", [P, 2, NT], f16)
        rank0 = sb("rank0", [P, NT])
        rank_s = sb("rank_s", [P, 2, CB])
        spare = sb("spare", [P, 5])
        badsum = sb("badsum", [P, 2])
        okv = sb("okv", [P, 1])
        flag = sb("flag", [P, 1], i32)

        xg = sb("xg", [P, 2, TG, D])
        gx = sb("gx", [P, 2, TG, W])
        gidx = sb("gidx", [P, 2, TG], i32)
        oh = sb("oh", [P, 2, TG, P])
        ohT = sb("ohT", [P, TG, P])
        xT = sb("xT", [P, TG, P])
        dT = sb("dT", [P, TG, P])
        hd = sb("hd", [P, TG, P])
        s1T = sb("s1T", [P, TG, P])
        s2T = sb("s2T", [P, TG, P])
        row3 = sb("row3", [3, 2, TG * P])
        p2 = sb("p2", [P, TG, D])
        res = sb("res", [P, TG, D])
        stats = sb("stats", [P, TG, 6])
        mv = sb("mv", [P, TG, 2])
        vare = sb("vare", [P, TG])
        rstd = sb("rstd", [P, TG])
        h1g = sb("h1g", [P, 2, TG, W])
        accg = sb("accg", [P, TG, 2 * D])
        locs = sb("locs", [P, 2, TG])
        col4 = sb("col4", [P, 2, 3, TG])
        diag = sort_area[:, 0:1024].rearrange("p (s t n) -> p s t n", s=2, t=TG)
        gam = sb("gam", [P, TG])
        gs = sort_area[:, 1024:2048].rearrange("p (t n) -> p t n", t=TG)
        q = sort_area[:, 2048:3072].rearrange("p (t n) -> p t n", t=TG)
        y = sort_area[:, 3072:4608].rearrange("p (t k n) -> p t k n", t=TG, k=3)
        ay = sort_area[:, 4608:6144].rearrange("p (k t n) -> p k t n", t=TG, k=3)
        dots = sb("dots", [P, 3, TG])
        gates = sb("gates", [P, 3, TG])
        dot_junk = nat_area[:, 0:3 * TG * D // 2].bitcast(f16).rearrange("p (k t n) -> p k t n", k=3, t=TG)
        outg = sort_area[:, 6144:7168].rearrange("p (s t n) -> p s t n", s=2, t=TG)

        e_idx = sb("e_idx", [P, 2], i32)
        e_key = sb("e_key", [P, 1])
        e_ok = sb("e_ok", [P, 1])
        e_rows = sb("e_rows", [P, 2, W])
        e_diff = sb("e_diff", [P, D])
        e_diffT = sb("e_diffT", [P, D])
        e_pay = sb("e_pay", [P, 2 * D])
        e_keyb = sb("e_keyb", [P, P])
        e_same = sb("e_same", [P, P])
        e_junk = sb("e_junk", [P, P])
        e_prev = sb("e_prev", [P, 1])
        e_lead = sb("e_lead", [P, 1])
        e_tgt = sb("e_tgt", [P, 1])
        e_tgti = sb("e_tgti", [P, 1], i32)
        e_sum = sb("e_sum", [P, 2 * D])
        g_oh = tile_oh[:, 0:2]
        g_loh = rank_oh[:, 0:2]

        wload = sem("weights_loaded")
        bload = sem("z_biases_loaded")
        eload = sem("edges_loaded")
        iotas = sem("iotas_ready")
        consts = sem("constants_ready")
        vchain = sem("vector_steps")
        pchain = sem("pool_steps")
        zeroed = sem("buffers_zeroed")
        wT_ps = sem("weights_transposed")
        wT_sb = sem("weights_copied")
        nat = sem("edges_as_float")
        edgeT = sem("edges_transposed")
        t_ready = sem("dst_tiles_ready")
        t0_ps = sem("first_tiles_summed")
        masks = sem("masks_ready")
        sums_ps = sem("chunk_sums_ready")
        pre_rd = sem("chunk_sums_read")
        lower_ps = sem("ranks_in_chunk_ready")
        place = sem("place_onehots_ready")
        placed = sem("chunks_placed")
        block_rd = sem("block_fields_copied")
        fieldT = sem("block_fields_transposed")
        fieldT_sb = sem("block_transposes_copied")
        fold_rdy = sem("fold_onehots_ready")
        folded = sem("blocks_folded")
        tab1 = sem("table1_ready")
        s_staged = sem("sort_columns_staged")
        s_used = sem("sort_columns_used")
        s_oh = sem("sort_tile_onehots")
        s_src = sem("sort_src_onehots")
        s_rankps = sem("sort_ranks_in_psum")
        s_rank = sem("sort_ranks_read")
        s_kept = sem("sort_ranks_kept")
        s_roh = sem("sort_rank_onehots")
        s_val = sem("sort_value_onehots")
        s_done = sem("sort_columns_done")
        bad_rdy = sem("bad_sums_ready")
        bad_ps = sem("bad_total_ready")
        flagged = sem("flag_ready")
        stat_rdy = sem("stats_ready")
        dinv_rdy = sem("dinv_ready")
        statT_ps = sem("stats_transposed")
        statT_sb = sem("stats_transposed_copied")
        rows_st = sem("stat_rows_stored")

        xl = [sem(f"x_loaded{s}") for s in range(2)]
        rl = [sem(f"rows_loaded{s}") for s in range(2)]
        gidx_rdy = sem("gather_indices_ready")
        gat = [sem(f"rows_gathered{s}") for s in range(2)]
        oh_rdy = sem("onehots_ready")
        trans = sem("l0_transposed")
        diag0 = sem("l0_diagonals_ready")
        n_self_rdy = sem("self_counts_ready")
        xT_sb = sem("l0_xT_copied")
        ohT_sb = sem("l0_onehotT_copied")
        dT_ps = sem("l0_differences_ready")
        dT_sb = sem("l0_differences_copied")
        hd_ps = sem("l0_edge_products_ready")
        hd_sb = sem("l0_edge_abs_ready")
        s1_ps = sem("l0_sums_ready")
        s1_sb = sem("l0_sums_copied")
        s2_ps = sem("l0_abs_sums_ready")
        s2_sb = sem("l0_abs_sums_copied")
        z_ps = sem("l0_z_ready")
        p2_sb = sem("l0_p2_scaled")
        z_rd = sem("l0_z_read")
        var0 = sem("l0_var_ready")
        rstd0 = sem("l0_rstd_ready")
        h1_rdy = sem("l0_rows_ready")
        h1_st = [sem(f"l0_rows_stored{s}") for s in range(2)]

        hl = [sem(f"l1_rows_loaded{s}") for s in range(2)]
        gat1 = [sem(f"l1_rows_gathered{s}") for s in range(2)]
        gidx1 = sem("l1_gather_indices_ready")
        cols_rdy = sem("l1_columns_staged")
        oh1 = sem("l1_onehots_ready")
        diag_rdy = sem("l1_diagonals_ready")
        yT_ps = sem("l1_yT_ready")
        yT_sb = sem("l1_yT_copied")
        hT_ps = sem("l1_hT_ready")
        hT_sb = sem("l1_hT_copied")
        g_ps = sem("l1_g_ready")
        g_sb = sem("l1_g_scaled")
        x_ps = sem("l1_x_ready")
        x_rd = sem("l1_x_read")
        gam_rd = sem("l1_gamma_read")
        dots_rdy = sem("l1_dots_ready")
        gate_rdy = sem("l1_gates_ready")
        ay_rdy = sem("l1_gated_ready")
        ay_rd = sem("l1_gated_read")
        var1 = sem("l1_var_ready")
        rstd1 = sem("l1_rstd_ready")
        out_rdy = sem("l1_out_ready")
        out_st = [sem(f"l1_out_stored{s}") for s in range(2)]

        accz = sem("gen_accumulators_zeroed")
        accl = sem("gen_accumulators_loaded")
        acc_rd = sem("gen_accumulators_read")
        g_chain = sem("gen_vector_steps")
        g_ohr = sem("gen_onehots_ready")
        g_cnt = sem("gen_counted")
        g_take = sem("gen_waits_taken")
        g_idx = sem("gen_indices_ready")
        g_gat = sem("gen_rows_gathered")
        g_dif = sem("gen_differences_ready")
        g_pe = sem("gen_products_ready")
        g_v = sem("gen_vector_ready")
        g_sct = sem("gen_rows_added")
        g_hst = sem("gen_l0_stores_seen")

        block = ctx.enter_context(nc.Block())

        class Steps:

            def __init__(self, eng, s):
                self.eng, self.s, self.n = eng, s, 0

            def mark(self, ins):
                self.n += 1
                ins.then_inc(self.s, 1)

            def link(self, ins):
                self.mark(ins)
                self.eng.wait_ge(self.s, self.n)

        LAST = N - (NG - 1) * P * TG
        LT, LR = LAST // P, LAST % P

        def group_parts(dram, g, tile):
            if not isinstance(g, int) or g < NG - 1:
                return [(dram[bass.ds(g * (P * TG), P * TG), :].rearrange("(t p) d -> p t d", p=P), tile[:, 0:TG, :])]
            at = (NG - 1) * P * TG
            return [(dram[at:at + LT * P, :].rearrange("(t p) d -> p t d", p=P), tile[:, 0:LT, :]),
                    (dram[at + LT * P:N, :], tile[0:LR, LT, :])]

        LAST_PARTS = 2

        @block.sync
        def _(sp):
            for t, d in ((wn, wn_d), (we, we_d), (wl, wl_d), (w1[:, 0, :], whp_d), (w1[:, 1, :], wlp_d), (w1[:, 2, :], wi_d)):
                sp.dma_start(t[:] if t in (wn, we, wl) else t, d[:, :]).then_inc(wload, 16)
            for k, d in enumerate((bn_d, be_d)):
                sp.dma_start(bcol[:, k:k + 1], d.rearrange("(p o) -> p o", o=1)).then_inc(wload, 16)
            row = lambda d: d.rearrange("(o n) -> o n", o=1)
            for k, d in enumerate((bhp_d, bi_d)):
                sp.dma_start(bx[0:1, k * D:(k + 1) * D], row(d)).then_inc(wload, 16)
            for k, d in enumerate((bhp_d, blp_d, wvh_d, wvl_d, wvi_d)):
                sp.dma_start(vec_row[0:1, k * D:(k + 1) * D], row(d)).then_inc(wload, 16)
            for k, d in enumerate((bvh_d, bvl_d, bvi_d)):
                sp.dma_start(vec_row[0:1, 5 * D + k:5 * D + k + 1], row(d)).then_inc(wload, 16)
            sp.wait_ge(zeroed, 2)
            full = NB - 1
            for raw, d in ((s_raw, src_d), (d_raw, dst_d)):
                sp.dma_start(raw[:, 0:full, :], d[0:full * P * P].rearrange("(b k p) -> k b p", k=P, p=P)).then_inc(eload, 16)
                left = (E - full * P * P) // P
                sp.dma_start(raw[0:left, full, :], d[full * P * P:(full * P + left) * P].rearrange("(k p) -> k p", p=P)).then_inc(eload, 16)
                sp.dma_start(raw[left:left + 1, full, 0:E % P], d[E - E % P:E].rearrange("(o p) -> o p", o=1)).then_inc(eload, 16)
            sp.wait_ge(zeroed, 4)
            sp.dma_start(bias3[2:3, :], row(bl_d)).then_inc(bload, 16)
            sp.wait_ge(wT_sb, 3)
            sp.dma_start(bias3[0:1, :], brow[0:1, 0, :]).then_inc(bload, 16)
            sp.dma_start(bias3[1:2, :], brow[0:1, 1, :]).then_inc(bload, 16)
            sp.wait_ge(flagged, 1)
            general = sp.value_load(flag[0:1, 0:1], min_val=0, max_val=1)
            with sp.If(general > 0):
                for g in range(NG):
                    sp.dma_start(acc0_d[g * 512:(g + 1) * 512, :].rearrange("(t p) d -> p t d", p=P), zeros[:]).then_inc(accz, 16)
                    sp.dma_start(acc1_d[g * 512:(g + 1) * 512, :].rearrange("(t p) d -> p t d", p=P), zeros[:, :, 0:W]).then_inc(accz, 16)
                sp.dma_start(acc0_d[NPAD:NPAD + P, :], zeros[:, 0, :]).then_inc(accz, 16)
                sp.dma_start(acc1_d[NPAD:NPAD + P, :], zeros[:, 0, 0:W]).then_inc(accz, 16)
                sp.wait_ge(accz, 16 * (2 * NG + 2))
            sp.wait_ge(statT_sb, 1)
            NB4 = -(-NT // P)
            for k in range(2):
                for b in range(NB4):
                    n = min(P, NT - b * P)
                    sp.dma_start(rows_d[k, b * P * P:(b * P + n) * P].rearrange("(t p) -> t p", p=P),
                                 statT[0:n, k, b, :]).then_inc(rows_st, 16)
            with sp.If(general > 0):
                sp.wait_ge(g_sct, 16 * NC)

            sp.wait_ge(rows_st, 16 * 2 * NB4)

            def l0_load(g, s, first):
                if not first:
                    sp.wait_ge(z_ps, g - 1)
                for a, b in group_parts(x_d, g, xg[:, s]):
                    sp.dma_start(b, a).then_inc(xl[s], 16)
                sp.dma_start(row3[0:2, s, :], rows_d[:, bass.ds(g * (P * TG), P * TG)]).then_inc(rl[s], 16)

            def acc_load(acc_d, width, g, base):
                with sp.If(general > 0):
                    if not (isinstance(g, int) and g + base == 0):
                        sp.wait_ge(acc_rd, g + base)
                    sp.dma_start(accg[:, :, 0:width],
                                 acc_d[bass.ds(g * (P * TG), P * TG), :].rearrange("(t p) d -> p t d", p=P)).then_inc(accl, 16)

            def l0_store(g, s):
                sp.wait_ge(h1_rdy, g + 1)
                for a, b in group_parts(h1_d, g, h1g[:, s]):
                    sp.dma_start(a, b).then_inc(h1_st[s], 16)

            l0_load(0, 0, True)
            acc_load(acc0_d, 2 * D, 0, 0)
            l0_load(1, 1, True)
            acc_load(acc0_d, 2 * D, 1, 0)
            with sp.Fori(0, NG // 2 - 2) as i:
                for s in range(2):
                    l0_load(2 * i + (2 + s), s, False)
                    acc_load(acc0_d, 2 * D, 2 * i + (2 + s), 0)
                    l0_store(2 * i + s, s)
            for g in (NG - 2, NG - 1):
                l0_load(g, g % 2, False)
                acc_load(acc0_d, 2 * D, g, 0)
                l0_store(g - 2, g % 2)
            for g in (NG - 2, NG - 1):
                l0_store(g, g % 2)
            for s in range(2):
                sp.wait_ge(h1_st[s], 16 * (NG // 2 + (LAST_PARTS - 1) * s))
            with sp.If(general > 0):
                sp.wait_ge(g_sct, 16 * 2 * NC)

            def l1_load(g, s, first):
                if not first:
                    sp.wait_ge(ay_rd, g - 1)
                for a, b in group_parts(h1_d, g, h1g[:, s]):
                    sp.dma_start(b, a).then_inc(hl[s], 16)

            def l1_store(g, s):
                sp.wait_ge(out_rdy, g + 1)
                for a, b in group_parts(out_d, g, outg[:, s]):
                    sp.dma_start(a, b).then_inc(out_st[s], 16)

            l1_load(0, 0, True)
            acc_load(acc1_d, W, 0, NG)
            l1_load(1, 1, True)
            acc_load(acc1_d, W, 1, NG)
            with sp.Fori(0, NG // 2 - 2) as i:
                for s in range(2):
                    l1_load(2 * i + (2 + s), s, False)
                    acc_load(acc1_d, W, 2 * i + (2 + s), NG)
                    l1_store(2 * i + s, s)
            for g in (NG - 2, NG - 1):
                l1_load(g, g % 2, False)
                acc_load(acc1_d, W, g, NG)
                l1_store(g - 2, g % 2)
            for g in (NG - 2, NG - 1):
                l1_store(g, g % 2)
            for s in range(2):
                sp.wait_ge(out_st[s], 16 * (NG // 2 + (LAST_PARTS - 1) * s))

        @block.gpsimd
        def _(pool):
            st = Steps(pool, pchain)
            last_node, last_row = pool.to_reg(N - 1), pool.to_reg(NPAD + P - 1)
            nc.gpsimd.memset(s_raw[:], N - 1).then_inc(zeroed, 1)
            nc.gpsimd.memset(d_raw[:], N - 1).then_inc(zeroed, 1)
            nc.gpsimd.memset(row3[:], 1.0).then_inc(zeroed, 1)
            nc.gpsimd.memset(ones_row[:], 1.0).then_inc(zeroed, 1)
            nc.gpsimd.iota(iota_i[:], pattern=[[P, NCP]], base=0, channel_multiplier=1).then_inc(iotas, 1)
            nc.gpsimd.iota(tmp_i[:], pattern=[[1, NCP]], base=0, channel_multiplier=0).then_inc(iotas, 1)
            nc.gpsimd.memset(ones[:], 1.0).then_inc(pchain, 1)
            nc.gpsimd.memset(minus_half[:], -0.5)
            nc.gpsimd.memset(zeros[:], 0.0)
            nc.gpsimd.memset(gx[:], 0.0)
            nc.gpsimd.memset(accg[:], 0.0)
            nc.gpsimd.memset(e_rows[:], 0.0)
            nc.gpsimd.memset(xg[:], 0.0)
            nc.gpsimd.memset(h1g[:], 0.0)
            pool.wait_ge(pchain, 1)
            st.n = 1
            st.mark(nc.gpsimd.affine_select(out=before[:], in_=ones[:], compare_op=ALU.is_gt, fill=0.0, base=0,
                                            pattern=[[1, P]], channel_multiplier=-1))
            st.mark(nc.gpsimd.affine_select(out=after[:], in_=ones[:], compare_op=ALU.is_gt, fill=0.0, base=0,
                                            pattern=[[-1, P]], channel_multiplier=1))
            st.mark(nc.gpsimd.affine_select(out=ident[:], in_=ones[:], compare_op=ALU.is_equal, fill=0.0, base=0,
                                            pattern=[[1, P]], channel_multiplier=-1))
            st.link(nc.gpsimd.affine_select(out=row0[:], in_=ones[:], compare_op=ALU.is_equal, fill=0.0, base=0,
                                            pattern=[[0, P]], channel_multiplier=1))
            nc.gpsimd.tensor_copy(before16[:], before[:]).then_inc(consts, 1)
            nc.gpsimd.tensor_copy(ident16[:], ident[:]).then_inc(consts, 1)
            nc.gpsimd.tensor_scalar(neg_ident[:], ident[:], -1.0, 0.0, ALU.mult, ALU.add).then_inc(consts, 1)
            nc.gpsimd.tensor_scalar(notbefore16[:], before[:], -1.0, 1.0, ALU.mult, ALU.add).then_inc(consts, 1)

            def src_onehots(i, s):
                pool.wait_ge(s_staged, i + 1)
                for c in range(CB):
                    if not (isinstance(i, int) and i == 0):
                        pool.wait_ge(s_done, CB * i + (c + 1 - CB))
                        nc.gpsimd.tensor_tensor(spare[0:1, c:c + 1], ones[0:1, 0:1], ones[0:1, 0:1], ALU.add)
                    nc.gpsimd.tensor_scalar(src_oh[:, c, :], iota[:], sort_s[:, s, c, 1:2], None, ALU.is_equal).then_inc(s_src, 1)

            for i in range(2):
                src_onehots(i, i)
            with pool.Fori(1, NT // CB // 2) as i:
                for s in range(2):
                    src_onehots(2 * i + s, s)

            pool.wait_ge(flagged, 1)
            general = pool.value_load(flag[0:1, 0:1], min_val=0, max_val=1)

            pool.wait_ge(stat_rdy, 1)
            nc.gpsimd.tensor_tensor(dinv[:], slot_f[:], slot_hi[:], ALU.pow).then_inc(dinv_rdy, 1)

            def take(idx_count, count):
                if not isinstance(count, int):
                    pool.wait_ge(g_take, count)
                    pool.wait_ge(g_idx, idx_count)
                nc.gpsimd.tensor_tensor(spare[0:1, 2:3], ones[0:1, 0:1], ones[0:1, 0:1], ALU.add).then_inc(g_take, 1)

            def edge_rows(count, rows, width, acc, payload):
                take(count, count)
                for k, (table, col) in enumerate(rows):
                    nc.gpsimd.indirect_dma_start(out=e_rows[:, k, 0:width], out_offset=None, in_=table,
                                                 in_offset=bass.IndirectOffsetOnAxis(ap=e_idx[:, col:col + 1], axis=0),
                                                 bounds_check=last_node, oob_is_err=False).then_inc(g_gat, 16)

            with pool.If(general > 0):
                pool.wait_ge(accz, 16 * (2 * NG + 2))
                take(0, 0)
                with pool.Fori(0, NC) as k:
                    edge_rows(2 * k + 1, [(x_d, 0), (x_d, 1)], D, acc0_d, e_sum)
                    take(2 * k + 2, 2 * k + 2)
                    nc.gpsimd.indirect_dma_start(out=acc0_d, out_offset=bass.IndirectOffsetOnAxis(ap=e_tgti[:, 0:1], axis=0),
                                                 in_=e_sum[:, 0:2 * D], in_offset=None, bounds_check=last_row,
                                                 compute_op=ALU.add).then_inc(g_sct, 16)
                    pool.wait_ge(g_sct, 16 * k + 16)

            def gathers(g, s, table, width, sems, ready):
                pool.wait_ge(ready, g + 1)
                if not isinstance(g, int):
                    nc.gpsimd.tensor_tensor(spare[0:1, s:s + 1], ones[0:1, 0:1], ones[0:1, 0:1], ALU.add)
                for t in range(TG):
                    nc.gpsimd.indirect_dma_start(out=gx[:, s, t, 0:width], out_offset=None, in_=table,
                                                 in_offset=bass.IndirectOffsetOnAxis(ap=gidx[:, s, t:t + 1], axis=0),
                                                 bounds_check=last_node, oob_is_err=False).then_inc(sems[s], 16)

            def rstds(g, var, done):
                pool.wait_ge(var, g + 1)
                nc.gpsimd.tensor_tensor(rstd[:], vare[:], minus_half[:], ALU.pow).then_inc(done, 1)

            gathers(0, 0, x_d, D, gat, gidx_rdy)
            gathers(1, 1, x_d, D, gat, gidx_rdy)
            with pool.Fori(0, NG // 2 - 1) as i:
                for s in range(2):
                    rstds(2 * i + s, var0, rstd0)
                    gathers(2 * i + (2 + s), s, x_d, D, gat, gidx_rdy)
            for g in (NG - 2, NG - 1):
                rstds(g, var0, rstd0)

            for s in range(2):
                pool.wait_ge(h1_st[s], 16 * (NG // 2 + (LAST_PARTS - 1) * s))
            with pool.If(general > 0):
                with pool.Fori(0, NC) as k:
                    edge_rows(2 * k + (2 * NC + 1), [(h1_d, 0)], W, acc1_d, e_sum)
                    take(2 * k + (2 * NC + 2), 2 * k + (2 * NC + 2))
                    nc.gpsimd.indirect_dma_start(out=acc1_d, out_offset=bass.IndirectOffsetOnAxis(ap=e_tgti[:, 0:1], axis=0),
                                                 in_=e_sum[:, 0:W], in_offset=None, bounds_check=last_row,
                                                 compute_op=ALU.add).then_inc(g_sct, 16)
                    pool.wait_ge(g_sct, 16 * k + (16 * NC + 16))
            gathers(0, 0, h1_d, W, gat1, gidx1)
            gathers(1, 1, h1_d, W, gat1, gidx1)
            with pool.Fori(0, NG // 2 - 1) as i:
                for s in range(2):
                    rstds(2 * i + s, var1, rstd1)
                    gathers(2 * i + (2 + s), s, h1_d, W, gat1, gidx1)
            for g in (NG - 2, NG - 1):
                rstds(g, var1, rstd1)

        @block.vector
        def _(dve):
            v = nc.vector
            st = Steps(dve, vchain)
            L = st.link
            G = Steps(dve, g_chain).link
            dve.wait_ge(iotas, 2)
            v.tensor_copy(iota[:], tmp_i[:, 0:P])
            v.tensor_copy(iota_t[:], tmp_i[:, 0:NT])
            v.tensor_copy(part[:], iota_i[:, 0:1])
            L(v.tensor_scalar(valid[:], iota_i[:], float(E), None, ALU.is_lt))
            dve.wait_ge(eload, 16 * 6)
            v.tensor_copy(s_nat[:], s_raw[:])
            v.tensor_scalar(t0_raw[:], d_raw[:, :, 0], 7, None, ALU.arith_shift_right)
            L(v.tensor_copy(d_nat[:], d_raw[:]))
            v.tensor_copy(t0_col[:, 0, :], t0_raw[:]).then_inc(nat, 1)
            dve.wait_ge(wT_ps, 1)
            v.tensor_copy(wnT[:], bank(4)[:, 0:D])
            v.tensor_tensor(wz[:, 0:D], bank(4)[:, D:2 * D], ident[:], ALU.add)
            v.tensor_copy(wx[:, 0:D], bank(4)[:, 3 * D:4 * D])
            v.tensor_scalar(wg[:, 0:D], bank(4)[:, 3 * D:4 * D], -1.0, None, ALU.mult)
            v.tensor_copy(wg[:, D:2 * D], bank(5)[:, 0:D])
            v.tensor_copy(wx[:, D:2 * D], bank(5)[:, D:2 * D])
            v.tensor_copy(wl2T[:], bank(4)[:, 2 * D:3 * D]).then_inc(wT_sb, 1)
            dve.wait_ge(wT_ps, 2)
            v.tensor_copy(wz[:, D:2 * D], bank(6)[:, 0:D])
            v.tensor_copy(wabs[:], bank(6)[:, 2 * D:3 * D])
            v.tensor_copy(wmid[:], bank(6)[:, D:2 * D]).then_inc(wT_sb, 1)
            dve.wait_ge(wT_ps, 3)
            v.tensor_copy(wsum[:], bank(7)[:, 0:D])
            v.tensor_scalar(vec[:, 0:D], bank(4)[:, 0:D], -1.0, None, ALU.mult)
            v.tensor_copy(vec[:, D:512], bank(4)[:, D:512])
            v.tensor_copy(vec[:, 512:5 * D + 3], bank(5)[:, 0:5 * D + 3 - 512])
            v.tensor_copy(brow[0:1, :, :], bank(7)[0:1, D:3 * D].rearrange("p (a n) -> p a n", a=2)).then_inc(wT_sb, 1)
            dve.wait_ge(edgeT, 1)
            v.memset(s_i[:], N - 1)
            L(v.memset(d_i[:], N - 1))
            v.tensor_copy(s_i[:, 0:NC], bank(0, 2)[:, 0:NC])
            L(v.tensor_copy(d_i[:, 0:NC], bank(2, 2)[:, 0:NC]))
            L(v.tensor_scalar(tmp_i[:], d_i[:], 7, None, ALU.arith_shift_right))
            v.tensor_copy(td[:], tmp_i[:]).then_inc(t_ready, 1)
            L(v.tensor_scalar(tmp2_i[:], d_i[:], 127, None, ALU.bitwise_and))
            v.tensor_copy(ld[:], tmp2_i[:])
            L(v.scalar_tensor_tensor(tmp2_i[:], s_i[:], 7, tmp2_i[:], ALU.logical_shift_left, ALU.bitwise_or))
            L(v.tensor_scalar(tmp_i[:], tmp2_i[:], 12, None, ALU.arith_shift_right))
            L(v.tensor_scalar(tmp2_i[:], tmp2_i[:], 4095, None, ALU.bitwise_and))
            v.tensor_scalar(hi[:], tmp_i[:], 1.0, None, ALU.add)
            v.tensor_scalar(lo[:], tmp2_i[:], -float(HALF), None, ALU.add)
            L(v.tensor_tensor(ta[:], s_i[:], d_i[:], ALU.is_equal))
            L(v.tensor_tensor(selfe[:], ta[:], valid[:], ALU.mult))
            v.tensor_tensor(other[:], valid[:], selfe[:], ALU.subtract)
            dve.wait_ge(t0_ps, 1)
            L(v.tensor_copy(t0[:], bank(0, 2)[:, 0:NCP]))
            L(v.tensor_tensor(ta[:], td[:], t0[:], ALU.subtract))
            v.scalar_tensor_tensor(in0[:], ta[:], 0.0, valid[:], ALU.is_equal, ALU.mult)
            L(v.scalar_tensor_tensor(in1[:], ta[:], 1.0, valid[:], ALU.is_equal, ALU.mult))
            v.tensor_tensor(tb[:], other[:], in0[:], ALU.mult).then_inc(masks, 1)
            dve.wait_ge(sums_ps, 1)
            v.tensor_copy(cols[:], bank(2, 2)[:, 0:NCP])
            v.tensor_copy(o_first[:], bank(4, 2)[:, 0:NCP])
            L(v.tensor_copy(n_first[:], bank(6, 2)[:, 0:NCP]))
            v.memset(ta[:], 1.0).then_inc(pre_rd, 1)
            dve.wait_ge(pre_rd, 1)
            L(v.tensor_tensor_scan(tb[:], ta[:], cols[:], 0.0, ALU.mult, ALU.add))
            L(v.tensor_tensor(pre[:], tb[:], cols[:], ALU.subtract))
            L(v.tensor_tensor(nxt[:], pre[:], o_first[:], ALU.add))
            L(v.memset(ta[:, 0:1], 0.0))
            L(v.tensor_tensor(ta[:, 1:NCP], t0[:, 1:NCP], t0[:, 0:NCP - 1], ALU.subtract))
            v.memset(start[:, 0:1], 0.0)
            L(v.scalar_tensor_tensor(start[:, 1:NCP], ta[:, 1:NCP], 1.0, nxt[:, 0:NCP - 1], ALU.is_equal, ALU.mult))
            L(v.scalar_tensor_tensor(tb[:], ta[:], 1.5, pre[:], ALU.is_gt, ALU.mult))
            L(v.tensor_tensor(start[:], start[:], tb[:], ALU.add))
            L(v.memset(tb[:], 0.0))
            L(v.tensor_tensor_scan(rank[:], tb[:], start[:], 0.0, ALU.add, ALU.max))
            L(v.tensor_copy(start[:], rank[:]))
            L(v.memset(bad[:], 0.0))
            L(v.tensor_scalar(tb[:, 0:NCP - 1], n_first[:, 0:NCP - 1], float(P), None, ALU.is_lt))
            L(v.tensor_tensor(bad[:, 1:NC], ta[:, 1:NC], tb[:, 0:NC - 1], ALU.is_lt))
            L(v.tensor_scalar(tb[:], n_first[:], part[:, 0:1], None, ALU.is_le))
            L(v.tensor_tensor(tb[:], tb[:], valid[:], ALU.mult))
            L(v.tensor_tensor(tb[:], tb[:], in1[:], ALU.not_equal))
            L(v.tensor_tensor(bad[:], bad[:], tb[:], ALU.add))
            L(v.tensor_tensor(tb[:], in0[:], in1[:], ALU.add))
            L(v.tensor_tensor(tb[:], tb[:], valid[:], ALU.not_equal))
            L(v.tensor_tensor(bad[:], bad[:], tb[:], ALU.add))
            dve.wait_ge(lower_ps, 1)
            L(v.tensor_tensor(rank[:], bank(0, 2)[:, 0:NCP], pre[:], ALU.add))
            L(v.tensor_tensor(rank[:], rank[:], start[:], ALU.subtract))
            L(v.tensor_tensor(tb[:], nxt[:], start[:], ALU.subtract))
            L(v.tensor_tensor(tb[:], tb[:], in1[:], ALU.mult))
            L(v.tensor_tensor(rank[:], rank[:], tb[:], ALU.subtract))
            L(v.scalar_tensor_tensor(tb[:], rank[:], float(P) - 0.5, other[:], ALU.is_gt, ALU.mult))
            L(v.tensor_tensor(bad[:], bad[:], tb[:], ALU.add))
            L(v.tensor_reduce(badsum[:, 0:1], bad[:], AX.X, ALU.add))
            L(v.tensor_tensor(ta[:], other[:], in0[:], ALU.mult))
            L(v.tensor_tensor(tb[:], other[:], in1[:], ALU.mult))
            v.tensor_tensor(place_v[:, :, 0], hi[:], ta[:], ALU.mult)
            v.tensor_tensor(place_v[:, :, 1], lo[:], ta[:], ALU.mult)
            v.tensor_tensor(place_v[:, :, 2], hi[:], tb[:], ALU.mult)
            v.tensor_tensor(place_v[:, :, 3], lo[:], tb[:], ALU.mult)
            v.tensor_tensor(count_v[:, :, 0], selfe[:], in0[:], ALU.mult)
            v.tensor_copy(count_v[:, :, 1], ta[:])
            v.tensor_tensor(count_v[:, :, 2], selfe[:], in1[:], ALU.mult)
            L(v.tensor_copy(count_v[:, :, 3], tb[:]))
            L(v.tensor_scalar(t0_col[:, 1, :], t0_col[:, 0, :], 1.0, None, ALU.add))

            def place_step(i, s):
                def wide(t):
                    return t[:, bass.ds(i * CB, CB)].unsqueeze(2).broadcast_to([P, CB, P])
                io = iota[:].unsqueeze(1).broadcast_to([P, CB, P])
                v.tensor_tensor(place_oh[:, s], io, wide(rank), ALU.is_equal)
                v.tensor_tensor(local_oh[:, s], io, wide(ld), ALU.is_equal).then_inc(place, 1)

            at = 0
            for b in range(NB):
                steps = min(P, NCP - b * P) // CB
                n2 = steps // 2
                if b == 0:
                    place_step(0, 0)
                    place_step(1, 1)
                with dve.Fori(1 if b == 0 else 0, n2) as i:
                    for s in range(2):
                        dve.wait_ge(placed, 2 * i + (at + s - 1))
                        place_step(2 * i + (at + s), s)
                at += 2 * n2
                if steps % 2:
                    dve.wait_ge(placed, at - 1)
                    place_step(at, at % 2)
                    at += 1
                if b:
                    dve.wait_ge(folded, b)
                v.tensor_scalar(fold[:, 0, :], iota_t[:], t0_col[:, 0, b:b + 1], None, ALU.is_equal)
                v.tensor_scalar(fold[:, 1, :], iota_t[:], t0_col[:, 1, b:b + 1], None, ALU.is_equal).then_inc(fold_rdy, 1)
                dve.wait_ge(fieldT, b + 1)
                v.tensor_copy(fieldsT[:], bank(2).bitcast(f16).rearrange("p (a n) -> p a n", a=8)).then_inc(fieldT_sb, 1)
            dve.wait_ge(folded, NB)
            v.tensor_copy(slot_hi[:], bank(4)[:, 0:NT])
            v.tensor_copy(slot_lo[:], bank(5)[:, 0:NT])
            v.tensor_copy(n_self[:], bank(6)[:, 0:NT])
            L(v.tensor_copy(n_in[:], bank(7)[:, 0:NT]))

            def table(loc, idx, far_f):
                L(v.tensor_scalar(occ[:], slot_hi[:], 0.5, None, ALU.is_gt))
                L(v.tensor_scalar(slot_f[:], slot_lo[:], float(HALF - 2 * HALF), None, ALU.add))
                L(v.scalar_tensor_tensor(slot_f[:], slot_hi[:], float(2 * HALF), slot_f[:], ALU.mult, ALU.add))
                L(v.tensor_scalar(slot_f[:], slot_f[:], 0.0, None, ALU.max))
                L(v.tensor_copy(slot_i[:], slot_f[:]))
                v.tensor_scalar(slot_j[:], slot_i[:], 127, None, ALU.bitwise_and)
                L(v.tensor_scalar(slot_k[:], slot_i[:], 7, None, ALU.arith_shift_right))
                v.tensor_copy(far_f[:], slot_k[:])
                L(v.tensor_scalar(loc[:], slot_j[:], 1.0, None, ALU.add))
                L(v.tensor_tensor(loc[:], loc[:], occ[:], ALU.mult))
                L(v.tensor_scalar(loc[:], loc[:], -1.0, None, ALU.add))
                L(v.scalar_tensor_tensor(slot_f[:], far_f[:], float(OOB), occ[:], ALU.subtract, ALU.mult))
                L(v.tensor_scalar(slot_f[:], slot_f[:], float(OOB), None, ALU.add))
                v.tensor_copy(idx[:], slot_f[:])

            table(loc1, idx1, slot_lo)
            L(v.tensor_scalar(slot_j[:], slot_k[:], 7, None, ALU.arith_shift_right))
            L(v.tensor_copy(slot_f[:], slot_j[:]))
            L(v.tensor_scalar(slot_f[:], slot_f[:], -999.0, None, ALU.add))
            L(v.tensor_tensor(slot_f[:], slot_f[:], occ[:], ALU.mult))
            v.tensor_scalar(sort_f[:, :, 0], slot_f[:], 999.0, None, ALU.add)
            L(v.tensor_scalar(slot_j[:], slot_k[:], 127, None, ALU.bitwise_and))
            v.tensor_copy(sort_f[:, :, 1], slot_j[:])
            L(v.scalar_tensor_tensor(slot_f[:], iota_t[:], float(P), loc1[:], ALU.mult, ALU.add))
            L(v.tensor_tensor(slot_f[:], slot_f[:], occ[:], ALU.mult))
            L(v.tensor_copy(slot_i[:], slot_f[:]))
            L(v.scalar_tensor_tensor(slot_i[:], slot_i[:], 7, slot_j[:], ALU.logical_shift_left, ALU.bitwise_or))
            L(v.tensor_scalar(slot_k[:], slot_i[:], 12, None, ALU.arith_shift_right))
            L(v.tensor_scalar(slot_i[:], slot_i[:], 4095, None, ALU.bitwise_and))
            v.tensor_scalar(sort_f[:, :, 2], slot_k[:], 1.0, None, ALU.add)
            v.tensor_scalar(sort_f[:, :, 3], slot_i[:], -float(HALF), None, ALU.add).then_inc(tab1, 1)
            dve.wait_ge(tab1, 1)

            def tile_onehot(i, s, c):
                if not (isinstance(i, int) and i == 0):
                    dve.wait_ge(s_done, CB * i + (c + 1 - CB))
                if c == 0:
                    dve.wait_ge(s_staged, i + 1)
                v.tensor_scalar(tile_oh[:, c, :], iota_t[:], sort_s[:, s, c, 0:1], None, ALU.is_equal).then_inc(s_oh, 1)

            def sort_step(i, s, last=False):
                for c in range(CB):
                    dve.wait_ge(s_rankps, CB * i + (c + 1))
                    v.tensor_tensor_reduce(out=junk[:, c % 2, :], in0=tile_oh[:, c, :], in1=bank(0)[:, 0:NT], scale=1.0, scalar=0.0,
                                           op0=ALU.mult, op1=ALU.add, accum_out=rank_s[:, s, c:c + 1]).then_inc(s_rank, 1)
                    if c < 2:
                        tile_onehot(i, s, c + 2)
                    elif not last:
                        tile_onehot(i + 1, 1 - s, c - 2)
                    dve.wait_ge(s_rank, CB * i + (c + 1))
                    v.tensor_scalar(rank_oh[:, c, :], iota[:], rank_s[:, s, c:c + 1], None, ALU.is_equal).then_inc(s_roh, 1)
                v.tensor_copy(rank0[:, bass.ds(CB * i, CB)], rank_s[:, s, :]).then_inc(s_kept, 1)

            tile_onehot(0, 0, 0)
            tile_onehot(0, 0, 1)
            sort_step(0, 0)
            sort_step(1, 1)
            with dve.Fori(1, NT // CB // 2 - 1) as i:
                for s in range(2):
                    sort_step(2 * i + s, s)
            sort_step(NT // CB - 2, 0)
            sort_step(NT // CB - 1, 1, last=True)
            dve.wait_ge(s_done, NT)
            v.tensor_copy(slot_hi[:], bank(1)[:, 0:NT])
            dve.wait_ge(s_kept, NT // CB)
            L(v.tensor_scalar(junk[:, 0, :], rank0[:], float(P) - 0.5, None, ALU.is_gt))
            L(v.tensor_reduce(badsum[:, 1:2], junk[:, 0, :], AX.X, ALU.add))
            L(v.tensor_tensor(badsum[:, 0:1], badsum[:, 0:1], badsum[:, 1:2], ALU.add))
            v.tensor_copy(slot_lo[:], bank(2)[:, 0:NT])
            v.tensor_copy(n_out[:], bank(3)[:, 0:NT]).then_inc(bad_rdy, 1)
            dve.wait_ge(bad_rdy, 1)
            table(loc0, idx0, slot_lo)
            dve.wait_ge(bad_ps, 1)
            L(v.tensor_scalar(okv[:], bank(0)[:, 0:1], 0.5, None, ALU.is_lt))
            L(v.tensor_scalar(badsum[:, 0:1], okv[:], -1.0, 1.0, ALU.mult, ALU.add))
            v.tensor_copy(flag[:], badsum[:, 0:1]).then_inc(flagged, 1)
            for loc, idx in ((loc0, idx0), (loc1, idx1)):
                L(v.tensor_scalar(loc[:], loc[:], 1.0, okv[:, 0:1], ALU.add, ALU.mult))
                L(v.tensor_scalar(loc[:], loc[:], -1.0, None, ALU.add))
                L(v.tensor_copy(slot_f[:], idx[:]))
                L(v.tensor_scalar(slot_f[:], slot_f[:], -float(OOB), okv[:, 0:1], ALU.add, ALU.mult))
                L(v.tensor_scalar(slot_f[:], slot_f[:], float(OOB), None, ALU.add))
                L(v.tensor_copy(idx[:], slot_f[:]))
            v.tensor_scalar(n_self[:], n_self[:], okv[:, 0:1], None, ALU.mult).then_inc(n_self_rdy, 1)
            dve.wait_ge(n_self_rdy, 1)
            dve.wait_ge(flagged, 1)
            general = dve.value_load(flag[0:1, 0:1], min_val=0, max_val=1)
            with dve.If(general > 0):
                G(v.tensor_scalar(tmp_i[:], s_i[:], 7, None, ALU.arith_shift_right))
                G(v.tensor_copy(ta[:], tmp_i[:]))
                G(v.tensor_scalar(tmp_i[:], s_i[:], 127, None, ALU.bitwise_and))
                G(v.tensor_copy(tb[:], tmp_i[:]))
                G(v.tensor_scalar(in0[:], valid[:], -999.0, 999.0, ALU.mult, ALU.add))
                G(v.tensor_tensor(ta[:], ta[:], in0[:], ALU.add))
                G(v.tensor_tensor(in1[:], td[:], in0[:], ALU.add))

                def count_onehots(k):
                    v.tensor_scalar(g_loh[:, 0, :], iota[:], tb[:, bass.ds(k, 1)], None, ALU.is_equal)
                    v.tensor_scalar(g_loh[:, 1, :], iota[:], ld[:, bass.ds(k, 1)], None, ALU.is_equal)
                    v.tensor_scalar(g_oh[:, 0, :], iota_t[:], ta[:, bass.ds(k, 1)], None, ALU.is_equal)
                    v.tensor_scalar(g_oh[:, 1, :], iota_t[:], in1[:, bass.ds(k, 1)], None, ALU.is_equal).then_inc(g_ohr, 1)

                count_onehots(0)
                with dve.Fori(1, NC) as k:
                    dve.wait_ge(g_cnt, k)
                    count_onehots(k)
                dve.wait_ge(g_cnt, NC)
                v.tensor_copy(n_out[:], bank(1)[:, 0:NT]).then_inc(g_v, 1)
                v.tensor_copy(n_in[:], bank(2)[:, 0:NT]).then_inc(g_v, 1)
                dve.wait_ge(g_v, 2)
            L(v.tensor_tensor(slot_f[:], n_out[:], n_self[:], ALU.add))
            v.tensor_scalar(some[:], slot_f[:], 1.0, None, ALU.min)
            L(v.tensor_scalar(slot_f[:], slot_f[:], 1.0, None, ALU.max))
            L(v.reciprocal(rc[:], slot_f[:]))
            v.memset(slot_hi[:], -0.5)
            L(v.tensor_scalar(self_w[:], n_self[:], 1.0, None, ALU.add))
            v.tensor_tensor(slot_f[:], n_in[:], self_w[:], ALU.add).then_inc(stat_rdy, 1)
            dve.wait_ge(dinv_rdy, 1)
            L(v.tensor_tensor(self_w[:], self_w[:], dinv[:], ALU.mult))
            dve.wait_ge(statT_ps, 1)
            rest = NT % P
            both = bank(4, 2)[:, 0:1024].rearrange("p (a b n) -> p a b n", a=2, b=4)
            v.tensor_copy(statT[:, :, 0:NT // P, :], both[:, :, 0:NT // P, :])
            v.tensor_copy(statT[0:rest, :, NT // P, :], both[0:rest, :, NT // P, :]).then_inc(statT_sb, 1)

            with dve.If(general > 0):
                with dve.Fori(0, NC) as k:
                    ev, dv, kv = e_ok[:, 0:1], None, None
                    col = bass.ds(k, 1)

                    def own(j):
                        dve.wait_ge(g_v, 2 + 12 * k + j)
                    v.tensor_scalar(e_tgt[:], s_i[:, col], -float(OOB), valid[:, col], ALU.add, ALU.mult).then_inc(g_v, 1)
                    v.tensor_scalar(e_key[:], d_i[:, col], -float(OOB), valid[:, col], ALU.add, ALU.mult).then_inc(g_v, 1)
                    own(2)
                    v.tensor_scalar(e_idx[:, 0:1], e_tgt[:], float(OOB), None, ALU.add)
                    v.tensor_scalar(e_idx[:, 1:2], e_key[:], float(OOB), None, ALU.add).then_inc(g_idx, 1)
                    v.tensor_scalar(e_keyb[:], ones[:], e_tgt[:, 0:1], None, ALU.mult).then_inc(g_dif, 1)
                    dve.wait_ge(g_gat, 32 * k + 32)
                    v.tensor_tensor(e_diff[:], e_rows[:, 0, 0:D], e_rows[:, 1, 0:D], ALU.subtract).then_inc(g_dif, 1)
                    v.tensor_copy(e_pay[:, 0:D], e_rows[:, 1, 0:D])
                    dve.wait_ge(g_pe, 4 * k + 1)
                    v.tensor_scalar(e_same[:], bank(0)[:, 0:P], e_tgt[:, 0:1], None, ALU.is_equal).then_inc(g_v, 1)
                    dve.wait_ge(g_pe, 4 * k + 2)
                    v.tensor_copy(e_diffT[:], bank(1)[:, 0:D]).then_inc(g_dif, 1)
                    own(3)
                    v.tensor_tensor(e_junk[:], e_same[:], after[:], ALU.mult).then_inc(g_v, 1)
                    own(4)
                    v.tensor_reduce(e_prev[:], e_junk[:], AX.X, ALU.add).then_inc(g_v, 1)
                    own(5)
                    v.tensor_scalar(e_prev[:], e_prev[:], 0.5, None, ALU.is_lt).then_inc(g_v, 1)
                    own(6)
                    v.tensor_tensor(e_lead[:], e_prev[:], valid[:, col], ALU.mult).then_inc(g_v, 1)
                    v.tensor_scalar(e_key[:], part[:], float(NPAD - OOB), None, ALU.add).then_inc(g_v, 1)
                    own(8)
                    v.tensor_tensor(e_tgt[:], e_tgt[:], e_key[:], ALU.subtract).then_inc(g_v, 1)
                    own(9)
                    v.scalar_tensor_tensor(e_tgt[:], e_tgt[:], e_lead[:, 0:1], e_key[:], ALU.mult, ALU.add).then_inc(g_v, 1)
                    own(10)
                    v.tensor_scalar(e_tgti[:], e_tgt[:], float(OOB), None, ALU.add)
                    dve.wait_ge(g_pe, 4 * k + 3)
                    v.tensor_scalar(e_junk[:], bank(2)[:, 0:D], -1.0, None, ALU.mult).then_inc(g_v, 1)
                    own(11)
                    v.tensor_tensor(e_pay[:, D:2 * D], bank(2)[:, 0:D], e_junk[:], ALU.max).then_inc(g_dif, 1)
                    dve.wait_ge(g_pe, 4 * k + 4)
                    v.tensor_copy(e_sum[:], bank(3)[:, 0:2 * D]).then_inc(g_v, 1)
                    own(12)
                    v.tensor_copy(e_prev[:], e_prev[:]).then_inc(g_idx, 1)
                    dve.wait_ge(g_sct, 16 * k + 16)

            def l0_prepare(g, s, first):
                if not first:
                    dve.wait_ge(s1_ps, g - 1)
                    dve.wait_ge(s2_ps, g - 1)
                v.tensor_copy(gidx[:, s, :], idx0[:, bass.ds(g * TG, TG)]).then_inc(gidx_rdy, 1)
                v.tensor_tensor(oh[:, s], iota[:].unsqueeze(1).broadcast_to([P, TG, P]),
                                loc0[:, bass.ds(g * TG, TG)].unsqueeze(2).broadcast_to([P, TG, P]), ALU.is_equal).then_inc(oh_rdy, 1)

            def norm(g, dst, width, own, base, var, done, ready):
                for t in range(TG):
                    v.bn_stats(stats[:, t, :], res[:, t, :]).then_inc(own, 1)
                dve.wait_ge(own, base + TG)
                v.memset(spare[0:1, 3:4], 0.0)
                for t in range(TG):
                    v.bn_aggr(mv[:, t, :], stats[:, t, :]).then_inc(own, 1)
                dve.wait_ge(own, base + 2 * TG)
                v.tensor_scalar(vare[:], mv[:, :, 1], EPS, None, ALU.add).then_inc(var, 1)

            def l0_sums(g, s):
                dve.wait_ge(s1_ps, g + 1)
                if not (isinstance(g, int) and g == 0):
                    dve.wait_ge(z_ps, g)
                v.tensor_copy(s1T[:], bank(4).rearrange("p (t n) -> p t n", t=TG)).then_inc(s1_sb, 1)
                dve.wait_ge(s2_ps, g + 1)
                v.tensor_copy(s2T[:], bank(5).rearrange("p (t n) -> p t n", t=TG)).then_inc(s2_sb, 1)

            n0 = st.n
            OWN0 = 1 + 2 * TG

            def l0_finish(g, s, first):
                base = n0 + OWN0 * g
                dve.wait_ge(p2_sb, g + 1)
                v.tensor_tensor(res[:], bank(6, 2).rearrange("p (t c n) -> p t c n", t=TG, c=2)[:, :, 0, :],
                                p2[:], ALU.add).then_inc(z_rd, 1)
                dve.wait_ge(z_rd, g + 1)
                norm(g, None, None, vchain, base, var0, None, None)
                if not first:
                    dve.wait_ge(h1_st[s], self_landed(g, s))
                v.tensor_copy(h1g[:, s, :, D], dinv[:, bass.ds(g * TG, TG)])
                dve.wait_ge(rstd0, g + 1)
                for t in range(TG):
                    last = v.tensor_scalar(h1g[:, s, t, 0:D], res[:, t, :], mv[:, t, 0:1], rstd[:, t:t + 1],
                                           ALU.subtract, ALU.mult)
                last.then_inc(h1_rdy, 1)
                v.tensor_copy(mv[:, :, 1], vare[:]).then_inc(vchain, 1)

            def self_landed(g, s):
                if isinstance(g, int):
                    return 16 * ((g - s) // 2)
                return g_half * 16

            g_half = None
            l0_prepare(0, 0, True)
            l0_prepare(1, 1, True)
            l0_sums(0, 0)
            l0_finish(0, 0, True)
            l0_prepare(2, 0, False)
            l0_sums(1, 1)
            l0_finish(1, 1, True)
            l0_prepare(3, 1, False)
            with dve.Fori(1, NG // 2 - 1) as i:
                g_half = i
                for s in range(2):
                    l0_sums(2 * i + s, s)
                    l0_finish(2 * i + s, s, False)
                    l0_prepare(2 * i + (2 + s), s, False)
            for g in (NG - 2, NG - 1):
                l0_sums(g, g % 2)
                l0_finish(g, g % 2, False)
            n1 = n0 + OWN0 * NG

            with dve.If(general > 0):
                with dve.Fori(0, NC) as k:
                    col = bass.ds(k, 1)
                    vb = 2 + 12 * NC

                    def own(j):
                        dve.wait_ge(g_v, (vb + j) + 12 * k)
                    v.tensor_scalar(e_key[:], s_i[:, col], -float(OOB), valid[:, col], ALU.add, ALU.mult).then_inc(g_v, 1)
                    v.tensor_scalar(e_tgt[:], d_i[:, col], -float(OOB), valid[:, col], ALU.add, ALU.mult).then_inc(g_v, 1)
                    own(2)
                    v.tensor_scalar(e_idx[:, 0:1], e_key[:], float(OOB), None, ALU.add).then_inc(g_idx, 1)
                    v.tensor_scalar(e_keyb[:], ones[:], e_tgt[:, 0:1], None, ALU.mult).then_inc(g_dif, 1)
                    dve.wait_ge(g_gat, 16 * k + (32 * NC + 16))
                    v.tensor_scalar(e_pay[:, 0:D], e_rows[:, 0, 0:D], e_rows[:, 0, D:W], None, ALU.mult)
                    v.tensor_copy(e_pay[:, D:W], e_rows[:, 0, D:W]).then_inc(g_v, 1)
                    dve.wait_ge(g_pe, 2 * k + (4 * NC + 1))
                    v.tensor_scalar(e_same[:], bank(0)[:, 0:P], e_tgt[:, 0:1], None, ALU.is_equal).then_inc(g_dif, 1)
                    dve.wait_ge(g_dif, 4 * NC + 2 * k + 2)
                    v.tensor_tensor(e_junk[:], e_same[:], after[:], ALU.mult).then_inc(g_v, 1)
                    own(4)
                    v.tensor_reduce(e_prev[:], e_junk[:], AX.X, ALU.add).then_inc(g_v, 1)
                    own(5)
                    v.tensor_scalar(e_prev[:], e_prev[:], 0.5, None, ALU.is_lt).then_inc(g_v, 1)
                    own(6)
                    v.tensor_tensor(e_lead[:], e_prev[:], valid[:, col], ALU.mult).then_inc(g_v, 1)
                    v.tensor_scalar(e_key[:], part[:], float(NPAD - OOB), None, ALU.add).then_inc(g_v, 1)
                    own(8)
                    v.tensor_tensor(e_tgt[:], e_tgt[:], e_key[:], ALU.subtract).then_inc(g_v, 1)
                    own(9)
                    v.scalar_tensor_tensor(e_tgt[:], e_tgt[:], e_lead[:, 0:1], e_key[:], ALU.mult, ALU.add).then_inc(g_v, 1)
                    own(10)
                    v.tensor_scalar(e_tgti[:], e_tgt[:], float(OOB), None, ALU.add).then_inc(g_v, 1)
                    dve.wait_ge(g_pe, 2 * k + (4 * NC + 2))
                    v.tensor_copy(e_sum[:, 0:W], bank(3)[:, 0:W]).then_inc(g_v, 1)
                    own(12)
                    v.tensor_copy(e_prev[:], e_prev[:]).then_inc(g_idx, 1)
                    dve.wait_ge(g_sct, 16 * k + (16 * NC + 16))

            def l1_prepare(g, s, first):
                if not first:
                    dve.wait_ge(yT_ps, g - 1)
                v.tensor_copy(gidx[:, s, :], idx1[:, bass.ds(g * TG, TG)]).then_inc(gidx1, 1)
                if not first:
                    dve.wait_ge(g_sb, g - 1)
                    dve.wait_ge(gam_rd, g - 1)
                v.tensor_copy(locs[:, s, :], loc1[:, bass.ds(g * TG, TG)])
                v.tensor_copy(col4[:, s, 0, :], dinv[:, bass.ds(g * TG, TG)])
                v.tensor_copy(col4[:, s, 1, :], self_w[:, bass.ds(g * TG, TG)]).then_inc(cols_rdy, 1)

            def l1_onehots(g, s):
                dve.wait_ge(cols_rdy, g + 1)
                dve.wait_ge(gat1[s], g_gathered(g, s))
                for t in range(TG):
                    last = v.tensor_scalar(oh[:, s, t, :], iota[:], locs[:, s, t:t + 1], gx[:, s, t, D:W],
                                           ALU.is_equal, ALU.mult)
                last.then_inc(oh1, 1)

            def g_gathered(g, s):
                if isinstance(g, int):
                    return 16 * TG * ((g - s) // 2 + 1)
                return (g_half + (g_off + 1)) * (16 * TG)

            g_off = 0
            OWN1 = 2 * TG + 7

            def l1_gate(g, s):
                base = n1 + OWN1 * g
                dve.wait_ge(yT_ps, g + 1)
                v.tensor_tensor(gam[:], bank(3)[:, 0:TG], col4[:, s, 1, :], ALU.add).then_inc(vchain, 1)
                dve.wait_ge(vchain, base + 1)
                v.tensor_tensor(gam[:], gam[:], col4[:, s, 0, :], ALU.mult).then_inc(gam_rd, 1)
                dve.wait_ge(gam_rd, g + 1)
                dve.wait_ge(g_sb, g + 1)
                for t in range(TG):
                    last = v.scalar_tensor_tensor(q[:, t, :], vec[:, 0:2 * D], gam[:, t:t + 1], gs[:, t, :], ALU.mult, ALU.add)
                last.then_inc(vchain, 1)
                dve.wait_ge(x_ps, g + 1)
                if not (isinstance(g, int) and g == 0):
                    dve.wait_ge(ay_rdy, g)
                dve.wait_ge(vchain, base + 2)
                xb = bank(6, 2).rearrange("p (t c n) -> p t c n", t=TG, c=2)
                v.tensor_tensor(y[:, :, 0, :], xb[:, :, 0, :], q[:, :, 0:D], ALU.add)
                v.tensor_copy(y[:, :, 1, :], q[:, :, D:2 * D])
                v.tensor_copy(y[:, :, 2, :], xb[:, :, 1, :]).then_inc(x_rd, 1)
                dve.wait_ge(x_rd, g + 1)
                for k in range(3):
                    for t in range(TG):
                        last = v.scalar_tensor_tensor(dot_junk[:, k, t, :], y[:, t, k, :], 0.0, vec[:, (2 + k) * D:(3 + k) * D],
                                                      ALU.max, ALU.mult, accum_out=dots[:, k, t:t + 1])
                        last.then_inc(vchain, 1) if False else None
                last.then_inc(dots_rdy, 1)

            def l1_finish(g, s, first):
                base = n1 + OWN1 * g + 2
                dve.wait_ge(hl[s], h_loaded(g, s))
                dve.wait_ge(ay_rdy, g + 1)
                v.tensor_tensor(res[:], ay[:, 0], ay[:, 1], ALU.add).then_inc(vchain, 1)
                dve.wait_ge(vchain, base + 1)
                v.tensor_tensor(res[:], res[:], ay[:, 2], ALU.add).then_inc(vchain, 1)
                dve.wait_ge(vchain, base + 2)
                v.tensor_tensor(res[:], res[:], h1g[:, s, :, 0:D], ALU.add).then_inc(ay_rd, 1)
                dve.wait_ge(ay_rd, g + 1)
                norm(g, None, None, vchain, base + 2, var1, None, None)
                if not first:
                    dve.wait_ge(out_st[s], self_landed(g, s))
                dve.wait_ge(rstd1, g + 1)
                for t in range(TG):
                    last = v.tensor_scalar(outg[:, s, t, :], res[:, t, :], mv[:, t, 0:1], rstd[:, t:t + 1],
                                           ALU.subtract, ALU.mult)
                last.then_inc(out_rdy, 1)
                v.tensor_copy(mv[:, :, 1], vare[:]).then_inc(vchain, 1)
                dve.wait_ge(vchain, base + 3 + 2 * TG)
                v.tensor_copy(mv[:, :, 1], vare[:]).then_inc(vchain, 1)
                v.tensor_copy(mv[:, :, 0], vare[:]).then_inc(vchain, 1)

            def h_loaded(g, s):
                if isinstance(g, int):
                    n = (g - s) // 2 + 1
                    return 16 * (n + (LAST_PARTS - 1 if g == NG - 1 else 0))
                return (g_half + 1) * 16

            l1_prepare(0, 0, True)
            l1_prepare(1, 1, True)
            l1_onehots(0, 0)
            for g in (0, 1):
                l1_gate(g, g)
                l1_onehots(g + 1, (g + 1) % 2) if g == 0 else None
                l1_prepare(g + 2, g, False)
                if g == 1:
                    l1_onehots(2, 0)
                l1_finish(g, g, True)
            with dve.Fori(1, NG // 2 - 1) as i:
                g_half = i
                for s in range(2):
                    l1_gate(2 * i + s, s)
                    if s == 0:
                        g_off = 0
                        l1_onehots(2 * i + 1, 1)
                        l1_prepare(2 * i + 2, 0, False)
                    else:
                        l1_prepare(2 * i + 3, 1, False)
                        g_off = 1
                        l1_onehots(2 * i + 2, 0)
                        g_off = 0
                    l1_finish(2 * i + s, s, False)
            for g in (NG - 2, NG - 1):
                l1_gate(g, g % 2)
                if g == NG - 2:
                    l1_onehots(g + 1, 1)
                l1_finish(g, g % 2, False)

        @block.tensor
        def _(pe):
            mm = nc.tensor.matmul

            def wide_mm(b, lhsT, rhs, start=True, stop=True):
                mm(psum[:, 512 * b:512 * b + 512], lhsT, rhs[:, 0:512], start=start, stop=stop)
                return mm(psum[:, 512 * b + 512:512 * b + NCP], lhsT, rhs[:, 512:NCP], start=start, stop=stop)

            pe.wait_ge(consts, 4)
            pe.wait_ge(wload, 16 * 18)
            for k, w in enumerate((wn[:], wl[:, 0:D], wl[:, D:2 * D], w1[:, 0, :])):
                nc.tensor.transpose(bank(4)[:, k * D:(k + 1) * D], w, ident[:])
            nc.tensor.transpose(bank(5)[:, 0:D], w1[:, 1, :], ident[:])
            nc.tensor.transpose(bank(5)[:, D:2 * D], w1[:, 2, :], ident[:]).then_inc(wT_ps, 1)
            pe.wait_ge(wT_sb, 1)
            mm(bank(6)[:, 0:D], wn[:], wl2T[:], start=True, stop=True)
            mm(bank(6)[:, D:2 * D], we[:, 0:D], wl2T[:], start=True, stop=True)
            mm(bank(6)[:, 2 * D:3 * D], we[:, D:2 * D], wl2T[:], start=True, stop=True).then_inc(wT_ps, 1)
            pe.wait_ge(wT_sb, 2)
            mm(bank(7)[:, 0:D], wn[:], wmid[:], start=True, stop=True)
            mm(bank(7)[0:1, D:2 * D], bcol[:, 0:1], wl2T[:], start=True, stop=True)
            mm(bank(7)[0:1, 2 * D:3 * D], bcol[:, 1:2], wl2T[:], start=True, stop=False)
            mm(bank(7)[0:1, 2 * D:3 * D], bcol[:, 0:1], wmid[:], start=False, stop=True)
            mm(bank(4), ones_row[0:1, :], vec_row[0:1, 0:512], start=True, stop=True)
            mm(bank(5)[:, 0:5 * D + 3 - 512], ones_row[0:1, :], vec_row[0:1, 512:5 * D + 3], start=True, stop=True).then_inc(wT_ps, 1)

            pe.wait_ge(nat, 1)
            for b in range(NB):
                n = min(P, NC - b * P)
                nc.tensor.transpose(psum[:, b * P:b * P + n], s_nat[0:n, b, :], ident[0:n, 0:n])
                last = nc.tensor.transpose(psum[:, 1024 + b * P:1024 + b * P + n], d_nat[0:n, b, :], ident[0:n, 0:n])
            last.then_inc(edgeT, 1)
            pe.wait_ge(t_ready, 1)
            wide_mm(0, row0[:], td).then_inc(t0_ps, 1)
            pe.wait_ge(masks, 1)
            pe.wait_ge(wT_sb, 3)
            wide_mm(2, ones[:], other)
            wide_mm(4, ones[:], tb)
            wide_mm(6, ones[:], in0).then_inc(sums_ps, 1)
            wide_mm(0, before[:], other).then_inc(lower_ps, 1)

            def place_step(i, s, b):
                pe.wait_ge(place, i + 1)
                for c in range(CB):
                    k = i * CB + (c - b * P)
                    o = psum[:, 0:1024].rearrange("p (a f k) -> p a f k", a=2, f=4)
                    mm(o[:, 0, :, bass.ds(k, 1)].rearrange("p f o -> p (f o)"), place_oh[:, s, c, :],
                       place_v[:, bass.ds(i * CB + c, 1), :].rearrange("p o f -> p (o f)"), start=True, stop=True)
                    last = mm(o[:, 1, :, bass.ds(k, 1)].rearrange("p f o -> p (f o)"), local_oh[:, s, c, :],
                              count_v[:, bass.ds(i * CB + c, 1), :].rearrange("p o f -> p (o f)"), start=True, stop=True)
                last.then_inc(placed, 1)

            at = 0
            for b in range(NB):
                n = min(P, NCP - b * P)
                steps = n // CB
                n2 = steps // 2
                if b:
                    pe.wait_ge(block_rd, b)
                with pe.Fori(0, n2) as i:
                    for s in range(2):
                        place_step(2 * i + (at + s), s, b)
                at += 2 * n2
                if steps % 2:
                    place_step(at, at % 2, b)
                    at += 1
                pe.wait_ge(block_rd, b + 1)
                if b:
                    pe.wait_ge(fieldT_sb, b)
                fT = bank(2).bitcast(f16).rearrange("p (a n) -> p a n", a=8)
                for f in range(8):
                    last = nc.tensor.transpose(fT[0:n, f, :], fields[:, f, 0:n], ident16[:])
                last.then_inc(fieldT, 1)
                pe.wait_ge(fold_rdy, b + 1)
                pe.wait_ge(fieldT_sb, b + 1)
                for f in range(8):
                    which, i1 = 2 * (f // 4) + f % 2, (f % 4) // 2
                    last = mm(bank(4 + which)[:, 0:NT], fieldsT[0:n, f, :], fold[0:n, i1, :],
                              start=(b == 0 and i1 == 0), stop=(b == NB - 1 and i1 == 1), skip_group_check=True)
                last.then_inc(folded, 1)

            pe.wait_ge(tab1, 1)

            def rank_mm(j, k, first=False):
                pe.wait_ge(s_oh, j + 1)
                mm(bank(0)[:, 0:NT], before16[:], tile_oh[:, k, :], start=first, stop=True, skip_group_check=True).then_inc(s_rankps, 1)

            def rest_mm(j, k):
                pe.wait_ge(s_rank, j + 1)
                mm(bank(0)[:, 0:NT], notbefore16[:], tile_oh[:, k, :], start=False, stop=True, skip_group_check=True)

            def slots_mm(j, k, first=False):
                pe.wait_ge(s_src, j + 1)
                mm(bank(3)[:, 0:NT], src_oh[:, k, :], tile_oh[:, k, :], start=first, stop=True, skip_group_check=True)
                pe.wait_ge(s_val, j + 1)
                mm(bank(1)[:, 0:NT], hi_oh[:, k, :], tile_oh[:, k, :], start=first, stop=True, skip_group_check=True)
                mm(bank(2)[:, 0:NT], lo_oh[:, k, :], tile_oh[:, k, :], start=first, stop=True, skip_group_check=True).then_inc(s_done, 1)

            rank_mm(0, 0, True)
            rest_mm(0, 0)
            rank_mm(1, 1)
            rest_mm(1, 1)
            rank_mm(2, 2)
            slots_mm(0, 0, True)
            rest_mm(2, 2)
            rank_mm(3, 3)
            slots_mm(1, 1)
            rest_mm(3, 3)
            rank_mm(4, 0)
            slots_mm(2, 2)
            with pe.Fori(1, NT // CB - 1) as i:
                for c in range(CB):
                    rest_mm(CB * i + c, c)
                    rank_mm(CB * i + (c + 1), (c + 1) % CB)
                    slots_mm(CB * i + (c - 1), (c - 1) % CB)
            for j in range(NT - CB, NT):
                rest_mm(j, j % CB)
                if j + 1 < NT:
                    rank_mm(j + 1, (j + 1) % CB)
                slots_mm(j - 1, (j - 1) % CB)
            slots_mm(NT - 1, (NT - 1) % CB)
            pe.wait_ge(bad_rdy, 1)
            mm(bank(0)[:, 0:1], ones[:], badsum[:, 0:1], start=True, stop=True).then_inc(bad_ps, 1)
            pe.wait_ge(flagged, 1)
            general = pe.value_load(flag[0:1, 0:1], min_val=0, max_val=1)
            with pe.If(general > 0):
                def count_mm(j, first):
                    pe.wait_ge(g_ohr, j + 1)
                    mm(bank(1)[:, 0:NT], g_loh[:, 0, :], g_oh[:, 0, :], start=first, stop=True, skip_group_check=True)
                    mm(bank(2)[:, 0:NT], g_loh[:, 1, :], g_oh[:, 1, :], start=first, stop=True, skip_group_check=True).then_inc(g_cnt, 1)
                count_mm(0, True)
                with pe.Fori(1, NC) as k:
                    count_mm(k, False)
            pe.wait_ge(stat_rdy, 1)
            NB4 = -(-NT // P)
            for k, t in enumerate((rc, some)):
                for b in range(NB4):
                    n = min(P, NT - b * P)
                    last = nc.tensor.transpose(psum[0:n, 2048 + 512 * k + P * b:2048 + 512 * k + P * (b + 1)], t[:, b * P:b * P + n], ident[:])
            last.then_inc(statT_ps, 1)

            with pe.If(general > 0):
                with pe.Fori(0, NC) as k:
                    pe.wait_ge(g_dif, 4 * k + 1)
                    nc.tensor.transpose(bank(0)[:, 0:P], e_keyb[:], ident[:]).then_inc(g_pe, 1)
                    pe.wait_ge(g_dif, 4 * k + 2)
                    nc.tensor.transpose(bank(1)[:, 0:P], e_diff[:], ident[:]).then_inc(g_pe, 1)
                    pe.wait_ge(g_dif, 4 * k + 3)
                    mm(bank(2)[:, 0:D], e_diffT[:], wnT[:], start=True, stop=True).then_inc(g_pe, 1)
                    pe.wait_ge(g_dif, 4 * k + 4)
                    mm(bank(3)[:, 0:2 * D], e_same[:], e_pay[:], start=True, stop=True).then_inc(g_pe, 1)
                pe.wait_ge(g_idx, 2 * NC)

            pe.wait_ge(bload, 16 * 3)
            pe.wait_ge(statT_sb, 1)
            LAND = 16

            def landed(g, s, per, half):
                if isinstance(g, int):
                    return per * ((g - s) // 2 + 1) + (per * (LAST_PARTS - 1) if g == NG - 1 and per == 16 else 0)
                return half * per

            def transposes(g, s, half):
                pe.wait_ge(xl[s], landed(g, s, 16, half))
                pe.wait_ge(oh_rdy, g + 1)
                if not (isinstance(g, int) and g == 0):
                    pe.wait_ge(xT_sb, g)
                    pe.wait_ge(ohT_sb, g)
                for t in range(TG):
                    nc.tensor.transpose(bank(0)[:, t * P:(t + 1) * P], xg[:, s, t, :], ident[:])
                for t in range(TG):
                    last = nc.tensor.transpose(bank(1)[:, t * P:(t + 1) * P], oh[:, s, t, :], ident[:])
                last.then_inc(trans, 1)

            def differences(g, s, half):
                pe.wait_ge(ohT_sb, g + 1)
                pe.wait_ge(gat[s], landed(g, s, 16 * TG, half))
                if not (isinstance(g, int) and g == 0):
                    pe.wait_ge(dT_sb, g)
                for t in range(TG):
                    o = bank(2)[:, t * P:(t + 1) * P]
                    mm(o, xg[:, s, t, :], ohT[:, t, :], start=True, stop=False)
                    last = mm(o, gx[:, s, t, 0:D], neg_ident[:], start=False, stop=True)
                last.then_inc(dT_ps, 1)

            def edge_products(g, s):
                pe.wait_ge(dT_sb, g + 1)
                if not (isinstance(g, int) and g == 0):
                    pe.wait_ge(hd_sb, g)
                for t in range(TG):
                    last = mm(bank(3)[:, t * P:(t + 1) * P], dT[:, t, :], wnT[:], start=True, stop=True)
                last.then_inc(hd_ps, 1)

            def sums(g, s, add):
                pe.wait_ge(diag0, g + 1)
                if not (isinstance(g, int) and g == 0):
                    pe.wait_ge(s1_sb, g)
                for t in range(TG):
                    o = bank(4)[:, t * P:(t + 1) * P]
                    mm(o, gx[:, s, t, 0:D], oh[:, s, t, :], start=(t == 0), stop=True, skip_group_check=True)
                    mm(o, xg[:, s, t, :], diag[:, s, t, :], start=False, stop=True, skip_group_check=True)
                with pe.If(general > 0):
                    pe.wait_ge(accl, 16 * g + 16)
                    for t in range(TG):
                        mm(bank(4)[:, t * P:(t + 1) * P], accg[:, t, 0:D], ident[:], start=False, stop=True, skip_group_check=True)
                pe.nop().then_inc(s1_ps, 1) if False else mm(bank(4)[:, 0:1], zcol(), zrow(), start=False, stop=True,
                                                             skip_group_check=True).then_inc(s1_ps, 1)

            def zcol():
                return zeros[0:1, 0, 0:P]

            def zrow():
                return zeros[0:1, 0, 0:1]

            def abs_sums(g, s):
                pe.wait_ge(hd_sb, g + 1)
                if not (isinstance(g, int) and g == 0):
                    pe.wait_ge(s2_sb, g)
                for t in range(TG):
                    mm(bank(5)[:, t * P:(t + 1) * P], hd[:, t, :], oh[:, s, t, :], start=(t == 0), stop=True,
                       skip_group_check=True)
                with pe.If(general > 0):
                    pe.wait_ge(accl, 16 * g + 16)
                    for t in range(TG):
                        last = mm(bank(5)[:, t * P:(t + 1) * P], accg[:, t, D:2 * D], ident[:], start=False, stop=True,
                                  skip_group_check=True)
                    last.then_inc(acc_rd, 1)
                mm(bank(5)[:, 0:1], zcol(), zrow(), start=False, stop=True, skip_group_check=True).then_inc(s2_ps, 1)

            def z_x(g, s, half):
                pe.wait_ge(xT_sb, g + 1)
                pe.wait_ge(s1_sb, g + 1)
                pe.wait_ge(rl[s], landed(g, s, 16, half) if not (isinstance(g, int) and g == NG - 1) else 16 * (NG // 2))
                if not (isinstance(g, int) and g == 0):
                    pe.wait_ge(z_rd, g)
                for t in range(TG):
                    o = psum[:, 3072 + 256 * t:3072 + 256 * (t + 1)]
                    mm(o, xT[:, t, :], wz[:], start=(t % 2 == 0), stop=True, skip_group_check=True)
                    mm(o[:, 0:D], row3[0:3, s, t * P:(t + 1) * P], bias3[0:3, :], start=False, stop=True, skip_group_check=True)
                    mm(o[:, D:2 * D], s1T[:, t, :], wsum[:], start=False, stop=True, skip_group_check=True)

            def z_abs(g, s):
                pe.wait_ge(s2_sb, g + 1)
                for t in range(TG):
                    o = psum[:, 3072 + 256 * t + D:3072 + 256 * (t + 1)]
                    last = mm(o, s2T[:, t, :], wabs[:], start=False, stop=True, skip_group_check=True)
                last.then_inc(z_ps, 1)

            def l0_step(g, s, half, nxt_half, more=True):
                abs_sums(g, s)
                z_x(g, s, half)
                if more:
                    transposes(g + 1, 1 - s, nxt_half)
                    differences(g + 1, 1 - s, nxt_half)
                z_abs(g, s)
                if more:
                    edge_products(g + 1, 1 - s)
                    sums(g + 1, 1 - s, None)

            transposes(0, 0, None)
            differences(0, 0, None)
            edge_products(0, 0)
            sums(0, 0, None)
            l0_step(0, 0, None, None)
            l0_step(1, 1, None, None)
            with pe.Fori(1, NG // 2 - 1) as i:
                l0_step(2 * i, 0, i + 1, i + 1)
                l0_step(2 * i + 1, 1, i + 1, i + 2)
            l0_step(NG - 2, 0, None, None)
            l0_step(NG - 1, 1, None, None, more=False)

            with pe.If(general > 0):
                pe.wait_ge(z_rd, NG)
                with pe.Fori(0, NC) as k:
                    pe.wait_ge(g_dif, 2 * k + (4 * NC + 1))
                    nc.tensor.transpose(bank(0)[:, 0:P], e_keyb[:], ident[:]).then_inc(g_pe, 1)
                    pe.wait_ge(g_dif, 2 * k + (4 * NC + 2))
                    mm(bank(3)[:, 0:W], e_same[:], e_pay[:, 0:W], start=True, stop=True).then_inc(g_pe, 1)
                pe.wait_ge(g_idx, 4 * NC)

            def l1_sums(g, s, half):
                first = isinstance(g, int) and g == 0
                pe.wait_ge(oh1, g + 1)
                pe.wait_ge(diag_rdy, g + 1)
                pe.wait_ge(hl[s], landed(g, s, 16, half))
                if not first:
                    pe.wait_ge(yT_sb, g)
                    pe.wait_ge(gam_rd, g)
                for t in range(TG):
                    o = bank(0)[:, t * P:(t + 1) * P]
                    mm(o, gx[:, s, t, 0:D], oh[:, s, t, :], start=(t == 0), stop=True, skip_group_check=True)
                    mm(o, h1g[:, s, t, 0:D], diag[:, s, t, :], start=False, stop=True, skip_group_check=True)
                    mm(bank(3)[:, t:t + 1], oh[:, s, t, :], ones[:, 0:1], start=(t == 0), stop=True, skip_group_check=True)
                with pe.If(general > 0):
                    pe.wait_ge(accl, 16 * g + (16 * NG + 16))
                    for t in range(TG):
                        mm(bank(0)[:, t * P:(t + 1) * P], accg[:, t, 0:D], ident[:], start=False, stop=True, skip_group_check=True)
                        last = mm(bank(3)[:, t:t + 1], ident[:], accg[:, t, D:W], start=False, stop=True, skip_group_check=True)
                    last.then_inc(acc_rd, 1)
                mm(bank(0)[:, 0:1], zcol(), zrow(), start=False, stop=True, skip_group_check=True).then_inc(yT_ps, 1)

            def l1_transposes(g, s, half):
                first = isinstance(g, int) and g == 0
                if not first:
                    pe.wait_ge(hT_sb, g)
                for t in range(TG):
                    last = nc.tensor.transpose(bank(1)[:, t * P:(t + 1) * P], h1g[:, s, t, 0:D], ident[:])
                last.then_inc(hT_ps, 1)

            def l1_g(g, s):
                pe.wait_ge(yT_sb, g + 1)
                if not (isinstance(g, int) and g == 0):
                    pe.wait_ge(g_sb, g)
                for t in range(TG):
                    last = mm(psum[:, 2048 + 256 * t:2048 + 256 * (t + 1)], yT(t), wg[:], start=(t % 2 == 0), stop=True, skip_group_check=True)
                last.then_inc(g_ps, 1)

            def yT(t):
                return s1T[:, t, :]

            def l1_x(g, s):
                pe.wait_ge(hT_sb, g + 1)
                if not (isinstance(g, int) and g == 0):
                    pe.wait_ge(x_rd, g)
                for t in range(TG):
                    o = psum[:, 3072 + 256 * t:3072 + 256 * (t + 1)]
                    mm(o, xT[:, t, :], wx[:], start=(t % 2 == 0), stop=True, skip_group_check=True)
                    last = mm(o, ones_row[0:1, :], bx[0:1, :], start=False, stop=True, skip_group_check=True)
                last.then_inc(x_ps, 1)

            def l1_step(g, s, half):
                l1_sums(g, s, half)
                l1_transposes(g, s, half)
                l1_g(g, s)
                l1_x(g, s)

            l1_step(0, 0, None)
            l1_step(1, 1, None)
            with pe.Fori(1, NG // 2 - 1) as i:
                l1_step(2 * i, 0, i + 1)
                l1_step(2 * i + 1, 1, i + 1)
            l1_step(NG - 2, 0, None)
            l1_step(NG - 1, 1, None)

        @block.scalar
        def _(act):
            a = nc.scalar
            for b in range(NB):
                dst_steps = 0
                n = min(P, NCP - b * P)
                act.wait_ge(placed, min((b + 1) * P, NCP) // CB)
                if b:
                    act.wait_ge(fieldT, b)
                a.copy(fields[:, :, 0:n], psum[:, 0:1024].rearrange("p (f k) -> p f k", f=8)[:, :, 0:n]).then_inc(block_rd, 1)
            act.wait_ge(tab1, 1)

            def sort_stage(i, s, first=False):
                if not first:
                    act.wait_ge(s_done, CB * i - CB)
                a.copy(sort_s[:, s], sort_f[:, bass.ds(i * CB, CB), :]).then_inc(s_staged, 1)

            def sort_values(i, s):
                act.wait_ge(s_staged, i + 1)
                for c in range(CB):
                    if not (isinstance(i, int) and i == 0):
                        act.wait_ge(s_done, CB * i + (c + 1 - CB))
                    act.wait_ge(s_roh, CB * i + (c + 1))
                    a.activation(hi_oh[:, c, :], rank_oh[:, c, :], ACT.Copy, scale=sort_s[:, s, c, 2:3])
                    a.activation(lo_oh[:, c, :], rank_oh[:, c, :], ACT.Copy, scale=sort_s[:, s, c, 3:4]).then_inc(s_val, 1)

            sort_stage(0, 0, True)
            sort_stage(1, 1, True)
            sort_values(0, 0)
            sort_stage(2, 0)
            sort_values(1, 1)
            sort_stage(3, 1)
            with act.Fori(1, NT // CB // 2 - 1) as i:
                for s in range(2):
                    sort_values(2 * i + s, s)
                    sort_stage(2 * i + (2 + s), s)
            for i in (NT // CB - 2, NT // CB - 1):
                sort_values(i, i % 2)

            def copy4(dst, b, func=ACT.Copy):
                return a.activation(dst, bank(b).rearrange("p (t n) -> p t n", t=TG), func)

            def l0_front(g):
                act.wait_ge(trans, g + 1)
                if not (isinstance(g, int) and g == 0):
                    act.wait_ge(dT_ps, g)
                copy4(ohT[:], 1).then_inc(ohT_sb, 1)
                copy4(xT[:], 0).then_inc(xT_sb, 1)

            def l0_mid(g):
                act.wait_ge(dT_ps, g + 1)
                if not (isinstance(g, int) and g == 0):
                    act.wait_ge(hd_ps, g)
                copy4(dT[:], 2).then_inc(dT_sb, 1)

            def l0_abs(g):
                act.wait_ge(hd_ps, g + 1)
                if not (isinstance(g, int) and g == 0):
                    act.wait_ge(s2_ps, g)
                copy4(hd[:], 3, ACT.Abs).then_inc(hd_sb, 1)

            def l0_p2(g):
                act.wait_ge(z_ps, g + 1)
                if not (isinstance(g, int) and g == 0):
                    act.wait_ge(z_rd, g)
                for t in range(TG):
                    last = a.activation(p2[:, t, :], psum[:, 3072 + 256 * t + D:3072 + 256 * (t + 1)], ACT.Copy,
                                        scale=rc[:, bass.ds(TG * g + t, 1)])
                last.then_inc(p2_sb, 1)

            def l0_diag(g, s, first):
                if not first:
                    act.wait_ge(s1_ps, g - 1)
                for t in range(TG):
                    last = a.activation(diag[:, s, t, :], ident[:], ACT.Copy, scale=n_self[:, bass.ds(TG * g + t, 1)])
                last.then_inc(diag0, 1)

            def l0_step(g, s, more=2):
                if more > 0:
                    l0_front(g + 1)
                    l0_mid(g + 1)
                l0_p2(g)
                if more > 0:
                    l0_abs(g + 1)
                if more > 1:
                    l0_diag(g + 2, s, False)

            act.wait_ge(n_self_rdy, 1)
            l0_diag(0, 0, True)
            l0_front(0)
            l0_mid(0)
            l0_abs(0)
            l0_diag(1, 1, True)
            with act.Fori(0, NG // 2 - 1) as i:
                for s in range(2):
                    l0_step(2 * i + s, s)
            l0_step(NG - 2, 0, 1)
            l0_step(NG - 1, 1, 0)

            def l1_diag(g, s, first):
                act.wait_ge(cols_rdy, g + 1)
                if not first:
                    act.wait_ge(yT_ps, g - 1)
                for t in range(TG):
                    last = a.activation(diag[:, s, t, :], ident[:], ACT.Copy, scale=col4[:, s, 1, t:t + 1])
                last.then_inc(diag_rdy, 1)

            def l1_mid(g, s):
                first = isinstance(g, int) and g == 0
                act.wait_ge(yT_ps, g + 1)
                if not first:
                    act.wait_ge(g_ps, g)
                copy4(s1T[:], 0).then_inc(yT_sb, 1)
                act.wait_ge(hT_ps, g + 1)
                if not first:
                    act.wait_ge(x_ps, g)
                copy4(xT[:], 1).then_inc(hT_sb, 1)
                act.wait_ge(g_ps, g + 1)
                if not first:
                    act.wait_ge(x_rd, g)
                for t in range(TG):
                    last = a.activation(gs[:, t, :], psum[:, 2048 + 256 * t:2048 + 256 * (t + 1)], ACT.Copy,
                                        scale=col4[:, s, 0, t:t + 1])
                last.then_inc(g_sb, 1)

            def l1_gates(g, s):
                first = isinstance(g, int) and g == 0
                act.wait_ge(dots_rdy, g + 1)
                for k in range(3):
                    last = a.activation(gates[:, k, :], dots[:, k, :], ACT.Sigmoid, bias=vec[:, 5 * D + k:5 * D + k + 1])
                last.then_inc(gate_rdy, 1)
                act.wait_ge(gate_rdy, g + 1)
                if not first:
                    act.wait_ge(ay_rd, g)
                for k in range(3):
                    for t in range(TG):
                        last = a.activation(ay[:, k, t, :], y[:, t, k, :], ACT.Relu, scale=gates[:, k, t:t + 1])
                last.then_inc(ay_rdy, 1)

            l1_diag(0, 0, True)
            l1_diag(1, 1, True)
            for g in (0, 1):
                l1_mid(g, g)
                l1_diag(g + 2, g, False)
                l1_gates(g, g)
            with act.Fori(1, NG // 2 - 1) as i:
                for s in range(2):
                    l1_mid(2 * i + s, s)
                    l1_diag(2 * i + (2 + s), s, False)
                    l1_gates(2 * i + s, s)
            for g in (NG - 2, NG - 1):
                l1_mid(g, g % 2)
                l1_gates(g, g % 2)


_INS = ['x', 'src', 'dst', 'L0_gnn_W_neigh', 'L0_gnn_b_neigh', 'L0_gnn_W_edge', 'L0_gnn_b_edge', 'L0_gnn_W_lin',
        'L0_gnn_b_lin', 'L1_gnn_W_hp', 'L1_gnn_b_hp', 'L1_gnn_W_lp', 'L1_gnn_b_lp', 'L1_gnn_W_i', 'L1_gnn_b_i',
        'L1_gnn_wlin_h', 'L1_gnn_blin_h', 'L1_gnn_wlin_l', 'L1_gnn_blin_l', 'L1_gnn_wlin_i', 'L1_gnn_blin_i']


def kernel(**inputs):
    import numpy as np
    import concourse.bacc as bacc
    from concourse import mybir
    from concourse.bass_utils import run_bass_kernel_spmd

    nc = bacc.Bacc("TRN2", target_bir_lowering=False, num_devices=1)
    arrays, args = {}, []
    for name in _INS:
        a = np.ascontiguousarray(inputs[name])
        a = a.reshape(a.shape if a.ndim else (1,))
        arrays[f"in_{name}"] = a
        args.append(nc.dram_tensor(f"in_{name}", a.shape, mybir.dt.from_np(a.dtype), kind="ExternalInput").ap())
    out = nc.dram_tensor("out", inputs["x"].shape, mybir.dt.float32, kind="ExternalOutput").ap()
    build(nc, *args, out)
    r = run_bass_kernel_spmd(nc, [arrays], core_ids=[0])
    return r.results[0]["out"]
```

```python
def build(nc, x_d, src_d, dst_d, wn_d, bn_d, we_d, be_d, wl_d, bl_d,
          whp_d, bhp_d, wlp_d, blp_d, wi_d, bi_d, wvh_d, bvh_d, wvl_d, bvl_d, wvi_d, bvi_d, out_d):
    from contextlib import ExitStack
    import concourse.bass as bass
    from concourse import mybir

    f32, f16, i32 = mybir.dt.float32, mybir.dt.float16, mybir.dt.int32
    ALU, ACT, AX = mybir.AluOpType, mybir.ActivationFunctionType, mybir.AxisListType
    P = 128
    N, D = x_d.shape
    E = src_d.shape[0]
    TG = 4
    NG = -(-N // (P * TG))
    NT = NG * TG
    NPAD = NT * P
    CB = 4
    NC = -(-E // P)
    NCP = -(-NC // CB) * CB
    NB = -(-NC // P)
    W = D + 1
    OOB = 60000
    HALF = 2048
    EPS = 1e-5
    assert NPAD + P > N and OOB > N and N * P < 2 ** 24

    h1_d = nc.dram_tensor("h1_scratch", (N, W), f32).ap()
    rows_d = nc.dram_tensor("rows_scratch", (2, NPAD), f32).ap()
    acc0_d = nc.dram_tensor("acc0_scratch", (NPAD + P, 2 * D), f32).ap()
    acc1_d = nc.dram_tensor("acc1_scratch", (NPAD + P, W), f32).ap()

    ctx = ExitStack()
    with ctx:
        def sb(name, shape, dt=f32):
            return ctx.enter_context(nc.sbuf_tensor(name, shape, dt))

        def sem(name):
            return ctx.enter_context(nc.semaphore(name))

        psum = ctx.enter_context(nc.psum_tensor("psum", [P, 8 * 512], f32))

        def bank(b, n=1):
            return psum[:, 512 * b:512 * (b + n)]

        ident = sb("ident", [P, P])
        ident16 = sb("ident16", [P, P], f16)
        neg_ident = sb("neg_ident", [P, P])
        iota_i = sb("iota_i", [P, NCP], i32)
        iota = sb("iota", [P, P])
        iota_t = sb("iota_t", [P, NT], f16)
        part = sb("part", [P, 1])
        before = sb("before", [P, P])
        before16 = sb("before16", [P, P], f16)
        notbefore16 = sb("notbefore16", [P, P], f16)
        after = sb("after", [P, P])
        row0 = sb("row0", [P, P])
        ones = sb("ones", [P, P])
        minus_half = sb("minus_half", [P, TG])
        zeros = sb("zeros", [P, TG, 2 * D])

        wn = sb("wn", [P, D])
        we = sb("we", [P, 2 * D])
        wl = sb("wl", [P, 2 * D])
        w1 = sb("w1", [P, 3, D])
        wnT = sb("wnT", [P, D])
        wl2T = sb("wl2T", [P, D])
        wz = sb("wz", [P, 2 * D])
        wmid = sb("wmid", [P, D])
        wsum = sb("wsum", [P, D])
        wabs = sb("wabs", [P, D])
        wx = sb("wx", [P, 2 * D])
        wg = sb("wg", [P, 2 * D])
        bcol = sb("bcol", [P, 2])
        bias3 = sb("bias3", [3, D])
        brow = sb("brow", [1, 2, D])
        bx = sb("bx", [1, 2 * D])
        vec_row = sb("vec_row", [1, 5 * D + 3])
        vec = sb("vec", [P, 5 * D + 3])
        ones_row = sb("ones_row", [1, P])

        sort_area = sb("sort_area", [P, 13 * NCP])

        s_raw = sb("s_raw", [P, NB, P], i32)
        d_raw = sb("d_raw", [P, NB, P], i32)
        nat_area = sb("nat_area", [P, 2 * NB * P])
        s_nat = nat_area[:, 0:NB * P].rearrange("p (b n) -> p b n", b=NB)
        d_nat = nat_area[:, NB * P:2 * NB * P].rearrange("p (b n) -> p b n", b=NB)
        t0_raw = sb("t0_raw", [P, NB], i32)
        t0_col = sb("t0_col", [P, 2, NB])
        s_i = sb("s_i", [P, NCP], i32)
        d_i = sb("d_i", [P, NCP], i32)
        tmp_i = sb("tmp_i", [P, NCP], i32)
        tmp2_i = sb("tmp2_i", [P, NCP], i32)
        td = sb("td", [P, NCP])
        ld = sb("ld", [P, NCP])
        hi = sort_area[:, 0 * NCP:1 * NCP]
        lo = sort_area[:, 1 * NCP:2 * NCP]
        valid = sb("valid", [P, NCP])
        selfe = sort_area[:, 2 * NCP:3 * NCP]
        other = sort_area[:, 3 * NCP:4 * NCP]
        in0 = sb("in0", [P, NCP])
        in1 = sb("in1", [P, NCP])
        t0 = sort_area[:, 4 * NCP:5 * NCP]
        cols = sort_area[:, 5 * NCP:6 * NCP]
        n_first = sort_area[:, 6 * NCP:7 * NCP]
        o_first = sort_area[:, 7 * NCP:8 * NCP]
        pre = sort_area[:, 8 * NCP:9 * NCP]
        nxt = sort_area[:, 9 * NCP:10 * NCP]
        start = sort_area[:, 10 * NCP:11 * NCP]
        rank = sort_area[:, 11 * NCP:12 * NCP]
        ta = sb("ta", [P, NCP])
        tb = sb("tb", [P, NCP])
        bad = sort_area[:, 12 * NCP:13 * NCP]
        place_v = sb("place_v", [P, NCP, 4], f16)
        count_v = sb("count_v", [P, NCP, 4], f16)
        place_oh = sb("place_oh", [P, 2, CB, P], f16)
        local_oh = sb("local_oh", [P, 2, CB, P], f16)
        fields = sb("fields", [P, 8, P], f16)
        fieldsT = sb("fieldsT", [P, 8, P], f16)
        fold = sb("fold", [P, 2, NT], f16)

        slot_hi = sb("slot_hi", [P, NT])
        slot_lo = sb("slot_lo", [P, NT])
        slot_i = sb("slot_i", [P, NT], i32)
        slot_j = sb("slot_j", [P, NT], i32)
        slot_k = sb("slot_k", [P, NT], i32)
        slot_f = sb("slot_f", [P, NT])
        occ = sb("occ", [P, NT])
        idx0 = sb("idx0", [P, NT], i32)
        loc0 = sb("loc0", [P, NT])
        idx1 = sb("idx1", [P, NT], i32)
        loc1 = sb("loc1", [P, NT])
        n_self = sb("n_self", [P, NT])
        n_in = sb("n_in", [P, NT])
        n_out = sb("n_out", [P, NT])
        dinv = sb("dinv", [P, NT])
        self_w = sb("self_w", [P, NT])
        rc = sb("rc", [P, NT])
        some = sb("some", [P, NT])
        statT = sb("statT", [P, 2, 4, P])
        sort_f = sb("sort_f", [P, NT, 4])
        sort_s = sb("sort_s", [P, 2, CB, 4])
        tile_oh = sb("tile_oh", [P, CB, NT], f16)
        src_oh = sb("src_oh", [P, CB, P], f16)
        rank_oh = sb("rank_oh", [P, CB, P], f16)
        hi_oh = sb("hi_oh", [P, CB, P], f16)
        lo_oh = sb("lo_oh", [P, CB, P], f16)
        junk = sb("junk", [P, 2, NT], f16)
        rank0 = sb("rank0", [P, NT])
        rank_s = sb("rank_s", [P, 2, CB])
        spare = sb("spare", [P, 5])
        badsum = sb("badsum", [P, 2])
        okv = sb("okv", [P, 1])
        flag = sb("flag", [P, 1], i32)

        xg = sb("xg", [P, 2, TG, D])
        gx = sb("gx", [P, 2, TG, W])
        gidx = sb("gidx", [P, 2, TG], i32)
        oh = sb("oh", [P, 2, TG, P])
        ohT = sb("ohT", [P, TG, P])
        xT = [sb("xT", [P, TG, P])[:], sort_area[:, 3072:3584].rearrange("p (t n) -> p t n", t=TG)]
        dT = sb("dT", [P, TG, P])
        hd = sb("hd", [P, TG, P])
        s1T = sb("s1T", [P, TG, P])
        s2T = sb("s2T", [P, TG, P])
        row3 = sb("row3", [3, 2, TG * P])
        p2 = sb("p2", [P, TG, D])
        res = sb("res", [P, TG, D])
        stats = sb("stats", [P, TG, 6])
        mv = sb("mv", [P, TG, 2])
        vare = sb("vare", [P, TG])
        rstd = sb("rstd", [P, TG])
        h1g = sb("h1g", [P, 2, TG, W])
        accg = sb("accg", [P, TG, 2 * D])
        diag = sort_area[:, 0:1024].rearrange("p (s t n) -> p s t n", s=2, t=TG)
        gam = sb("gam", [P, TG])
        gs = sort_area[:, 1024:2048].rearrange("p (t n) -> p t n", t=TG)
        q = sort_area[:, 2048:4096].rearrange("p (s t n) -> p s t n", s=2, t=TG)
        ay = sort_area[:, 4096:5632].rearrange("p (k t n) -> p k t n", t=TG, k=3)
        outg = sort_area[:, 5632:6656].rearrange("p (s t n) -> p s t n", s=2, t=TG)
        dot_junk = nat_area[:, 0:3 * TG * D // 2].bitcast(f16).rearrange("p (k t n) -> p k t n", k=3, t=TG)
        own_sum = xg
        nb_sum = (dT, hd)
        dots = sb("dots", [P, 3, TG])
        gates = sb("gates", [P, 3, TG])

        e_idx = sb("e_idx", [P, 2], i32)
        e_key = sb("e_key", [P, 1])
        e_ok = sb("e_ok", [P, 1])
        e_rows = sb("e_rows", [P, 2, W])
        e_diff = sb("e_diff", [P, D])
        e_diffT = sb("e_diffT", [P, D])
        e_pay = sb("e_pay", [P, 2 * D])
        e_keyb = sb("e_keyb", [P, P])
        e_same = sb("e_same", [P, P])
        e_junk = sb("e_junk", [P, P])
        e_prev = sb("e_prev", [P, 1])
        e_lead = sb("e_lead", [P, 1])
        e_tgt = sb("e_tgt", [P, 1])
        e_tgti = sb("e_tgti", [P, 1], i32)
        e_sum = sb("e_sum", [P, 2 * D])
        g_oh = tile_oh[:, 0:2]
        g_loh = rank_oh[:, 0:2]

        wload = sem("weights_loaded")
        bload = sem("z_biases_loaded")
        eload = sem("edges_loaded")
        iotas = sem("iotas_ready")
        consts = sem("constants_ready")
        vchain = sem("vector_steps")
        pchain = sem("pool_steps")
        zeroed = sem("buffers_zeroed")
        wT_ps = sem("weights_transposed")
        wT_sb = sem("weights_copied")
        nat = sem("edges_as_float")
        edgeT = sem("edges_transposed")
        t_ready = sem("dst_tiles_ready")
        t0_ps = sem("first_tiles_summed")
        masks = sem("masks_ready")
        sums_ps = sem("chunk_sums_ready")
        pre_rd = sem("chunk_sums_read")
        lower_ps = sem("ranks_in_chunk_ready")
        place = sem("place_onehots_ready")
        placed = sem("chunks_placed")
        block_rd = sem("block_fields_copied")
        fieldT = sem("block_fields_transposed")
        fieldT_sb = sem("block_transposes_copied")
        fold_rdy = sem("fold_onehots_ready")
        folded = sem("blocks_folded")
        tab1 = sem("table1_ready")
        s_staged = sem("sort_columns_staged")
        s_used = sem("sort_columns_used")
        s_oh = sem("sort_tile_onehots")
        s_src = sem("sort_src_onehots")
        s_rankps = sem("sort_ranks_in_psum")
        s_rank = sem("sort_ranks_read")
        s_kept = sem("sort_ranks_kept")
        s_roh = sem("sort_rank_onehots")
        s_val = sem("sort_value_onehots")
        s_done = sem("sort_columns_done")
        bad_rdy = sem("bad_sums_ready")
        bad_ps = sem("bad_total_ready")
        flagged = sem("flag_ready")
        stat_rdy = sem("stats_ready")
        dinv_rdy = sem("dinv_ready")
        statT_ps = sem("stats_transposed")
        statT_sb = sem("stats_transposed_copied")
        rows_st = sem("stat_rows_stored")

        xl = [sem(f"x_loaded{s}") for s in range(2)]
        rl = [sem(f"rows_loaded{s}") for s in range(2)]
        gidx_rdy = sem("gather_indices_ready")
        gat = [sem(f"rows_gathered{s}") for s in range(2)]
        oh_rdy = sem("onehots_ready")
        trans = sem("l0_transposed")
        diag0 = sem("l0_diagonals_ready")
        n_self_rdy = sem("self_counts_ready")
        xT_sb = sem("l0_xT_copied")
        ohT_sb = sem("l0_onehotT_copied")
        dT_ps = sem("l0_differences_ready")
        dT_sb = sem("l0_differences_copied")
        hd_ps = sem("l0_edge_products_ready")
        hd_sb = sem("l0_edge_abs_ready")
        s1_ps = sem("l0_sums_ready")
        s1_sb = sem("l0_sums_copied")
        s2_ps = sem("l0_abs_sums_ready")
        s2_sb = sem("l0_abs_sums_copied")
        z_ps = sem("l0_z_ready")
        p2_sb = sem("l0_p2_scaled")
        z_rd = sem("l0_z_read")
        stats0 = sem("l0_stats_ready")
        var0 = sem("l0_var_ready")
        rstd0 = sem("l0_rstd_ready")
        h1_rdy = sem("l0_rows_ready")
        h1_st = [sem(f"l0_rows_stored{s}") for s in range(2)]

        hl = [sem(f"l1_rows_loaded{s}") for s in range(2)]
        gat1 = [sem(f"l1_rows_gathered{s}") for s in range(2)]
        gidx1 = sem("l1_gather_indices_ready")
        oh1 = sem("l1_onehots_ready")
        diag_rdy = sem("l1_diagonals_ready")
        yT_ps = sem("l1_yT_ready")
        yT_sb = sem("l1_yT_copied")
        hT_ps = sem("l1_hT_ready")
        hT_sb = sem("l1_hT_copied")
        g_ps = sem("l1_g_ready")
        g_sb = sem("l1_g_scaled")
        x_rd = sem("l1_x_read")
        gam_rd = sem("l1_gamma_read")
        xi_ps = sem("l1_own_products_ready")
        xh_ps = sem("l1_high_products_ready")
        gam_sum = sem("l1_gamma_summed")
        q_rdy = sem("l1_neighbour_parts_ready")
        dots2_rdy = sem("l1_own_dots_ready")
        gate2_rdy = sem("l1_own_gates_ready")
        ay2_rdy = sem("l1_own_gated_ready")
        dots_rdy = sem("l1_dots_ready")
        gate_rdy = sem("l1_gates_ready")
        ay_rdy = sem("l1_gated_ready")
        own_rdy = sem("l1_own_sums_ready")
        nb_rdy = sem("l1_neighbour_sums_ready")
        res_rdy = sem("l1_residuals_ready")
        stats1 = sem("l1_stats_ready")
        var1 = sem("l1_var_ready")
        rstd1 = sem("l1_rstd_ready")
        out_rdy = sem("l1_out_ready")
        out_st = [sem(f"l1_out_stored{s}") for s in range(2)]

        accz = sem("gen_accumulators_zeroed")
        accl = sem("gen_accumulators_loaded")
        acc_rd = sem("gen_accumulators_read")
        g_chain = sem("gen_vector_steps")
        g_ohr = sem("gen_onehots_ready")
        g_cnt = sem("gen_counted")
        g_take = sem("gen_waits_taken")
        g_idx = sem("gen_indices_ready")
        g_gat = sem("gen_rows_gathered")
        g_dif = sem("gen_differences_ready")
        g_pe = sem("gen_products_ready")
        g_v = sem("gen_vector_ready")
        g_sct = sem("gen_rows_added")
        g_hst = sem("gen_l0_stores_seen")

        block = ctx.enter_context(nc.Block())

        class Steps:

            def __init__(self, eng, s):
                self.eng, self.s, self.n = eng, s, 0

            def mark(self, ins):
                self.n += 1
                ins.then_inc(self.s, 1)

            def link(self, ins):
                self.mark(ins)
                self.eng.wait_ge(self.s, self.n)

        LAST = N - (NG - 1) * P * TG
        LT, LR = LAST // P, LAST % P

        def group_parts(dram, g, tile):
            if not isinstance(g, int) or g < NG - 1:
                return [(dram[bass.ds(g * (P * TG), P * TG), :].rearrange("(t p) d -> p t d", p=P), tile[:, 0:TG, :])]
            at = (NG - 1) * P * TG
            return [(dram[at:at + LT * P, :].rearrange("(t p) d -> p t d", p=P), tile[:, 0:LT, :]),
                    (dram[at + LT * P:N, :], tile[0:LR, LT, :])]

        LAST_PARTS = 2

        @block.sync
        def _(sp):
            for t, d in ((wn, wn_d), (we, we_d), (wl, wl_d), (w1[:, 0, :], whp_d), (w1[:, 1, :], wlp_d), (w1[:, 2, :], wi_d)):
                sp.dma_start(t[:] if t in (wn, we, wl) else t, d[:, :]).then_inc(wload, 16)
            for k, d in enumerate((bn_d, be_d)):
                sp.dma_start(bcol[:, k:k + 1], d.rearrange("(p o) -> p o", o=1)).then_inc(wload, 16)
            row = lambda d: d.rearrange("(o n) -> o n", o=1)
            for k, d in enumerate((bhp_d, bi_d)):
                sp.dma_start(bx[0:1, k * D:(k + 1) * D], row(d)).then_inc(wload, 16)
            for k, d in enumerate((bhp_d, blp_d, wvh_d, wvl_d, wvi_d)):
                sp.dma_start(vec_row[0:1, k * D:(k + 1) * D], row(d)).then_inc(wload, 16)
            for k, d in enumerate((bvh_d, bvl_d, bvi_d)):
                sp.dma_start(vec_row[0:1, 5 * D + k:5 * D + k + 1], row(d)).then_inc(wload, 16)
            sp.wait_ge(zeroed, 2)
            full = NB - 1
            for raw, d in ((s_raw, src_d), (d_raw, dst_d)):
                sp.dma_start(raw[:, 0:full, :], d[0:full * P * P].rearrange("(b k p) -> k b p", k=P, p=P)).then_inc(eload, 16)
                left = (E - full * P * P) // P
                sp.dma_start(raw[0:left, full, :], d[full * P * P:(full * P + left) * P].rearrange("(k p) -> k p", p=P)).then_inc(eload, 16)
                sp.dma_start(raw[left:left + 1, full, 0:E % P], d[E - E % P:E].rearrange("(o p) -> o p", o=1)).then_inc(eload, 16)
            sp.wait_ge(zeroed, 4)
            sp.dma_start(bias3[2:3, :], row(bl_d)).then_inc(bload, 16)
            sp.wait_ge(wT_sb, 3)
            sp.dma_start(bias3[0:1, :], brow[0:1, 0, :]).then_inc(bload, 16)
            sp.dma_start(bias3[1:2, :], brow[0:1, 1, :]).then_inc(bload, 16)
            sp.wait_ge(flagged, 1)
            general = sp.value_load(flag[0:1, 0:1], min_val=0, max_val=1)
            with sp.If(general > 0):
                for g in range(NG):
                    sp.dma_start(acc0_d[g * 512:(g + 1) * 512, :].rearrange("(t p) d -> p t d", p=P), zeros[:]).then_inc(accz, 16)
                    sp.dma_start(acc1_d[g * 512:(g + 1) * 512, :].rearrange("(t p) d -> p t d", p=P), zeros[:, :, 0:W]).then_inc(accz, 16)
                sp.dma_start(acc0_d[NPAD:NPAD + P, :], zeros[:, 0, :]).then_inc(accz, 16)
                sp.dma_start(acc1_d[NPAD:NPAD + P, :], zeros[:, 0, 0:W]).then_inc(accz, 16)
                sp.wait_ge(accz, 16 * (2 * NG + 2))
            sp.wait_ge(statT_sb, 1)
            NB4 = -(-NT // P)
            for k in range(2):
                for b in range(NB4):
                    n = min(P, NT - b * P)
                    sp.dma_start(rows_d[k, b * P * P:(b * P + n) * P].rearrange("(t p) -> t p", p=P),
                                 statT[0:n, k, b, :]).then_inc(rows_st, 16)
            with sp.If(general > 0):
                sp.wait_ge(g_sct, 16 * NC)

            sp.wait_ge(rows_st, 16 * 2 * NB4)

            def l0_load(g, s):
                if not (isinstance(g, int) and g < 2):
                    sp.wait_ge(s1_ps, g - 1)
                for a, b in group_parts(x_d, g, xg[:, s]):
                    sp.dma_start(b, a).then_inc(xl[s], 16)

            def l0_load_rows(g, s):
                sp.dma_start(row3[0:2, s, :], rows_d[:, bass.ds(g * (P * TG), P * TG)]).then_inc(rl[s], 16)

            def acc_load(acc_d, width, g, base):
                with sp.If(general > 0):
                    if not (isinstance(g, int) and g + base == 0):
                        sp.wait_ge(acc_rd, g + base)
                    sp.dma_start(accg[:, :, 0:width],
                                 acc_d[bass.ds(g * (P * TG), P * TG), :].rearrange("(t p) d -> p t d", p=P)).then_inc(accl, 16)

            def l0_store(g, s, z_count=None):
                sp.wait_ge(h1_rdy, g + 1)
                if z_count is not None:
                    sp.wait_ge(z_ps, z_count)
                for a, b in group_parts(h1_d, g, h1g[:, s]):
                    sp.dma_start(a, b).then_inc(h1_st[s], 16)

            for g in (0, 1):
                l0_load(g, g)
                acc_load(acc0_d, 2 * D, g, 0)
                l0_load_rows(g, g)
            l0_load(2, 0)
            acc_load(acc0_d, 2 * D, 2, 0)
            sp.wait_ge(z_ps, 1)
            l0_load_rows(2, 0)
            with sp.Fori(0, NG // 2 - 2) as i:
                for s in range(2):
                    l0_load(2 * i + (3 + s), 1 - s)
                    acc_load(acc0_d, 2 * D, 2 * i + (3 + s), 0)
                    l0_store(2 * i + s, s, 2 * i + (2 + s))
                    l0_load_rows(2 * i + (3 + s), 1 - s)
            l0_load(NG - 1, 1)
            acc_load(acc0_d, 2 * D, NG - 1, 0)
            l0_store(NG - 4, 0, NG - 2)
            l0_load_rows(NG - 1, 1)
            for g in (NG - 3, NG - 2, NG - 1):
                l0_store(g, g % 2)
            for s in range(2):
                sp.wait_ge(h1_st[s], 16 * (NG // 2 + (LAST_PARTS - 1) * s))
            with sp.If(general > 0):
                sp.wait_ge(g_sct, 16 * 2 * NC)

            def l1_load(g, s, first):
                if not first:
                    sp.wait_ge(own_rdy, g - 1)
                for a, b in group_parts(h1_d, g, h1g[:, s]):
                    sp.dma_start(b, a).then_inc(hl[s], 16)

            def l1_store(g, s):
                sp.wait_ge(out_rdy, g + 1)
                for a, b in group_parts(out_d, g, outg[:, s]):
                    sp.dma_start(a, b).then_inc(out_st[s], 16)

            def l1_step(g, s):
                l1_load(g, s, isinstance(g, int) and g < 2)
                acc_load(acc1_d, W, g, NG)

            for g in range(4):
                l1_step(g, g % 2)
            with sp.Fori(0, NG // 2 - 3) as i:
                for s in range(2):
                    l1_store(2 * i + s, s)
                    l1_step(2 * i + (4 + s), s)
            for g in range(NG - 6, NG):
                l1_store(g, g % 2)
                if g + 4 < NG:
                    l1_step(g + 4, g % 2)
            for s in range(2):
                sp.wait_ge(out_st[s], 16 * (NG // 2 + (LAST_PARTS - 1) * s))

        @block.gpsimd
        def _(pool):
            st = Steps(pool, pchain)
            last_node, last_row = pool.to_reg(N - 1), pool.to_reg(NPAD + P - 1)
            nc.gpsimd.memset(s_raw[:], N - 1).then_inc(zeroed, 1)
            nc.gpsimd.memset(d_raw[:], N - 1).then_inc(zeroed, 1)
            nc.gpsimd.memset(row3[:], 1.0).then_inc(zeroed, 1)
            nc.gpsimd.memset(ones_row[:], 1.0).then_inc(zeroed, 1)
            nc.gpsimd.iota(iota_i[:], pattern=[[P, NCP]], base=0, channel_multiplier=1).then_inc(iotas, 1)
            nc.gpsimd.iota(tmp_i[:], pattern=[[1, NCP]], base=0, channel_multiplier=0).then_inc(iotas, 1)
            nc.gpsimd.memset(ones[:], 1.0).then_inc(pchain, 1)
            nc.gpsimd.memset(minus_half[:], -0.5)
            nc.gpsimd.memset(zeros[:], 0.0)
            nc.gpsimd.memset(gx[:], 0.0)
            nc.gpsimd.memset(accg[:], 0.0)
            nc.gpsimd.memset(e_rows[:], 0.0)
            nc.gpsimd.memset(xg[:], 0.0)
            nc.gpsimd.memset(h1g[:], 0.0)
            pool.wait_ge(pchain, 1)
            st.n = 1
            st.mark(nc.gpsimd.affine_select(out=before[:], in_=ones[:], compare_op=ALU.is_gt, fill=0.0, base=0,
                                            pattern=[[1, P]], channel_multiplier=-1))
            st.mark(nc.gpsimd.affine_select(out=after[:], in_=ones[:], compare_op=ALU.is_gt, fill=0.0, base=0,
                                            pattern=[[-1, P]], channel_multiplier=1))
            st.mark(nc.gpsimd.affine_select(out=ident[:], in_=ones[:], compare_op=ALU.is_equal, fill=0.0, base=0,
                                            pattern=[[1, P]], channel_multiplier=-1))
            st.link(nc.gpsimd.affine_select(out=row0[:], in_=ones[:], compare_op=ALU.is_equal, fill=0.0, base=0,
                                            pattern=[[0, P]], channel_multiplier=1))
            nc.gpsimd.tensor_copy(before16[:], before[:]).then_inc(consts, 1)
            nc.gpsimd.tensor_copy(ident16[:], ident[:]).then_inc(consts, 1)
            nc.gpsimd.tensor_scalar(neg_ident[:], ident[:], -1.0, 0.0, ALU.mult, ALU.add).then_inc(consts, 1)
            nc.gpsimd.tensor_scalar(notbefore16[:], before[:], -1.0, 1.0, ALU.mult, ALU.add).then_inc(consts, 1)

            def src_onehots(i, s):
                pool.wait_ge(s_staged, i + 1)
                for c in range(CB):
                    if not (isinstance(i, int) and i == 0):
                        pool.wait_ge(s_done, CB * i + (c + 1 - CB))
                        nc.gpsimd.tensor_tensor(spare[0:1, c:c + 1], ones[0:1, 0:1], ones[0:1, 0:1], ALU.add)
                    nc.gpsimd.tensor_scalar(src_oh[:, c, :], iota[:], sort_s[:, s, c, 1:2], None, ALU.is_equal).then_inc(s_src, 1)

            for i in range(2):
                src_onehots(i, i)
            with pool.Fori(1, NT // CB // 2) as i:
                for s in range(2):
                    src_onehots(2 * i + s, s)

            pool.wait_ge(flagged, 1)
            general = pool.value_load(flag[0:1, 0:1], min_val=0, max_val=1)

            pool.wait_ge(stat_rdy, 1)
            nc.gpsimd.tensor_tensor(dinv[:], slot_f[:], slot_hi[:], ALU.pow).then_inc(dinv_rdy, 1)

            def take(idx_count, count):
                if not isinstance(count, int):
                    pool.wait_ge(g_take, count)
                    pool.wait_ge(g_idx, idx_count)
                nc.gpsimd.tensor_tensor(spare[0:1, 2:3], ones[0:1, 0:1], ones[0:1, 0:1], ALU.add).then_inc(g_take, 1)

            def edge_rows(count, rows, width, acc, payload):
                take(count, count)
                for k, (table, col) in enumerate(rows):
                    nc.gpsimd.indirect_dma_start(out=e_rows[:, k, 0:width], out_offset=None, in_=table,
                                                 in_offset=bass.IndirectOffsetOnAxis(ap=e_idx[:, col:col + 1], axis=0),
                                                 bounds_check=last_node, oob_is_err=False).then_inc(g_gat, 16)

            with pool.If(general > 0):
                pool.wait_ge(accz, 16 * (2 * NG + 2))
                take(0, 0)
                with pool.Fori(0, NC) as k:
                    edge_rows(2 * k + 1, [(x_d, 0), (x_d, 1)], D, acc0_d, e_sum)
                    take(2 * k + 2, 2 * k + 2)
                    nc.gpsimd.indirect_dma_start(out=acc0_d, out_offset=bass.IndirectOffsetOnAxis(ap=e_tgti[:, 0:1], axis=0),
                                                 in_=e_sum[:, 0:2 * D], in_offset=None, bounds_check=last_row,
                                                 compute_op=ALU.add).then_inc(g_sct, 16)
                    pool.wait_ge(g_sct, 16 * k + 16)

            def gathers(g, s, table, width, sems, ready):
                pool.wait_ge(ready, g + 1)
                if not isinstance(g, int):
                    nc.gpsimd.tensor_tensor(spare[0:1, s:s + 1], ones[0:1, 0:1], ones[0:1, 0:1], ALU.add)
                for t in range(TG):
                    nc.gpsimd.indirect_dma_start(out=gx[:, s, t, 0:width], out_offset=None, in_=table,
                                                 in_offset=bass.IndirectOffsetOnAxis(ap=gidx[:, s, t:t + 1], axis=0),
                                                 bounds_check=last_node, oob_is_err=False).then_inc(sems[s], 16)

            def rstds(g, var, done):
                pool.wait_ge(var, g + 1)
                nc.gpsimd.tensor_tensor(rstd[:], vare[:], minus_half[:], ALU.pow).then_inc(done, 1)

            gathers(0, 0, x_d, D, gat, gidx_rdy)
            gathers(1, 1, x_d, D, gat, gidx_rdy)
            gathers(2, 0, x_d, D, gat, gidx_rdy)
            with pool.Fori(0, NG // 2 - 2) as i:
                for s in range(2):
                    rstds(2 * i + s, var0, rstd0)
                    gathers(2 * i + (3 + s), 1 - s, x_d, D, gat, gidx_rdy)
            rstds(NG - 4, var0, rstd0)
            gathers(NG - 1, 1, x_d, D, gat, gidx_rdy)
            for g in (NG - 3, NG - 2, NG - 1):
                rstds(g, var0, rstd0)

            for s in range(2):
                pool.wait_ge(h1_st[s], 16 * (NG // 2 + (LAST_PARTS - 1) * s))
            with pool.If(general > 0):
                with pool.Fori(0, NC) as k:
                    edge_rows(2 * k + (2 * NC + 1), [(h1_d, 0)], W, acc1_d, e_sum)
                    take(2 * k + (2 * NC + 2), 2 * k + (2 * NC + 2))
                    nc.gpsimd.indirect_dma_start(out=acc1_d, out_offset=bass.IndirectOffsetOnAxis(ap=e_tgti[:, 0:1], axis=0),
                                                 in_=e_sum[:, 0:W], in_offset=None, bounds_check=last_row,
                                                 compute_op=ALU.add).then_inc(g_sct, 16)
                    pool.wait_ge(g_sct, 16 * k + (16 * NC + 16))
            def own_sums(g, s):
                if not (isinstance(g, int) and g < 2):
                    pool.wait_ge(res_rdy, g - 1)
                pool.wait_ge(ay2_rdy, g + 1)
                nc.gpsimd.tensor_tensor(own_sum[:, s], ay[:, 2], h1g[:, s, :, 0:D], ALU.add).then_inc(own_rdy, 1)

            def neighbour_sums(g, s):
                pool.wait_ge(ay_rdy, g + 1)
                nc.gpsimd.tensor_tensor(nb_sum[s][:], ay[:, 0], ay[:, 1], ALU.add).then_inc(nb_rdy, 1)

            for g in range(3):
                gathers(g, g % 2, h1_d, W, gat1, gidx1)

            def l1_step(g, s):
                own_sums(g, s)
                if not (isinstance(g, int) and g + 3 >= NG):
                    gathers(g + 3, 1 - s, h1_d, W, gat1, gidx1)
                neighbour_sums(g, s)
                if not (isinstance(g, int) and g == 0):
                    rstds(g - 1, var1, rstd1)

            l1_step(0, 0)
            l1_step(1, 1)
            with pool.Fori(1, NG // 2 - 2) as i:
                for s in range(2):
                    l1_step(2 * i + s, s)
            for g in range(NG - 4, NG):
                l1_step(g, g % 2)
            rstds(NG - 1, var1, rstd1)

        @block.vector
        def _(dve):
            v = nc.vector
            st = Steps(dve, vchain)
            L = st.link
            G = Steps(dve, g_chain).link
            dve.wait_ge(iotas, 2)
            v.tensor_copy(iota[:], tmp_i[:, 0:P])
            v.tensor_copy(iota_t[:], tmp_i[:, 0:NT])
            v.tensor_copy(part[:], iota_i[:, 0:1])
            L(v.tensor_scalar(valid[:], iota_i[:], float(E), None, ALU.is_lt))
            dve.wait_ge(eload, 16 * 6)
            v.tensor_copy(s_nat[:], s_raw[:])
            v.tensor_scalar(t0_raw[:], d_raw[:, :, 0], 7, None, ALU.arith_shift_right)
            L(v.tensor_copy(d_nat[:], d_raw[:]))
            v.tensor_copy(t0_col[:, 0, :], t0_raw[:]).then_inc(nat, 1)
            dve.wait_ge(wT_ps, 1)
            v.tensor_copy(wnT[:], bank(4)[:, 0:D])
            v.tensor_tensor(wz[:, 0:D], bank(4)[:, D:2 * D], ident[:], ALU.add)
            v.tensor_copy(wx[:, 0:D], bank(4)[:, 3 * D:4 * D])
            v.tensor_scalar(wg[:, 0:D], bank(4)[:, 3 * D:4 * D], -1.0, None, ALU.mult)
            v.tensor_copy(wg[:, D:2 * D], bank(5)[:, 0:D])
            v.tensor_copy(wx[:, D:2 * D], bank(5)[:, D:2 * D])
            v.tensor_copy(wl2T[:], bank(4)[:, 2 * D:3 * D]).then_inc(wT_sb, 1)
            dve.wait_ge(wT_ps, 2)
            v.tensor_copy(wz[:, D:2 * D], bank(6)[:, 0:D])
            v.tensor_copy(wabs[:], bank(6)[:, 2 * D:3 * D])
            v.tensor_copy(wmid[:], bank(6)[:, D:2 * D]).then_inc(wT_sb, 1)
            dve.wait_ge(wT_ps, 3)
            v.tensor_copy(wsum[:], bank(7)[:, 0:D])
            v.tensor_scalar(vec[:, 0:D], bank(4)[:, 0:D], -1.0, None, ALU.mult)
            v.tensor_copy(vec[:, D:512], bank(4)[:, D:512])
            v.tensor_copy(vec[:, 512:5 * D + 3], bank(5)[:, 0:5 * D + 3 - 512])
            v.tensor_copy(brow[0:1, :, :], bank(7)[0:1, D:3 * D].rearrange("p (a n) -> p a n", a=2)).then_inc(wT_sb, 1)
            dve.wait_ge(edgeT, 1)
            v.memset(s_i[:], N - 1)
            L(v.memset(d_i[:], N - 1))
            v.tensor_copy(s_i[:, 0:NC], bank(0, 2)[:, 0:NC])
            L(v.tensor_copy(d_i[:, 0:NC], bank(2, 2)[:, 0:NC]))
            L(v.tensor_scalar(tmp_i[:], d_i[:], 7, None, ALU.arith_shift_right))
            v.tensor_copy(td[:], tmp_i[:]).then_inc(t_ready, 1)
            L(v.tensor_scalar(tmp2_i[:], d_i[:], 127, None, ALU.bitwise_and))
            v.tensor_copy(ld[:], tmp2_i[:])
            L(v.scalar_tensor_tensor(tmp2_i[:], s_i[:], 7, tmp2_i[:], ALU.logical_shift_left, ALU.bitwise_or))
            L(v.tensor_scalar(tmp_i[:], tmp2_i[:], 12, None, ALU.arith_shift_right))
            L(v.tensor_scalar(tmp2_i[:], tmp2_i[:], 4095, None, ALU.bitwise_and))
            v.tensor_scalar(hi[:], tmp_i[:], 1.0, None, ALU.add)
            v.tensor_scalar(lo[:], tmp2_i[:], -float(HALF), None, ALU.add)
            L(v.tensor_tensor(ta[:], s_i[:], d_i[:], ALU.is_equal))
            L(v.tensor_tensor(selfe[:], ta[:], valid[:], ALU.mult))
            v.tensor_tensor(other[:], valid[:], selfe[:], ALU.subtract)
            dve.wait_ge(t0_ps, 1)
            L(v.tensor_copy(t0[:], bank(0, 2)[:, 0:NCP]))
            L(v.tensor_tensor(ta[:], td[:], t0[:], ALU.subtract))
            v.scalar_tensor_tensor(in0[:], ta[:], 0.0, valid[:], ALU.is_equal, ALU.mult)
            L(v.scalar_tensor_tensor(in1[:], ta[:], 1.0, valid[:], ALU.is_equal, ALU.mult))
            v.tensor_tensor(tb[:], other[:], in0[:], ALU.mult).then_inc(masks, 1)
            dve.wait_ge(sums_ps, 1)
            v.tensor_copy(cols[:], bank(2, 2)[:, 0:NCP])
            v.tensor_copy(o_first[:], bank(4, 2)[:, 0:NCP])
            L(v.tensor_copy(n_first[:], bank(6, 2)[:, 0:NCP]))
            v.memset(ta[:], 1.0).then_inc(pre_rd, 1)
            dve.wait_ge(pre_rd, 1)
            L(v.tensor_tensor_scan(tb[:], ta[:], cols[:], 0.0, ALU.mult, ALU.add))
            L(v.tensor_tensor(pre[:], tb[:], cols[:], ALU.subtract))
            L(v.tensor_tensor(nxt[:], pre[:], o_first[:], ALU.add))
            L(v.memset(ta[:, 0:1], 0.0))
            L(v.tensor_tensor(ta[:, 1:NCP], t0[:, 1:NCP], t0[:, 0:NCP - 1], ALU.subtract))
            v.memset(start[:, 0:1], 0.0)
            L(v.scalar_tensor_tensor(start[:, 1:NCP], ta[:, 1:NCP], 1.0, nxt[:, 0:NCP - 1], ALU.is_equal, ALU.mult))
            L(v.scalar_tensor_tensor(tb[:], ta[:], 1.5, pre[:], ALU.is_gt, ALU.mult))
            L(v.tensor_tensor(start[:], start[:], tb[:], ALU.add))
            L(v.memset(tb[:], 0.0))
            L(v.tensor_tensor_scan(rank[:], tb[:], start[:], 0.0, ALU.add, ALU.max))
            L(v.tensor_copy(start[:], rank[:]))
            L(v.memset(bad[:], 0.0))
            L(v.tensor_scalar(tb[:, 0:NCP - 1], n_first[:, 0:NCP - 1], float(P), None, ALU.is_lt))
            L(v.tensor_tensor(bad[:, 1:NC], ta[:, 1:NC], tb[:, 0:NC - 1], ALU.is_lt))
            L(v.tensor_scalar(tb[:], n_first[:], part[:, 0:1], None, ALU.is_le))
            L(v.tensor_tensor(tb[:], tb[:], valid[:], ALU.mult))
            L(v.tensor_tensor(tb[:], tb[:], in1[:], ALU.not_equal))
            L(v.tensor_tensor(bad[:], bad[:], tb[:], ALU.add))
            L(v.tensor_tensor(tb[:], in0[:], in1[:], ALU.add))
            L(v.tensor_tensor(tb[:], tb[:], valid[:], ALU.not_equal))
            L(v.tensor_tensor(bad[:], bad[:], tb[:], ALU.add))
            dve.wait_ge(lower_ps, 1)
            L(v.tensor_tensor(rank[:], bank(0, 2)[:, 0:NCP], pre[:], ALU.add))
            L(v.tensor_tensor(rank[:], rank[:], start[:], ALU.subtract))
            L(v.tensor_tensor(tb[:], nxt[:], start[:], ALU.subtract))
            L(v.tensor_tensor(tb[:], tb[:], in1[:], ALU.mult))
            L(v.tensor_tensor(rank[:], rank[:], tb[:], ALU.subtract))
            L(v.scalar_tensor_tensor(tb[:], rank[:], float(P) - 0.5, other[:], ALU.is_gt, ALU.mult))
            L(v.tensor_tensor(bad[:], bad[:], tb[:], ALU.add))
            L(v.tensor_reduce(badsum[:, 0:1], bad[:], AX.X, ALU.add))
            L(v.tensor_tensor(ta[:], other[:], in0[:], ALU.mult))
            L(v.tensor_tensor(tb[:], other[:], in1[:], ALU.mult))
            v.tensor_tensor(place_v[:, :, 0], hi[:], ta[:], ALU.mult)
            v.tensor_tensor(place_v[:, :, 1], lo[:], ta[:], ALU.mult)
            v.tensor_tensor(place_v[:, :, 2], hi[:], tb[:], ALU.mult)
            v.tensor_tensor(place_v[:, :, 3], lo[:], tb[:], ALU.mult)
            v.tensor_tensor(count_v[:, :, 0], selfe[:], in0[:], ALU.mult)
            v.tensor_copy(count_v[:, :, 1], ta[:])
            v.tensor_tensor(count_v[:, :, 2], selfe[:], in1[:], ALU.mult)
            L(v.tensor_copy(count_v[:, :, 3], tb[:]))
            L(v.tensor_scalar(t0_col[:, 1, :], t0_col[:, 0, :], 1.0, None, ALU.add))

            def place_step(i, s):
                def wide(t):
                    return t[:, bass.ds(i * CB, CB)].unsqueeze(2).broadcast_to([P, CB, P])
                io = iota[:].unsqueeze(1).broadcast_to([P, CB, P])
                v.tensor_tensor(place_oh[:, s], io, wide(rank), ALU.is_equal)
                v.tensor_tensor(local_oh[:, s], io, wide(ld), ALU.is_equal).then_inc(place, 1)

            at = 0
            for b in range(NB):
                steps = min(P, NCP - b * P) // CB
                n2 = steps // 2
                if b == 0:
                    place_step(0, 0)
                    place_step(1, 1)
                with dve.Fori(1 if b == 0 else 0, n2) as i:
                    for s in range(2):
                        dve.wait_ge(placed, 2 * i + (at + s - 1))
                        place_step(2 * i + (at + s), s)
                at += 2 * n2
                if steps % 2:
                    dve.wait_ge(placed, at - 1)
                    place_step(at, at % 2)
                    at += 1
                if b:
                    dve.wait_ge(folded, b)
                v.tensor_scalar(fold[:, 0, :], iota_t[:], t0_col[:, 0, b:b + 1], None, ALU.is_equal)
                v.tensor_scalar(fold[:, 1, :], iota_t[:], t0_col[:, 1, b:b + 1], None, ALU.is_equal).then_inc(fold_rdy, 1)
                dve.wait_ge(fieldT, b + 1)
                v.tensor_copy(fieldsT[:], bank(2).bitcast(f16).rearrange("p (a n) -> p a n", a=8)).then_inc(fieldT_sb, 1)
            dve.wait_ge(folded, NB)
            v.tensor_copy(slot_hi[:], bank(4)[:, 0:NT])
            v.tensor_copy(slot_lo[:], bank(5)[:, 0:NT])
            v.tensor_copy(n_self[:], bank(6)[:, 0:NT])
            L(v.tensor_copy(n_in[:], bank(7)[:, 0:NT]))

            def table(loc, idx, far_f):
                L(v.tensor_scalar(occ[:], slot_hi[:], 0.5, None, ALU.is_gt))
                L(v.tensor_scalar(slot_f[:], slot_lo[:], float(HALF - 2 * HALF), None, ALU.add))
                L(v.scalar_tensor_tensor(slot_f[:], slot_hi[:], float(2 * HALF), slot_f[:], ALU.mult, ALU.add))
                L(v.tensor_scalar(slot_f[:], slot_f[:], 0.0, None, ALU.max))
                L(v.tensor_copy(slot_i[:], slot_f[:]))
                v.tensor_scalar(slot_j[:], slot_i[:], 127, None, ALU.bitwise_and)
                L(v.tensor_scalar(slot_k[:], slot_i[:], 7, None, ALU.arith_shift_right))
                v.tensor_copy(far_f[:], slot_k[:])
                L(v.tensor_scalar(loc[:], slot_j[:], 1.0, None, ALU.add))
                L(v.tensor_tensor(loc[:], loc[:], occ[:], ALU.mult))
                L(v.tensor_scalar(loc[:], loc[:], -1.0, None, ALU.add))
                L(v.scalar_tensor_tensor(slot_f[:], far_f[:], float(OOB), occ[:], ALU.subtract, ALU.mult))
                L(v.tensor_scalar(slot_f[:], slot_f[:], float(OOB), None, ALU.add))
                v.tensor_copy(idx[:], slot_f[:])

            table(loc1, idx1, slot_lo)
            L(v.tensor_scalar(slot_j[:], slot_k[:], 7, None, ALU.arith_shift_right))
            L(v.tensor_copy(slot_f[:], slot_j[:]))
            L(v.tensor_scalar(slot_f[:], slot_f[:], -999.0, None, ALU.add))
            L(v.tensor_tensor(slot_f[:], slot_f[:], occ[:], ALU.mult))
            v.tensor_scalar(sort_f[:, :, 0], slot_f[:], 999.0, None, ALU.add)
            L(v.tensor_scalar(slot_j[:], slot_k[:], 127, None, ALU.bitwise_and))
            v.tensor_copy(sort_f[:, :, 1], slot_j[:])
            L(v.scalar_tensor_tensor(slot_f[:], iota_t[:], float(P), loc1[:], ALU.mult, ALU.add))
            L(v.tensor_tensor(slot_f[:], slot_f[:], occ[:], ALU.mult))
            L(v.tensor_copy(slot_i[:], slot_f[:]))
            L(v.scalar_tensor_tensor(slot_i[:], slot_i[:], 7, slot_j[:], ALU.logical_shift_left, ALU.bitwise_or))
            L(v.tensor_scalar(slot_k[:], slot_i[:], 12, None, ALU.arith_shift_right))
            L(v.tensor_scalar(slot_i[:], slot_i[:], 4095, None, ALU.bitwise_and))
            v.tensor_scalar(sort_f[:, :, 2], slot_k[:], 1.0, None, ALU.add)
            v.tensor_scalar(sort_f[:, :, 3], slot_i[:], -float(HALF), None, ALU.add).then_inc(tab1, 1)
            dve.wait_ge(tab1, 1)

            def tile_onehot(i, s, c):
                if not (isinstance(i, int) and i == 0):
                    dve.wait_ge(s_done, CB * i + (c + 1 - CB))
                if c == 0:
                    dve.wait_ge(s_staged, i + 1)
                v.tensor_scalar(tile_oh[:, c, :], iota_t[:], sort_s[:, s, c, 0:1], None, ALU.is_equal).then_inc(s_oh, 1)

            def sort_step(i, s, last=False):
                for c in range(CB):
                    dve.wait_ge(s_rankps, CB * i + (c + 1))
                    v.tensor_tensor_reduce(out=junk[:, c % 2, :], in0=tile_oh[:, c, :], in1=bank(0)[:, 0:NT], scale=1.0, scalar=0.0,
                                           op0=ALU.mult, op1=ALU.add, accum_out=rank_s[:, s, c:c + 1]).then_inc(s_rank, 1)
                    if c < 2:
                        tile_onehot(i, s, c + 2)
                    elif not last:
                        tile_onehot(i + 1, 1 - s, c - 2)
                    dve.wait_ge(s_rank, CB * i + (c + 1))
                    v.tensor_scalar(rank_oh[:, c, :], iota[:], rank_s[:, s, c:c + 1], None, ALU.is_equal).then_inc(s_roh, 1)
                v.tensor_copy(rank0[:, bass.ds(CB * i, CB)], rank_s[:, s, :]).then_inc(s_kept, 1)

            tile_onehot(0, 0, 0)
            tile_onehot(0, 0, 1)
            sort_step(0, 0)
            sort_step(1, 1)
            with dve.Fori(1, NT // CB // 2 - 1) as i:
                for s in range(2):
                    sort_step(2 * i + s, s)
            sort_step(NT // CB - 2, 0)
            sort_step(NT // CB - 1, 1, last=True)
            dve.wait_ge(s_done, NT)
            v.tensor_copy(slot_hi[:], bank(1)[:, 0:NT])
            dve.wait_ge(s_kept, NT // CB)
            L(v.tensor_scalar(junk[:, 0, :], rank0[:], float(P) - 0.5, None, ALU.is_gt))
            L(v.tensor_reduce(badsum[:, 1:2], junk[:, 0, :], AX.X, ALU.add))
            L(v.tensor_tensor(badsum[:, 0:1], badsum[:, 0:1], badsum[:, 1:2], ALU.add))
            v.tensor_copy(slot_lo[:], bank(2)[:, 0:NT])
            v.tensor_copy(n_out[:], bank(3)[:, 0:NT]).then_inc(bad_rdy, 1)
            dve.wait_ge(bad_rdy, 1)
            table(loc0, idx0, slot_lo)
            dve.wait_ge(bad_ps, 1)
            L(v.tensor_scalar(okv[:], bank(0)[:, 0:1], 0.5, None, ALU.is_lt))
            L(v.tensor_scalar(badsum[:, 0:1], okv[:], -1.0, 1.0, ALU.mult, ALU.add))
            v.tensor_copy(flag[:], badsum[:, 0:1]).then_inc(flagged, 1)
            for loc, idx in ((loc0, idx0), (loc1, idx1)):
                L(v.tensor_scalar(loc[:], loc[:], 1.0, okv[:, 0:1], ALU.add, ALU.mult))
                L(v.tensor_scalar(loc[:], loc[:], -1.0, None, ALU.add))
                L(v.tensor_copy(slot_f[:], idx[:]))
                L(v.tensor_scalar(slot_f[:], slot_f[:], -float(OOB), okv[:, 0:1], ALU.add, ALU.mult))
                L(v.tensor_scalar(slot_f[:], slot_f[:], float(OOB), None, ALU.add))
                L(v.tensor_copy(idx[:], slot_f[:]))
            v.tensor_scalar(n_self[:], n_self[:], okv[:, 0:1], None, ALU.mult).then_inc(n_self_rdy, 1)
            dve.wait_ge(n_self_rdy, 1)
            dve.wait_ge(flagged, 1)
            general = dve.value_load(flag[0:1, 0:1], min_val=0, max_val=1)
            with dve.If(general > 0):
                G(v.tensor_scalar(tmp_i[:], s_i[:], 7, None, ALU.arith_shift_right))
                G(v.tensor_copy(ta[:], tmp_i[:]))
                G(v.tensor_scalar(tmp_i[:], s_i[:], 127, None, ALU.bitwise_and))
                G(v.tensor_copy(tb[:], tmp_i[:]))
                G(v.tensor_scalar(in0[:], valid[:], -999.0, 999.0, ALU.mult, ALU.add))
                G(v.tensor_tensor(ta[:], ta[:], in0[:], ALU.add))
                G(v.tensor_tensor(in1[:], td[:], in0[:], ALU.add))

                def count_onehots(k):
                    v.tensor_scalar(g_loh[:, 0, :], iota[:], tb[:, bass.ds(k, 1)], None, ALU.is_equal)
                    v.tensor_scalar(g_loh[:, 1, :], iota[:], ld[:, bass.ds(k, 1)], None, ALU.is_equal)
                    v.tensor_scalar(g_oh[:, 0, :], iota_t[:], ta[:, bass.ds(k, 1)], None, ALU.is_equal)
                    v.tensor_scalar(g_oh[:, 1, :], iota_t[:], in1[:, bass.ds(k, 1)], None, ALU.is_equal).then_inc(g_ohr, 1)

                count_onehots(0)
                with dve.Fori(1, NC) as k:
                    dve.wait_ge(g_cnt, k)
                    count_onehots(k)
                dve.wait_ge(g_cnt, NC)
                v.tensor_copy(n_out[:], bank(1)[:, 0:NT]).then_inc(g_v, 1)
                v.tensor_copy(n_in[:], bank(2)[:, 0:NT]).then_inc(g_v, 1)
                dve.wait_ge(g_v, 2)
            L(v.tensor_tensor(slot_f[:], n_out[:], n_self[:], ALU.add))
            v.tensor_scalar(some[:], slot_f[:], 1.0, None, ALU.min)
            L(v.tensor_scalar(slot_f[:], slot_f[:], 1.0, None, ALU.max))
            L(v.reciprocal(rc[:], slot_f[:]))
            v.memset(slot_hi[:], -0.5)
            L(v.tensor_scalar(self_w[:], n_self[:], 1.0, None, ALU.add))
            v.tensor_tensor(slot_f[:], n_in[:], self_w[:], ALU.add).then_inc(stat_rdy, 1)
            dve.wait_ge(dinv_rdy, 1)
            L(v.tensor_tensor(self_w[:], self_w[:], dinv[:], ALU.mult))
            dve.wait_ge(statT_ps, 1)
            rest = NT % P
            both = bank(4, 2)[:, 0:1024].rearrange("p (a b n) -> p a b n", a=2, b=4)
            v.tensor_copy(statT[:, :, 0:NT // P, :], both[:, :, 0:NT // P, :])
            v.tensor_copy(statT[0:rest, :, NT // P, :], both[0:rest, :, NT // P, :]).then_inc(statT_sb, 1)

            with dve.If(general > 0):
                with dve.Fori(0, NC) as k:
                    ev, dv, kv = e_ok[:, 0:1], None, None
                    col = bass.ds(k, 1)

                    def own(j):
                        dve.wait_ge(g_v, 2 + 12 * k + j)
                    v.tensor_scalar(e_tgt[:], s_i[:, col], -float(OOB), valid[:, col], ALU.add, ALU.mult).then_inc(g_v, 1)
                    v.tensor_scalar(e_key[:], d_i[:, col], -float(OOB), valid[:, col], ALU.add, ALU.mult).then_inc(g_v, 1)
                    own(2)
                    v.tensor_scalar(e_idx[:, 0:1], e_tgt[:], float(OOB), None, ALU.add)
                    v.tensor_scalar(e_idx[:, 1:2], e_key[:], float(OOB), None, ALU.add).then_inc(g_idx, 1)
                    v.tensor_scalar(e_keyb[:], ones[:], e_tgt[:, 0:1], None, ALU.mult).then_inc(g_dif, 1)
                    dve.wait_ge(g_gat, 32 * k + 32)
                    v.tensor_tensor(e_diff[:], e_rows[:, 0, 0:D], e_rows[:, 1, 0:D], ALU.subtract).then_inc(g_dif, 1)
                    v.tensor_copy(e_pay[:, 0:D], e_rows[:, 1, 0:D])
                    dve.wait_ge(g_pe, 4 * k + 1)
                    v.tensor_scalar(e_same[:], bank(0)[:, 0:P], e_tgt[:, 0:1], None, ALU.is_equal).then_inc(g_v, 1)
                    dve.wait_ge(g_pe, 4 * k + 2)
                    v.tensor_copy(e_diffT[:], bank(1)[:, 0:D]).then_inc(g_dif, 1)
                    own(3)
                    v.tensor_tensor(e_junk[:], e_same[:], after[:], ALU.mult).then_inc(g_v, 1)
                    own(4)
                    v.tensor_reduce(e_prev[:], e_junk[:], AX.X, ALU.add).then_inc(g_v, 1)
                    own(5)
                    v.tensor_scalar(e_prev[:], e_prev[:], 0.5, None, ALU.is_lt).then_inc(g_v, 1)
                    own(6)
                    v.tensor_tensor(e_lead[:], e_prev[:], valid[:, col], ALU.mult).then_inc(g_v, 1)
                    v.tensor_scalar(e_key[:], part[:], float(NPAD - OOB), None, ALU.add).then_inc(g_v, 1)
                    own(8)
                    v.tensor_tensor(e_tgt[:], e_tgt[:], e_key[:], ALU.subtract).then_inc(g_v, 1)
                    own(9)
                    v.scalar_tensor_tensor(e_tgt[:], e_tgt[:], e_lead[:, 0:1], e_key[:], ALU.mult, ALU.add).then_inc(g_v, 1)
                    own(10)
                    v.tensor_scalar(e_tgti[:], e_tgt[:], float(OOB), None, ALU.add)
                    dve.wait_ge(g_pe, 4 * k + 3)
                    v.tensor_scalar(e_junk[:], bank(2)[:, 0:D], -1.0, None, ALU.mult).then_inc(g_v, 1)
                    own(11)
                    v.tensor_tensor(e_pay[:, D:2 * D], bank(2)[:, 0:D], e_junk[:], ALU.max).then_inc(g_dif, 1)
                    dve.wait_ge(g_pe, 4 * k + 4)
                    v.tensor_copy(e_sum[:], bank(3)[:, 0:2 * D]).then_inc(g_v, 1)
                    own(12)
                    v.tensor_copy(e_prev[:], e_prev[:]).then_inc(g_idx, 1)
                    dve.wait_ge(g_sct, 16 * k + 16)

            def l0_indices(g, s):
                if not (isinstance(g, int) and g < 2):
                    dve.wait_ge(s1_ps, g - 1)
                v.tensor_copy(gidx[:, s, :], idx0[:, bass.ds(g * TG, TG)]).then_inc(gidx_rdy, 1)

            def l0_onehots(g, s):
                if not (isinstance(g, int) and g < 2):
                    dve.wait_ge(s2_ps, g - 1)
                v.tensor_tensor(oh[:, s], iota[:].unsqueeze(1).broadcast_to([P, TG, P]),
                                loc0[:, bass.ds(g * TG, TG)].unsqueeze(2).broadcast_to([P, TG, P]), ALU.is_equal).then_inc(oh_rdy, 1)

            def norm(g, own, var):
                for t in range(TG):
                    v.bn_stats(stats[:, t, :], res[:, t, :]).then_inc(own, 1)
                dve.wait_ge(own, 2 * TG * g + TG)
                v.memset(spare[0:1, 3:4], 0.0)
                for t in range(TG):
                    v.bn_aggr(mv[:, t, :], stats[:, t, :]).then_inc(own, 1)
                dve.wait_ge(own, 2 * TG * g + 2 * TG)
                v.tensor_scalar(vare[:], mv[:, :, 1], EPS, None, ALU.add).then_inc(var, 1)

            def l0_abs_copy(g):
                dve.wait_ge(s2_ps, g + 1)
                if not (isinstance(g, int) and g == 0):
                    dve.wait_ge(z_ps, g)
                v.tensor_copy(s2T[:], bank(5).rearrange("p (t n) -> p t n", t=TG)).then_inc(s2_sb, 1)

            def l0_residual(g):
                if not (isinstance(g, int) and g == 0):
                    dve.wait_ge(h1_rdy, g)
                dve.wait_ge(p2_sb, g + 1)
                v.tensor_tensor(res[:], bank(6, 2).rearrange("p (t c n) -> p t c n", t=TG, c=2)[:, :, 0, :],
                                p2[:], ALU.add).then_inc(z_rd, 1)
                dve.wait_ge(z_rd, g + 1)
                norm(g, stats0, var0)

            def l0_apply(g, s, stores):
                if stores is not None:
                    dve.wait_ge(h1_st[s], stores)
                v.tensor_copy(h1g[:, s, :, D], dinv[:, bass.ds(g * TG, TG)])
                dve.wait_ge(rstd0, g + 1)
                for t in range(TG):
                    last = v.tensor_scalar(h1g[:, s, t, 0:D], res[:, t, :], mv[:, t, 0:1], rstd[:, t:t + 1],
                                           ALU.subtract, ALU.mult)
                last.then_inc(h1_rdy, 1)

            def l0_step(g, s, stores):
                whole = isinstance(g, int)
                if not (whole and g + 2 >= NG):
                    l0_indices(g + 2, s)
                l0_abs_copy(g)
                if not (whole and g + 2 >= NG):
                    l0_onehots(g + 2, s)
                if not (whole and g == 0):
                    l0_apply(g - 1, 1 - s, stores)
                l0_residual(g)

            l0_indices(0, 0)
            l0_onehots(0, 0)
            l0_indices(1, 1)
            l0_onehots(1, 1)
            l0_step(0, 0, None)
            l0_step(1, 1, None)
            l0_step(2, 0, None)
            with dve.Fori(1, NG // 2 - 2) as i:
                l0_step(2 * i + 1, 1, 16 * i)
                l0_step(2 * i + 2, 0, 16 * i)
            for g in (NG - 3, NG - 2, NG - 1):
                l0_step(g, g % 2, 16 * ((g - 1) // 2))
            l0_apply(NG - 1, 1, 16 * (NG // 2 - 1))

            with dve.If(general > 0):
                with dve.Fori(0, NC) as k:
                    col = bass.ds(k, 1)
                    vb = 2 + 12 * NC

                    def own(j):
                        dve.wait_ge(g_v, (vb + j) + 12 * k)
                    v.tensor_scalar(e_key[:], s_i[:, col], -float(OOB), valid[:, col], ALU.add, ALU.mult).then_inc(g_v, 1)
                    v.tensor_scalar(e_tgt[:], d_i[:, col], -float(OOB), valid[:, col], ALU.add, ALU.mult).then_inc(g_v, 1)
                    own(2)
                    v.tensor_scalar(e_idx[:, 0:1], e_key[:], float(OOB), None, ALU.add).then_inc(g_idx, 1)
                    v.tensor_scalar(e_keyb[:], ones[:], e_tgt[:, 0:1], None, ALU.mult).then_inc(g_dif, 1)
                    dve.wait_ge(g_gat, 16 * k + (32 * NC + 16))
                    v.tensor_scalar(e_pay[:, 0:D], e_rows[:, 0, 0:D], e_rows[:, 0, D:W], None, ALU.mult)
                    v.tensor_copy(e_pay[:, D:W], e_rows[:, 0, D:W]).then_inc(g_v, 1)
                    dve.wait_ge(g_pe, 2 * k + (4 * NC + 1))
                    v.tensor_scalar(e_same[:], bank(0)[:, 0:P], e_tgt[:, 0:1], None, ALU.is_equal).then_inc(g_dif, 1)
                    dve.wait_ge(g_dif, 4 * NC + 2 * k + 2)
                    v.tensor_tensor(e_junk[:], e_same[:], after[:], ALU.mult).then_inc(g_v, 1)
                    own(4)
                    v.tensor_reduce(e_prev[:], e_junk[:], AX.X, ALU.add).then_inc(g_v, 1)
                    own(5)
                    v.tensor_scalar(e_prev[:], e_prev[:], 0.5, None, ALU.is_lt).then_inc(g_v, 1)
                    own(6)
                    v.tensor_tensor(e_lead[:], e_prev[:], valid[:, col], ALU.mult).then_inc(g_v, 1)
                    v.tensor_scalar(e_key[:], part[:], float(NPAD - OOB), None, ALU.add).then_inc(g_v, 1)
                    own(8)
                    v.tensor_tensor(e_tgt[:], e_tgt[:], e_key[:], ALU.subtract).then_inc(g_v, 1)
                    own(9)
                    v.scalar_tensor_tensor(e_tgt[:], e_tgt[:], e_lead[:, 0:1], e_key[:], ALU.mult, ALU.add).then_inc(g_v, 1)
                    own(10)
                    v.tensor_scalar(e_tgti[:], e_tgt[:], float(OOB), None, ALU.add).then_inc(g_v, 1)
                    dve.wait_ge(g_pe, 2 * k + (4 * NC + 2))
                    v.tensor_copy(e_sum[:, 0:W], bank(3)[:, 0:W]).then_inc(g_v, 1)
                    own(12)
                    v.tensor_copy(e_prev[:], e_prev[:]).then_inc(g_idx, 1)
                    dve.wait_ge(g_sct, 16 * k + (16 * NC + 16))

            def l1_indices(g, s):
                if not (isinstance(g, int) and g < 2):
                    dve.wait_ge(yT_ps, g - 1)
                v.tensor_copy(gidx[:, s, :], idx1[:, bass.ds(g * TG, TG)]).then_inc(gidx1, 1)

            def l1_onehots(g, s, half):
                if not (isinstance(g, int) and g < 2):
                    dve.wait_ge(yT_ps, g - 1)
                dve.wait_ge(gat1[s], (half + 1) * (16 * TG))
                for t in range(TG):
                    last = v.tensor_scalar(oh[:, s, t, :], iota[:], loc1[:, bass.ds(g * TG + t, 1)], gx[:, s, t, D:W],
                                           ALU.is_equal, ALU.mult)
                last.then_inc(oh1, 1)

            def l1_gamma(g):
                dve.wait_ge(yT_ps, g + 1)
                v.tensor_tensor(gam[:], bank(3)[:, 0:TG], self_w[:, bass.ds(g * TG, TG)], ALU.add).then_inc(gam_sum, 1)
                dve.wait_ge(gam_sum, g + 1)
                v.tensor_tensor(gam[:], gam[:], dinv[:, bass.ds(g * TG, TG)], ALU.mult).then_inc(gam_rd, 1)

            xh = bank(6).rearrange("p (t n) -> p t n", t=TG)
            xi = bank(7).rearrange("p (t n) -> p t n", t=TG)

            def l1_dots(g, k, part_of, done):
                for t in range(TG):
                    last = v.scalar_tensor_tensor(dot_junk[:, k, t, :], part_of(t), 0.0, vec[:, (2 + k) * D:(3 + k) * D],
                                                  ALU.max, ALU.mult, accum_out=dots[:, k, t:t + 1])
                if done is not None:
                    last.then_inc(done, 1)

            def l1_gate(g, s):
                first = isinstance(g, int) and g == 0
                dve.wait_ge(xi_ps, g + 1)
                if not first:
                    dve.wait_ge(gate2_rdy, g)
                l1_dots(g, 2, lambda t: xi[:, t, :], dots2_rdy)
                if not (isinstance(g, int) and g < 2):
                    dve.wait_ge(ay_rdy, g - 1)
                dve.wait_ge(gam_rd, g + 1)
                dve.wait_ge(g_sb, g + 1)
                for t in range(TG):
                    last = v.scalar_tensor_tensor(q[:, s, t, :], vec[:, 0:2 * D], gam[:, t:t + 1], gs[:, t, :], ALU.mult, ALU.add)
                last.then_inc(q_rdy, 1)
                if not (isinstance(g, int) and g + 3 >= NG):
                    l1_indices(g + 3, 1 - s)
                dve.wait_ge(q_rdy, g + 1)
                dve.wait_ge(xh_ps, g + 1)
                v.tensor_tensor(q[:, s, :, 0:D], xh, q[:, s, :, 0:D], ALU.add).then_inc(x_rd, 1)
                if not first:
                    dve.wait_ge(gate_rdy, g)
                l1_dots(g, 1, lambda t: q[:, s, t, D:2 * D], None)
                dve.wait_ge(x_rd, g + 1)
                l1_dots(g, 0, lambda t: q[:, s, t, 0:D], dots_rdy)

            def l1_residual(g, s):
                if not (isinstance(g, int) and g == 0):
                    dve.wait_ge(out_rdy, g)
                dve.wait_ge(own_rdy, g + 1)
                dve.wait_ge(nb_rdy, g + 1)
                v.tensor_tensor(res[:], own_sum[:, s], nb_sum[s][:], ALU.add).then_inc(res_rdy, 1)
                dve.wait_ge(res_rdy, g + 1)
                norm(g, stats1, var1)

            def l1_apply(g, s, stores):
                if stores is not None:
                    dve.wait_ge(out_st[s], stores)
                dve.wait_ge(rstd1, g + 1)
                for t in range(TG):
                    last = v.tensor_scalar(outg[:, s, t, :], res[:, t, :], mv[:, t, 0:1], rstd[:, t:t + 1],
                                           ALU.subtract, ALU.mult)
                last.then_inc(out_rdy, 1)

            def l1_step(g, s, half):
                whole = isinstance(g, int)
                l1_gate(g, s)
                if not (whole and g + 1 >= NG):
                    l1_gamma(g + 1)
                if not (whole and g + 2 >= NG):
                    l1_onehots(g + 2, s, half + 1)
                if not (whole and g < 2):
                    l1_apply(g - 2, s, None if whole and g < 4 else (half - 1) * 16)
                if not (whole and g == 0):
                    l1_residual(g - 1, 1 - s)

            l1_indices(0, 0)
            l1_indices(1, 1)
            l1_onehots(0, 0, 0)
            l1_onehots(1, 1, 0)
            l1_indices(2, 0)
            l1_gamma(0)
            for g in range(4):
                l1_step(g, g % 2, g // 2)
            with dve.Fori(2, NG // 2 - 2) as i:
                for s in range(2):
                    l1_step(2 * i + s, s, i)
            for g in range(NG - 4, NG):
                l1_step(g, g % 2, g // 2)
            l1_apply(NG - 2, 0, 16 * (NG // 2 - 1))
            l1_residual(NG - 1, 1)
            l1_apply(NG - 1, 1, 16 * (NG // 2 - 1))

        @block.tensor
        def _(pe):
            mm = nc.tensor.matmul

            def wide_mm(b, lhsT, rhs, start=True, stop=True):
                mm(psum[:, 512 * b:512 * b + 512], lhsT, rhs[:, 0:512], start=start, stop=stop)
                return mm(psum[:, 512 * b + 512:512 * b + NCP], lhsT, rhs[:, 512:NCP], start=start, stop=stop)

            pe.wait_ge(consts, 4)
            pe.wait_ge(wload, 16 * 18)
            for k, w in enumerate((wn[:], wl[:, 0:D], wl[:, D:2 * D], w1[:, 0, :])):
                nc.tensor.transpose(bank(4)[:, k * D:(k + 1) * D], w, ident[:])
            nc.tensor.transpose(bank(5)[:, 0:D], w1[:, 1, :], ident[:])
            nc.tensor.transpose(bank(5)[:, D:2 * D], w1[:, 2, :], ident[:]).then_inc(wT_ps, 1)
            pe.wait_ge(wT_sb, 1)
            mm(bank(6)[:, 0:D], wn[:], wl2T[:], start=True, stop=True)
            mm(bank(6)[:, D:2 * D], we[:, 0:D], wl2T[:], start=True, stop=True)
            mm(bank(6)[:, 2 * D:3 * D], we[:, D:2 * D], wl2T[:], start=True, stop=True).then_inc(wT_ps, 1)
            pe.wait_ge(wT_sb, 2)
            mm(bank(7)[:, 0:D], wn[:], wmid[:], start=True, stop=True)
            mm(bank(7)[0:1, D:2 * D], bcol[:, 0:1], wl2T[:], start=True, stop=True)
            mm(bank(7)[0:1, 2 * D:3 * D], bcol[:, 1:2], wl2T[:], start=True, stop=False)
            mm(bank(7)[0:1, 2 * D:3 * D], bcol[:, 0:1], wmid[:], start=False, stop=True)
            mm(bank(4), ones_row[0:1, :], vec_row[0:1, 0:512], start=True, stop=True)
            mm(bank(5)[:, 0:5 * D + 3 - 512], ones_row[0:1, :], vec_row[0:1, 512:5 * D + 3], start=True, stop=True).then_inc(wT_ps, 1)

            pe.wait_ge(nat, 1)
            for b in range(NB):
                n = min(P, NC - b * P)
                nc.tensor.transpose(psum[:, b * P:b * P + n], s_nat[0:n, b, :], ident[0:n, 0:n])
                last = nc.tensor.transpose(psum[:, 1024 + b * P:1024 + b * P + n], d_nat[0:n, b, :], ident[0:n, 0:n])
            last.then_inc(edgeT, 1)
            pe.wait_ge(t_ready, 1)
            wide_mm(0, row0[:], td).then_inc(t0_ps, 1)
            pe.wait_ge(masks, 1)
            pe.wait_ge(wT_sb, 3)
            wide_mm(2, ones[:], other)
            wide_mm(4, ones[:], tb)
            wide_mm(6, ones[:], in0).then_inc(sums_ps, 1)
            wide_mm(0, before[:], other).then_inc(lower_ps, 1)

            def place_step(i, s, b):
                pe.wait_ge(place, i + 1)
                for c in range(CB):
                    k = i * CB + (c - b * P)
                    o = psum[:, 0:1024].rearrange("p (a f k) -> p a f k", a=2, f=4)
                    mm(o[:, 0, :, bass.ds(k, 1)].rearrange("p f o -> p (f o)"), place_oh[:, s, c, :],
                       place_v[:, bass.ds(i * CB + c, 1), :].rearrange("p o f -> p (o f)"), start=True, stop=True)
                    last = mm(o[:, 1, :, bass.ds(k, 1)].rearrange("p f o -> p (f o)"), local_oh[:, s, c, :],
                              count_v[:, bass.ds(i * CB + c, 1), :].rearrange("p o f -> p (o f)"), start=True, stop=True)
                last.then_inc(placed, 1)

            at = 0
            for b in range(NB):
                n = min(P, NCP - b * P)
                steps = n // CB
                n2 = steps // 2
                if b:
                    pe.wait_ge(block_rd, b)
                with pe.Fori(0, n2) as i:
                    for s in range(2):
                        place_step(2 * i + (at + s), s, b)
                at += 2 * n2
                if steps % 2:
                    place_step(at, at % 2, b)
                    at += 1
                pe.wait_ge(block_rd, b + 1)
                if b:
                    pe.wait_ge(fieldT_sb, b)
                fT = bank(2).bitcast(f16).rearrange("p (a n) -> p a n", a=8)
                for f in range(8):
                    last = nc.tensor.transpose(fT[0:n, f, :], fields[:, f, 0:n], ident16[:])
                last.then_inc(fieldT, 1)
                pe.wait_ge(fold_rdy, b + 1)
                pe.wait_ge(fieldT_sb, b + 1)
                for f in range(8):
                    which, i1 = 2 * (f // 4) + f % 2, (f % 4) // 2
                    last = mm(bank(4 + which)[:, 0:NT], fieldsT[0:n, f, :], fold[0:n, i1, :],
                              start=(b == 0 and i1 == 0), stop=(b == NB - 1 and i1 == 1), skip_group_check=True)
                last.then_inc(folded, 1)

            pe.wait_ge(tab1, 1)

            def rank_mm(j, k, first=False):
                pe.wait_ge(s_oh, j + 1)
                mm(bank(0)[:, 0:NT], before16[:], tile_oh[:, k, :], start=first, stop=True, skip_group_check=True).then_inc(s_rankps, 1)

            def rest_mm(j, k):
                pe.wait_ge(s_rank, j + 1)
                mm(bank(0)[:, 0:NT], notbefore16[:], tile_oh[:, k, :], start=False, stop=True, skip_group_check=True)

            def slots_mm(j, k, first=False):
                pe.wait_ge(s_src, j + 1)
                mm(bank(3)[:, 0:NT], src_oh[:, k, :], tile_oh[:, k, :], start=first, stop=True, skip_group_check=True)
                pe.wait_ge(s_val, j + 1)
                mm(bank(1)[:, 0:NT], hi_oh[:, k, :], tile_oh[:, k, :], start=first, stop=True, skip_group_check=True)
                mm(bank(2)[:, 0:NT], lo_oh[:, k, :], tile_oh[:, k, :], start=first, stop=True, skip_group_check=True).then_inc(s_done, 1)

            rank_mm(0, 0, True)
            rest_mm(0, 0)
            rank_mm(1, 1)
            rest_mm(1, 1)
            rank_mm(2, 2)
            slots_mm(0, 0, True)
            rest_mm(2, 2)
            rank_mm(3, 3)
            slots_mm(1, 1)
            rest_mm(3, 3)
            rank_mm(4, 0)
            slots_mm(2, 2)
            with pe.Fori(1, NT // CB - 1) as i:
                for c in range(CB):
                    rest_mm(CB * i + c, c)
                    rank_mm(CB * i + (c + 1), (c + 1) % CB)
                    slots_mm(CB * i + (c - 1), (c - 1) % CB)
            for j in range(NT - CB, NT):
                rest_mm(j, j % CB)
                if j + 1 < NT:
                    rank_mm(j + 1, (j + 1) % CB)
                slots_mm(j - 1, (j - 1) % CB)
            slots_mm(NT - 1, (NT - 1) % CB)
            pe.wait_ge(bad_rdy, 1)
            mm(bank(0)[:, 0:1], ones[:], badsum[:, 0:1], start=True, stop=True).then_inc(bad_ps, 1)
            pe.wait_ge(flagged, 1)
            general = pe.value_load(flag[0:1, 0:1], min_val=0, max_val=1)
            with pe.If(general > 0):
                def count_mm(j, first):
                    pe.wait_ge(g_ohr, j + 1)
                    mm(bank(1)[:, 0:NT], g_loh[:, 0, :], g_oh[:, 0, :], start=first, stop=True, skip_group_check=True)
                    mm(bank(2)[:, 0:NT], g_loh[:, 1, :], g_oh[:, 1, :], start=first, stop=True, skip_group_check=True).then_inc(g_cnt, 1)
                count_mm(0, True)
                with pe.Fori(1, NC) as k:
                    count_mm(k, False)
            pe.wait_ge(stat_rdy, 1)
            NB4 = -(-NT // P)
            for k, t in enumerate((rc, some)):
                for b in range(NB4):
                    n = min(P, NT - b * P)
                    last = nc.tensor.transpose(psum[0:n, 2048 + 512 * k + P * b:2048 + 512 * k + P * (b + 1)], t[:, b * P:b * P + n], ident[:])
            last.then_inc(statT_ps, 1)

            with pe.If(general > 0):
                with pe.Fori(0, NC) as k:
                    pe.wait_ge(g_dif, 4 * k + 1)
                    nc.tensor.transpose(bank(0)[:, 0:P], e_keyb[:], ident[:]).then_inc(g_pe, 1)
                    pe.wait_ge(g_dif, 4 * k + 2)
                    nc.tensor.transpose(bank(1)[:, 0:P], e_diff[:], ident[:]).then_inc(g_pe, 1)
                    pe.wait_ge(g_dif, 4 * k + 3)
                    mm(bank(2)[:, 0:D], e_diffT[:], wnT[:], start=True, stop=True).then_inc(g_pe, 1)
                    pe.wait_ge(g_dif, 4 * k + 4)
                    mm(bank(3)[:, 0:2 * D], e_same[:], e_pay[:], start=True, stop=True).then_inc(g_pe, 1)
                pe.wait_ge(g_idx, 2 * NC)

            pe.wait_ge(bload, 16 * 3)
            pe.wait_ge(statT_sb, 1)

            def landed(g, s, per, half):
                if isinstance(g, int):
                    return per * ((g - s) // 2 + 1) + (per * (LAST_PARTS - 1) if g == NG - 1 and per == 16 else 0)
                return half * per

            def transposes(g, s, half):
                pe.wait_ge(xl[s], landed(g, s, 16, half))
                pe.wait_ge(oh_rdy, g + 1)
                if not (isinstance(g, int) and g == 0):
                    pe.wait_ge(xT_sb, g)
                    pe.wait_ge(ohT_sb, g)
                for t in range(TG):
                    nc.tensor.transpose(bank(0)[:, t * P:(t + 1) * P], xg[:, s, t, :], ident[:])
                for t in range(TG):
                    last = nc.tensor.transpose(bank(1)[:, t * P:(t + 1) * P], oh[:, s, t, :], ident[:])
                last.then_inc(trans, 1)

            def differences(g, s, half):
                pe.wait_ge(ohT_sb, g + 1)
                pe.wait_ge(gat[s], landed(g, s, 16 * TG, half))
                if not (isinstance(g, int) and g == 0):
                    pe.wait_ge(dT_sb, g)
                for t in range(TG):
                    o = bank(2)[:, t * P:(t + 1) * P]
                    mm(o, xg[:, s, t, :], ohT[:, t, :], start=True, stop=False)
                    last = mm(o, gx[:, s, t, 0:D], neg_ident[:], start=False, stop=True)
                last.then_inc(dT_ps, 1)

            def edge_products(g, s):
                pe.wait_ge(dT_sb, g + 1)
                if not (isinstance(g, int) and g == 0):
                    pe.wait_ge(hd_sb, g)
                for t in range(TG):
                    last = mm(bank(3)[:, t * P:(t + 1) * P], dT[:, t, :], wnT[:], start=True, stop=True)
                last.then_inc(hd_ps, 1)

            def sums(g, s, add):
                pe.wait_ge(diag0, g + 1)
                if not (isinstance(g, int) and g == 0):
                    pe.wait_ge(s1_sb, g)
                for t in range(TG):
                    o = bank(4)[:, t * P:(t + 1) * P]
                    mm(o, gx[:, s, t, 0:D], oh[:, s, t, :], start=(t == 0), stop=True, skip_group_check=True)
                    mm(o, xg[:, s, t, :], diag[:, s, t, :], start=False, stop=True, skip_group_check=True)
                with pe.If(general > 0):
                    pe.wait_ge(accl, 16 * g + 16)
                    for t in range(TG):
                        mm(bank(4)[:, t * P:(t + 1) * P], accg[:, t, 0:D], ident[:], start=False, stop=True, skip_group_check=True)
                mm(bank(4)[:, 0:1], zcol(), zrow(), start=False, stop=True, skip_group_check=True).then_inc(s1_ps, 1)

            def zcol():
                return zeros[0:1, 0, 0:P]

            def zrow():
                return zeros[0:1, 0, 0:1]

            def abs_sums(g, s):
                pe.wait_ge(hd_sb, g + 1)
                if not (isinstance(g, int) and g == 0):
                    pe.wait_ge(s2_sb, g)
                for t in range(TG):
                    mm(bank(5)[:, t * P:(t + 1) * P], hd[:, t, :], oh[:, s, t, :], start=(t == 0), stop=True,
                       skip_group_check=True)
                with pe.If(general > 0):
                    pe.wait_ge(accl, 16 * g + 16)
                    for t in range(TG):
                        last = mm(bank(5)[:, t * P:(t + 1) * P], accg[:, t, D:2 * D], ident[:], start=False, stop=True,
                                  skip_group_check=True)
                    last.then_inc(acc_rd, 1)
                mm(bank(5)[:, 0:1], zcol(), zrow(), start=False, stop=True, skip_group_check=True).then_inc(s2_ps, 1)

            def z_x(g, s, half):
                pe.wait_ge(xT_sb, g + 1)
                pe.wait_ge(s1_sb, g + 1)
                pe.wait_ge(rl[s], landed(g, s, 16, half) if not (isinstance(g, int) and g == NG - 1) else 16 * (NG // 2))
                if not (isinstance(g, int) and g == 0):
                    pe.wait_ge(z_rd, g)
                for t in range(TG):
                    o = psum[:, 3072 + 256 * t:3072 + 256 * (t + 1)]
                    mm(o, xT[s][:, t, :], wz[:], start=(t % 2 == 0), stop=True, skip_group_check=True)
                    mm(o[:, 0:D], row3[0:3, s, t * P:(t + 1) * P], bias3[0:3, :], start=False, stop=True, skip_group_check=True)
                    mm(o[:, D:2 * D], s1T[:, t, :], wsum[:], start=False, stop=True, skip_group_check=True)

            def z_abs(g, s):
                pe.wait_ge(s2_sb, g + 1)
                for t in range(TG):
                    o = psum[:, 3072 + 256 * t + D:3072 + 256 * (t + 1)]
                    last = mm(o, s2T[:, t, :], wabs[:], start=False, stop=True, skip_group_check=True)
                last.then_inc(z_ps, 1)

            def l0_step(g, s, half, nxt_half, more=True):
                abs_sums(g, s)
                if more:
                    transposes(g + 1, 1 - s, nxt_half)
                z_x(g, s, half)
                if more:
                    differences(g + 1, 1 - s, nxt_half)
                z_abs(g, s)
                if more:
                    edge_products(g + 1, 1 - s)
                    sums(g + 1, 1 - s, None)

            transposes(0, 0, None)
            differences(0, 0, None)
            edge_products(0, 0)
            sums(0, 0, None)
            l0_step(0, 0, None, None)
            l0_step(1, 1, None, None)
            with pe.Fori(1, NG // 2 - 1) as i:
                l0_step(2 * i, 0, i + 1, i + 1)
                l0_step(2 * i + 1, 1, i + 1, i + 2)
            l0_step(NG - 2, 0, None, None)
            l0_step(NG - 1, 1, None, None, more=False)

            with pe.If(general > 0):
                pe.wait_ge(z_rd, NG)
                with pe.Fori(0, NC) as k:
                    pe.wait_ge(g_dif, 2 * k + (4 * NC + 1))
                    nc.tensor.transpose(bank(0)[:, 0:P], e_keyb[:], ident[:]).then_inc(g_pe, 1)
                    pe.wait_ge(g_dif, 2 * k + (4 * NC + 2))
                    mm(bank(3)[:, 0:W], e_same[:], e_pay[:, 0:W], start=True, stop=True).then_inc(g_pe, 1)
                pe.wait_ge(g_idx, 4 * NC)

            def l1_sums(g, s):
                first = isinstance(g, int) and g == 0
                pe.wait_ge(oh1, g + 1)
                pe.wait_ge(diag_rdy, g + 1)
                if not first:
                    pe.wait_ge(yT_sb, g)
                    pe.wait_ge(gam_rd, g)
                for t in range(TG):
                    o = bank(0)[:, t * P:(t + 1) * P]
                    mm(o, gx[:, s, t, 0:D], oh[:, s, t, :], start=(t == 0), stop=True, skip_group_check=True)
                    mm(o, h1g[:, s, t, 0:D], diag[:, s, t, :], start=False, stop=True, skip_group_check=True)
                    mm(bank(3)[:, t:t + 1], oh[:, s, t, :], ones[:, 0:1], start=(t == 0), stop=True, skip_group_check=True)
                with pe.If(general > 0):
                    pe.wait_ge(accl, 16 * g + (16 * NG + 16))
                    for t in range(TG):
                        mm(bank(0)[:, t * P:(t + 1) * P], accg[:, t, 0:D], ident[:], start=False, stop=True, skip_group_check=True)
                        last = mm(bank(3)[:, t:t + 1], ident[:], accg[:, t, D:W], start=False, stop=True, skip_group_check=True)
                    last.then_inc(acc_rd, 1)
                mm(bank(0)[:, 0:1], zcol(), zrow(), start=False, stop=True, skip_group_check=True).then_inc(yT_ps, 1)

            def l1_transposes(g, s, half):
                first = isinstance(g, int) and g == 0
                pe.wait_ge(hl[s], landed(g, s, 16, half))
                if not first:
                    pe.wait_ge(hT_sb, g)
                for t in range(TG):
                    last = nc.tensor.transpose(bank(1)[:, t * P:(t + 1) * P], h1g[:, s, t, 0:D], ident[:])
                last.then_inc(hT_ps, 1)

            def l1_g(g, s):
                pe.wait_ge(yT_sb, g + 1)
                if not (isinstance(g, int) and g == 0):
                    pe.wait_ge(g_sb, g)
                for t in range(TG):
                    last = mm(psum[:, 2048 + 256 * t:2048 + 256 * (t + 1)], yT(t), wg[:], start=(t % 2 == 0), stop=True, skip_group_check=True)
                last.then_inc(g_ps, 1)

            def yT(t):
                return s1T[:, t, :]

            def l1_x(g, b, used, done):
                k = b - 6
                if not (isinstance(g, int) and g == 0):
                    pe.wait_ge(used, g)
                mm(bank(b), ones_row[0:1, :], bx[0:1, k * D:(k + 1) * D].unsqueeze(1).broadcast_to([1, TG, D]),
                   start=True, stop=True, skip_group_check=True)
                for t in range(TG):
                    last = mm(bank(b)[:, t * P:(t + 1) * P], xT[0][:, t, :], wx[:, k * D:(k + 1) * D],
                              start=False, stop=True, skip_group_check=True)
                last.then_inc(done, 1)

            def l1_step(g, s, half):
                l1_transposes(g, s, half)
                l1_sums(g, s)
                pe.wait_ge(hT_sb, g + 1)
                l1_x(g, 7, ay2_rdy, xi_ps)
                l1_x(g, 6, x_rd, xh_ps)
                l1_g(g, s)

            l1_step(0, 0, None)
            l1_step(1, 1, None)
            with pe.Fori(1, NG // 2 - 1) as i:
                l1_step(2 * i, 0, i + 1)
                l1_step(2 * i + 1, 1, i + 1)
            l1_step(NG - 2, 0, None)
            l1_step(NG - 1, 1, None)

        @block.scalar
        def _(act):
            a = nc.scalar
            for b in range(NB):
                n = min(P, NCP - b * P)
                act.wait_ge(placed, min((b + 1) * P, NCP) // CB)
                if b:
                    act.wait_ge(fieldT, b)
                a.copy(fields[:, :, 0:n], psum[:, 0:1024].rearrange("p (f k) -> p f k", f=8)[:, :, 0:n]).then_inc(block_rd, 1)
            act.wait_ge(tab1, 1)

            def sort_stage(i, s, first=False):
                if not first:
                    act.wait_ge(s_done, CB * i - CB)
                a.copy(sort_s[:, s], sort_f[:, bass.ds(i * CB, CB), :]).then_inc(s_staged, 1)

            def sort_values(i, s):
                act.wait_ge(s_staged, i + 1)
                for c in range(CB):
                    if not (isinstance(i, int) and i == 0):
                        act.wait_ge(s_done, CB * i + (c + 1 - CB))
                    act.wait_ge(s_roh, CB * i + (c + 1))
                    a.activation(hi_oh[:, c, :], rank_oh[:, c, :], ACT.Copy, scale=sort_s[:, s, c, 2:3])
                    a.activation(lo_oh[:, c, :], rank_oh[:, c, :], ACT.Copy, scale=sort_s[:, s, c, 3:4]).then_inc(s_val, 1)

            sort_stage(0, 0, True)
            sort_stage(1, 1, True)
            sort_values(0, 0)
            sort_stage(2, 0)
            sort_values(1, 1)
            sort_stage(3, 1)
            with act.Fori(1, NT // CB // 2 - 1) as i:
                for s in range(2):
                    sort_values(2 * i + s, s)
                    sort_stage(2 * i + (2 + s), s)
            for i in (NT // CB - 2, NT // CB - 1):
                sort_values(i, i % 2)

            def copy4(dst, b, func=ACT.Copy):
                return a.activation(dst, bank(b).rearrange("p (t n) -> p t n", t=TG), func)

            def l0_front(g, s):
                act.wait_ge(trans, g + 1)
                if not (isinstance(g, int) and g == 0):
                    act.wait_ge(dT_ps, g)
                copy4(ohT[:], 1).then_inc(ohT_sb, 1)
                if not (isinstance(g, int) and g < 2):
                    act.wait_ge(z_ps, g - 1)
                copy4(xT[s], 0).then_inc(xT_sb, 1)

            def l0_sum_copy(g):
                act.wait_ge(s1_ps, g + 1)
                if not (isinstance(g, int) and g == 0):
                    act.wait_ge(z_ps, g)
                copy4(s1T[:], 4).then_inc(s1_sb, 1)

            def l0_mid(g):
                act.wait_ge(dT_ps, g + 1)
                if not (isinstance(g, int) and g == 0):
                    act.wait_ge(hd_ps, g)
                copy4(dT[:], 2).then_inc(dT_sb, 1)

            def l0_abs(g):
                act.wait_ge(hd_ps, g + 1)
                if not (isinstance(g, int) and g == 0):
                    act.wait_ge(s2_ps, g)
                copy4(hd[:], 3, ACT.Abs).then_inc(hd_sb, 1)

            def l0_p2(g):
                act.wait_ge(z_ps, g + 1)
                if not (isinstance(g, int) and g == 0):
                    act.wait_ge(z_rd, g)
                for t in range(TG):
                    last = a.activation(p2[:, t, :], psum[:, 3072 + 256 * t + D:3072 + 256 * (t + 1)], ACT.Copy,
                                        scale=rc[:, bass.ds(TG * g + t, 1)])
                last.then_inc(p2_sb, 1)

            def l0_diag(g, s, first):
                if not first:
                    act.wait_ge(s1_ps, g - 1)
                for t in range(TG):
                    last = a.activation(diag[:, s, t, :], ident[:], ACT.Copy, scale=n_self[:, bass.ds(TG * g + t, 1)])
                last.then_inc(diag0, 1)

            def l0_step(g, s, more=2):
                if more > 0:
                    l0_front(g + 1, 1 - s)
                    l0_mid(g + 1)
                l0_p2(g)
                if more > 0:
                    l0_abs(g + 1)
                    l0_sum_copy(g + 1)
                if more > 1:
                    l0_diag(g + 2, s, False)

            act.wait_ge(n_self_rdy, 1)
            l0_diag(0, 0, True)
            l0_front(0, 0)
            l0_mid(0)
            l0_abs(0)
            l0_sum_copy(0)
            l0_diag(1, 1, True)
            l0_step(0, 0)
            l0_step(1, 1)
            with act.Fori(1, NG // 2 - 1) as i:
                for s in range(2):
                    l0_step(2 * i + s, s)
            l0_step(NG - 2, 0, 1)
            l0_step(NG - 1, 1, 0)

            def l1_diag(g, s):
                if not (isinstance(g, int) and g < 2):
                    act.wait_ge(yT_ps, g - 1)
                for t in range(TG):
                    last = a.activation(diag[:, s, t, :], ident[:], ACT.Copy, scale=self_w[:, bass.ds(TG * g + t, 1)])
                last.then_inc(diag_rdy, 1)

            def l1_copyh(g):
                first = isinstance(g, int) and g == 0
                act.wait_ge(hT_ps, g + 1)
                if not first:
                    act.wait_ge(xh_ps, g)
                copy4(xT[0], 1).then_inc(hT_sb, 1)

            def l1_copyy(g):
                first = isinstance(g, int) and g == 0
                act.wait_ge(yT_ps, g + 1)
                if not first:
                    act.wait_ge(g_ps, g)
                copy4(s1T[:], 0).then_inc(yT_sb, 1)

            def l1_scale(g):
                act.wait_ge(g_ps, g + 1)
                if not (isinstance(g, int) and g == 0):
                    act.wait_ge(q_rdy, g)
                for t in range(TG):
                    last = a.activation(gs[:, t, :], psum[:, 2048 + 256 * t:2048 + 256 * (t + 1)], ACT.Copy,
                                        scale=dinv[:, bass.ds(TG * g + t, 1)])
                last.then_inc(g_sb, 1)

            def gate(k):
                return a.activation(gates[:, k, :], dots[:, k, :], ACT.Sigmoid, bias=vec[:, 5 * D + k:5 * D + k + 1])

            def l1_own_gate(g):
                act.wait_ge(dots2_rdy, g + 1)
                gate(2).then_inc(gate2_rdy, 1)
                act.wait_ge(gate2_rdy, g + 1)
                if not (isinstance(g, int) and g == 0):
                    act.wait_ge(own_rdy, g)
                for t in range(TG):
                    last = a.activation(ay[:, 2, t, :], bank(7)[:, t * P:(t + 1) * P], ACT.Relu,
                                        scale=gates[:, 2, t:t + 1])
                last.then_inc(ay2_rdy, 1)

            def l1_gates(g, s):
                act.wait_ge(dots_rdy, g + 1)
                gate(0)
                gate(1).then_inc(gate_rdy, 1)
                act.wait_ge(gate_rdy, g + 1)
                if not (isinstance(g, int) and g == 0):
                    act.wait_ge(nb_rdy, g)
                for k in range(2):
                    for t in range(TG):
                        last = a.activation(ay[:, k, t, :], q[:, s, t, k * D:(k + 1) * D], ACT.Relu, scale=gates[:, k, t:t + 1])
                last.then_inc(ay_rdy, 1)

            def l1_step(g, s, more=2):
                l1_scale(g)
                if more > 0:
                    l1_copyh(g + 1)
                l1_own_gate(g)
                if more > 0:
                    l1_copyy(g + 1)
                if more > 1:
                    l1_diag(g + 2, s)
                l1_gates(g, s)

            l1_diag(0, 0)
            l1_diag(1, 1)
            l1_copyh(0)
            l1_copyy(0)
            l1_step(0, 0)
            l1_step(1, 1)
            with act.Fori(1, NG // 2 - 1) as i:
                for s in range(2):
                    l1_step(2 * i + s, s)
            l1_step(NG - 2, 0, 1)
            l1_step(NG - 1, 1, 0)


_INS = ['x', 'src', 'dst', 'L0_gnn_W_neigh', 'L0_gnn_b_neigh', 'L0_gnn_W_edge', 'L0_gnn_b_edge', 'L0_gnn_W_lin',
        'L0_gnn_b_lin', 'L1_gnn_W_hp', 'L1_gnn_b_hp', 'L1_gnn_W_lp', 'L1_gnn_b_lp', 'L1_gnn_W_i', 'L1_gnn_b_i',
        'L1_gnn_wlin_h', 'L1_gnn_blin_h', 'L1_gnn_wlin_l', 'L1_gnn_blin_l', 'L1_gnn_wlin_i', 'L1_gnn_blin_i']


def kernel(**inputs):
    import numpy as np
    import concourse.bacc as bacc
    from concourse import mybir
    from concourse.bass_utils import run_bass_kernel_spmd

    nc = bacc.Bacc("TRN2", target_bir_lowering=False, num_devices=1)
    arrays, args = {}, []
    for name in _INS:
        a = np.ascontiguousarray(inputs[name])
        a = a.reshape(a.shape if a.ndim else (1,))
        arrays[f"in_{name}"] = a
        args.append(nc.dram_tensor(f"in_{name}", a.shape, mybir.dt.from_np(a.dtype), kind="ExternalInput").ap())
    out = nc.dram_tensor("out", inputs["x"].shape, mybir.dt.float32, kind="ExternalOutput").ap()
    build(nc, *args, out)
    r = run_bass_kernel_spmd(nc, [arrays], core_ids=[0])
    return r.results[0]["out"]
```

```python
def build(nc, x_d, src_d, dst_d, wn_d, bn_d, we_d, be_d, wl_d, bl_d,
          whp_d, bhp_d, wlp_d, blp_d, wi_d, bi_d, wvh_d, bvh_d, wvl_d, bvl_d, wvi_d, bvi_d, out_d):
    from contextlib import ExitStack
    import concourse.bass as bass
    from concourse import mybir

    f32, f16, bf16, i32 = mybir.dt.float32, mybir.dt.float16, mybir.dt.bfloat16, mybir.dt.int32
    ALU, ACT, AX = mybir.AluOpType, mybir.ActivationFunctionType, mybir.AxisListType
    P = 128
    N, D = x_d.shape
    E = src_d.shape[0]
    TG = 4
    NG = -(-N // (P * TG))
    NT = NG * TG
    NPAD = NT * P
    CB = 4
    NC = -(-E // P)
    NCP = -(-NC // CB) * CB
    NB = -(-NC // P)
    W = D + 1
    OOB = 60000
    HALF = 2048
    EPS = 1e-5
    BP = 3
    NR = BP * (BP + 1)
    assert NPAD + P > N and OOB > N and N * P < 2 ** 24

    h1_d = nc.dram_tensor("h1_scratch", (N, W), f32).ap()
    rows_d = nc.dram_tensor("rows_scratch", (NR, NPAD), bf16).ap()
    acc0_d = nc.dram_tensor("acc0_scratch", (NPAD + P, 2 * D), f32).ap()
    acc1_d = nc.dram_tensor("acc1_scratch", (NPAD + P, W), f32).ap()

    ctx = ExitStack()
    with ctx:
        def sb(name, shape, dt=f32):
            return ctx.enter_context(nc.sbuf_tensor(name, shape, dt))

        def sem(name):
            return ctx.enter_context(nc.semaphore(name))

        psum = ctx.enter_context(nc.psum_tensor("psum", [P, 8 * 512], f32))

        def bank(b, n=1):
            return psum[:, 512 * b:512 * (b + n)]

        ident = sb("ident", [P, P])
        ident16 = sb("ident16", [P, P], f16)
        iota_i = sb("iota_i", [P, NCP], i32)
        iota = sb("iota", [P, P])
        iota_t = sb("iota_t", [P, NT], f16)
        part = sb("part", [P, 1])
        before = sb("before", [P, P])
        before16 = sb("before16", [P, P], f16)
        notbefore16 = sb("notbefore16", [P, P], f16)
        all16 = sb("all16", [P, P], f16)
        after = sb("after", [P, P])
        row0 = sb("row0", [P, P])
        ones = sb("ones", [P, P])
        minus_half = sb("minus_half", [P, TG])
        zeros = sb("zeros", [P, 2 * D])

        wn = sb("wn", [P, D])
        we = sb("we", [P, 2 * D])
        wl = sb("wl", [P, 2 * D])
        w1 = sb("w1", [P, 3, D])
        wnT = sb("wnT", [P, D])
        wl2T = sb("wl2T", [P, D])
        wz = sb("wz", [P, 2 * D])
        wmid = sb("wmid", [P, D])
        wsum = sb("wsum", [P, D])
        wabs = sb("wabs", [P, D])
        wx = sb("wx", [P, 2 * D])
        wg = sb("wg", [P, 2 * D])
        bcol = sb("bcol", [P, 2])
        bias0 = sb("bias0", [NR + BP, D], bf16)
        bias1 = sb("bias1", [BP, 2 * D], bf16)
        brow = sb("brow", [1, 5 * D])
        bparts = sb("bparts", [1, BP, 5 * D], bf16)
        ones16 = sb("ones16", [BP, P], bf16)
        vec_row = sb("vec_row", [1, 5 * D + 3])
        vec = sb("vec", [P, 5 * D + 3])
        ones_row = sb("ones_row", [1, P])

        sort_area = sb("sort_area", [P, 13 * NCP])

        s_raw = sb("s_raw", [P, NB, P], i32)
        d_raw = sb("d_raw", [P, NB, P], i32)
        nat_area = sb("nat_area", [P, 2 * NB * P])
        s_nat = nat_area[:, 0:NB * P].rearrange("p (b n) -> p b n", b=NB)
        d_nat = nat_area[:, NB * P:2 * NB * P].rearrange("p (b n) -> p b n", b=NB)
        t0_raw = sb("t0_raw", [P, NB], i32)
        t0_col = sb("t0_col", [P, 2, NB])
        s_i = sb("s_i", [P, NCP], i32)
        d_i = sb("d_i", [P, NCP], i32)
        tmp_i = sb("tmp_i", [P, NCP], i32)
        tmp2_i = sb("tmp2_i", [P, NCP], i32)
        td = sb("td", [P, NCP])
        ld = sb("ld", [P, NCP])
        hi = sort_area[:, 0 * NCP:1 * NCP]
        lo = sort_area[:, 1 * NCP:2 * NCP]
        valid = sb("valid", [P, NCP])
        selfe = sort_area[:, 2 * NCP:3 * NCP]
        other = sort_area[:, 3 * NCP:4 * NCP]
        in0 = sb("in0", [P, NCP])
        in1 = sb("in1", [P, NCP])
        t0 = sort_area[:, 4 * NCP:5 * NCP]
        cols = sort_area[:, 5 * NCP:6 * NCP]
        n_first = sort_area[:, 6 * NCP:7 * NCP]
        o_first = sort_area[:, 7 * NCP:8 * NCP]
        pre = sort_area[:, 8 * NCP:9 * NCP]
        nxt = sort_area[:, 9 * NCP:10 * NCP]
        start = sort_area[:, 10 * NCP:11 * NCP]
        rank = sort_area[:, 11 * NCP:12 * NCP]
        ta = sb("ta", [P, NCP])
        tb = sb("tb", [P, NCP])
        bad = sort_area[:, 12 * NCP:13 * NCP]
        chunk_v = sb("chunk_v", [P, NCP, 2, 4], f16)
        place_v = chunk_v[:, :, 0, :]
        count_v = chunk_v[:, :, 1, :]
        step_v = sb("step_v", [P, 2, CB, 2, 4], f16)
        place_oh = sb("place_oh", [P, 2, CB, P], f16)
        local_oh = sb("local_oh", [P, 2, CB, P], f16)
        fields = sb("fields", [P, 8, P], f16)
        fieldsT = sb("fieldsT", [P, 8, P], f16)
        fold = sb("fold", [P, 2, NT], f16)

        slot_hi = sb("slot_hi", [P, NT])
        slot_lo = sb("slot_lo", [P, NT])
        slot_i = sb("slot_i", [P, NT], i32)
        slot_j = sb("slot_j", [P, NT], i32)
        slot_k = sb("slot_k", [P, NT], i32)
        slot_f = sb("slot_f", [P, NT])
        occ = sb("occ", [P, NT])
        idx0 = sb("idx0", [P, NT], i32)
        loc0 = sb("loc0", [P, NT])
        idx1 = sb("idx1", [P, NT], i32)
        loc1 = sb("loc1", [P, NT])
        n_self = sb("n_self", [P, NT])
        n_in = sb("n_in", [P, NT])
        n_out = sb("n_out", [P, NT])
        dinv = sb("dinv", [P, NT])
        self_w = sb("self_w", [P, NT])
        rc = sb("rc", [P, NT])
        some = sb("some", [P, NT])
        statT = sb("statT", [P, BP + 1, -(-NT // P), P], bf16)
        sort_f = sb("sort_f", [P, NT, 4])
        sort_s = sb("sort_s", [P, 2, CB, 4])
        tile_lo = sb("tile_oh", [P, CB, NT], f16)
        src_oh = sb("src_oh", [P, CB, P], f16)
        rank_oh = sb("rank_oh", [P, CB, P], f16)
        hi_oh = sb("hi_oh", [P, CB, P], f16)
        lo_oh = sb("lo_oh", [P, CB, P], f16)
        junk = sb("junk", [P, 2, NT], f16)
        rank0 = sb("rank0", [P, NT])
        rank_s = sb("rank_s", [P, 2, CB])
        spare = sb("spare", [P, 5])
        badsum = sb("badsum", [P, 2])
        okv = sb("okv", [P, 1])
        flag = sb("flag", [P, 1], i32)

        xg = sb("xg", [P, 2, TG, D])
        gx = sb("gx", [P, 2, TG, W])
        gidx = sb("gidx", [P, 2, TG], i32)
        oh = sb("oh", [P, 2, TG, P])
        tile_hi = oh[:].rearrange("p s t n -> p (s t n)")[:, 0:CB * NT // 2].bitcast(f16).rearrange("p (c n) -> p c n", c=CB)
        ohT = sb("ohT", [P, TG, P])
        xT = [sb("xT", [P, TG, P])[:], sort_area[:, 3072:3584].rearrange("p (t n) -> p t n", t=TG)]
        dT = sb("dT", [P, TG, P])
        hd = sb("hd", [P, TG, P])
        s1T = sb("s1T", [P, TG, P])
        s2T = sb("s2T", [P, TG, P])
        row0s = sb("row0s", [NR + BP, 2, TG * P], bf16)
        p2 = sb("p2", [P, TG, D])
        res = sb("res", [P, TG, D])
        stats = sb("stats", [P, TG, 6])
        mv = sb("mv", [P, TG, 2])
        vare = sb("vare", [P, TG])
        rstd = sb("rstd", [P, TG])
        h1g = sb("h1g", [P, 2, TG, W])
        accg = sb("accg", [P, TG, 2 * D])
        diag = sort_area[:, 0:1024].rearrange("p (s t n) -> p s t n", s=2, t=TG)
        gam = sb("gam", [P, TG])
        gs = sort_area[:, 1024:2048].rearrange("p (t n) -> p t n", t=TG)
        q = sort_area[:, 2048:4096].rearrange("p (s t n) -> p s t n", s=2, t=TG)
        ay = sort_area[:, 4096:5632].rearrange("p (k t n) -> p k t n", t=TG, k=3)
        outg = sort_area[:, 5632:6656].rearrange("p (s t n) -> p s t n", s=2, t=TG)
        dot_junk = nat_area[:, 0:3 * TG * D // 2].bitcast(f16).rearrange("p (k t n) -> p k t n", k=3, t=TG)
        own_sum = xg
        total = (dT, hd)
        dots = sb("dots", [P, 3, TG])
        gates = sb("gates", [P, 3, TG])

        e_idx = sb("e_idx", [P, 2], i32)
        e_key = sb("e_key", [P, 1])
        e_rows = sb("e_rows", [P, 2, W])
        e_diff = sb("e_diff", [P, D])
        e_diffT = sb("e_diffT", [P, D])
        e_pay = sb("e_pay", [P, 2 * D])
        e_keyb = sb("e_keyb", [P, P])
        e_same = sb("e_same", [P, P])
        e_junk = sb("e_junk", [P, P])
        e_prev = sb("e_prev", [P, 1])
        e_lead = sb("e_lead", [P, 1])
        e_tgt = sb("e_tgt", [P, 1])
        e_tgti = sb("e_tgti", [P, 1], i32)
        e_sum = sb("e_sum", [P, 2 * D])
        g_oh = tile_lo[:, 0:2]
        g_loh = rank_oh[:, 0:2]

        wload = sem("weights_loaded")
        bload = sem("bias_parts_loaded")
        bsplit = sem("biases_split")
        eload = sem("edges_loaded")
        iotas = sem("iotas_ready")
        consts = sem("constants_ready")
        vchain = sem("vector_steps")
        pchain = sem("pool_steps")
        zeroed = sem("buffers_zeroed")
        wT_ps = sem("weights_transposed")
        wT_sb = sem("weights_copied")
        nat = sem("edges_as_float")
        edgeT = sem("edges_transposed")
        t_ready = sem("dst_tiles_ready")
        t0_ps = sem("first_tiles_summed")
        masks = sem("masks_ready")
        sums_ps = sem("chunk_sums_ready")
        pre_rd = sem("chunk_sums_read")
        lower_ps = sem("ranks_in_chunk_ready")
        place = sem("place_onehots_ready")
        placed = sem("chunks_placed")
        p_staged = sem("place_values_staged")
        p_copied = sem("placed_fields_copied")
        fieldT = sem("block_fields_transposed")
        fieldT_sb = sem("block_transposes_copied")
        fold_rdy = sem("fold_onehots_ready")
        folded = sem("blocks_folded")
        tab1 = sem("table1_ready")
        s_staged = sem("sort_columns_staged")
        s_oh = sem("sort_tile_onehots")
        s_src = sem("sort_src_onehots")
        s_rankps = sem("sort_ranks_in_psum")
        s_rank = sem("sort_ranks_read")
        s_kept = sem("sort_ranks_kept")
        s_roh = sem("sort_rank_onehots")
        s_val = sem("sort_value_onehots")
        s_done = sem("sort_columns_done")
        bad_rdy = sem("bad_sums_ready")
        bad_ps = sem("bad_total_ready")
        flagged = sem("flag_ready")
        stat_rdy = sem("stats_ready")
        dinv_rdy = sem("dinv_ready")
        statT_ps = sem("stats_transposed")
        statT_sb = sem("stats_transposed_copied")
        rows_st = sem("stat_rows_stored")

        xl = [sem(f"x_loaded{s}") for s in range(2)]
        rl = [sem(f"rows_loaded{s}") for s in range(2)]
        gidx_rdy = sem("gather_indices_ready")
        gat = [sem(f"rows_gathered{s}") for s in range(2)]
        oh_rdy = sem("onehots_ready")
        trans = sem("l0_transposed")
        diag0 = sem("l0_diagonals_ready")
        n_self_rdy = sem("self_counts_ready")
        xT_sb = sem("l0_xT_copied")
        ohT_sb = sem("l0_onehotT_copied")
        gxT_sb = sem("l0_gathered_rows_copied")
        dT_ps = sem("l0_differences_ready")
        dT_sb = sem("l0_differences_copied")
        hd_ps = sem("l0_edge_products_ready")
        hd_sb = sem("l0_edge_abs_ready")
        s1_ps = sem("l0_sums_ready")
        s1_sb = sem("l0_sums_copied")
        s2_ps = sem("l0_abs_sums_ready")
        s2_sb = sem("l0_abs_sums_copied")
        z_ps = sem("l0_z_ready")
        p2_sb = sem("l0_p2_scaled")
        z_rd = sem("l0_z_read")
        stats0 = sem("l0_stats_ready")
        var0 = sem("l0_var_ready")
        rstd0 = sem("l0_rstd_ready")
        h1_rdy = sem("l0_rows_ready")
        h1_st = [sem(f"l0_rows_stored{s}") for s in range(2)]

        hl = [sem(f"l1_rows_loaded{s}") for s in range(2)]
        gat1 = [sem(f"l1_rows_gathered{s}") for s in range(2)]
        gidx1 = sem("l1_gather_indices_ready")
        oh1 = sem("l1_onehots_ready")
        diag_rdy = sem("l1_diagonals_ready")
        yT_ps = sem("l1_yT_ready")
        yT_sb = sem("l1_yT_copied")
        hT_ps = sem("l1_hT_ready")
        hT_sb = sem("l1_hT_copied")
        g_ps = sem("l1_g_ready")
        g_sb = sem("l1_g_scaled")
        x_rd = sem("l1_x_read")
        gam_rd = sem("l1_gamma_read")
        xi_ps = sem("l1_own_products_ready")
        xh_ps = sem("l1_high_products_ready")
        gam_sum = sem("l1_gamma_summed")
        q_rdy = sem("l1_neighbour_parts_ready")
        dots2_rdy = sem("l1_own_dots_ready")
        gate2_rdy = sem("l1_own_gates_ready")
        ay2_rdy = sem("l1_own_gated_ready")
        dots_rdy = sem("l1_dots_ready")
        gate_rdy = sem("l1_gates_ready")
        ay_rdy = sem("l1_gated_ready")
        own_rdy = sem("l1_own_sums_ready")
        nb_rdy = sem("l1_neighbour_sums_ready")
        res_rdy = sem("l1_residuals_ready")
        stats1 = sem("l1_stats_ready")
        var1 = sem("l1_var_ready")
        rstd1 = sem("l1_rstd_ready")
        out_rdy = sem("l1_out_ready")
        out_st = [sem(f"l1_out_stored{s}") for s in range(2)]

        accz = sem("gen_accumulators_zeroed")
        accl = sem("gen_accumulators_loaded")
        acc_rd = sem("gen_accumulators_read")
        g_chain = sem("gen_vector_steps")
        g_ohr = sem("gen_onehots_ready")
        g_cnt = sem("gen_counted")
        g_take = sem("gen_waits_taken")
        g_idx = sem("gen_indices_ready")
        g_gat = sem("gen_rows_gathered")
        g_dif = sem("gen_differences_ready")
        g_pe = sem("gen_products_ready")
        g_v = sem("gen_vector_ready")
        g_sct = sem("gen_rows_added")
        gen_deg = sem("gen_degrees_ready")

        block = ctx.enter_context(nc.Block())

        def tile_oh(k):
            return tile_lo[:, k, :] if k < CB else tile_hi[:, k - CB, :]

        class Steps:

            def __init__(self, eng, s):
                self.eng, self.s, self.n = eng, s, 0

            def mark(self, ins):
                self.n += 1
                ins.then_inc(self.s, 1)

            def link(self, ins):
                self.mark(ins)
                self.eng.wait_ge(self.s, self.n)

        LAST = N - (NG - 1) * P * TG
        LT, LR = LAST // P, LAST % P

        def group_parts(dram, g, tile):
            if not isinstance(g, int) or g < NG - 1:
                return [(dram[bass.ds(g * (P * TG), P * TG), :].rearrange("(t p) d -> p t d", p=P), tile[:, 0:TG, :])]
            at = (NG - 1) * P * TG
            return [(dram[at:at + LT * P, :].rearrange("(t p) d -> p t d", p=P), tile[:, 0:LT, :]),
                    (dram[at + LT * P:N, :], tile[0:LR, LT, :])]

        LAST_PARTS = 2

        @block.sync
        def _(sp):
            for t, d in ((wn, wn_d), (we, we_d), (wl, wl_d), (w1[:, 0, :], whp_d), (w1[:, 1, :], wlp_d), (w1[:, 2, :], wi_d)):
                sp.dma_start(t[:] if t in (wn, we, wl) else t, d[:, :]).then_inc(wload, 16)
            for k, d in enumerate((bn_d, be_d)):
                sp.dma_start(bcol[:, k:k + 1], d.rearrange("(p o) -> p o", o=1)).then_inc(wload, 16)
            row = lambda d: d.rearrange("(o n) -> o n", o=1)
            for k, d in enumerate((bl_d, bhp_d, bi_d)):
                sp.dma_start(brow[0:1, (2 + k) * D:(3 + k) * D], row(d)).then_inc(wload, 16)
            for k, d in enumerate((bhp_d, blp_d, wvh_d, wvl_d, wvi_d)):
                sp.dma_start(vec_row[0:1, k * D:(k + 1) * D], row(d)).then_inc(wload, 16)
            for k, d in enumerate((bvh_d, bvl_d, bvi_d)):
                sp.dma_start(vec_row[0:1, 5 * D + k:5 * D + k + 1], row(d)).then_inc(wload, 16)
            sp.wait_ge(zeroed, 2)
            full = NB - 1
            for raw, d in ((s_raw, src_d), (d_raw, dst_d)):
                sp.dma_start(raw[:, 0:full, :], d[0:full * P * P].rearrange("(b k p) -> k b p", k=P, p=P)).then_inc(eload, 16)
                left = (E - full * P * P) // P
                sp.dma_start(raw[0:left, full, :], d[full * P * P:(full * P + left) * P].rearrange("(k p) -> k p", p=P)).then_inc(eload, 16)
                sp.dma_start(raw[left:left + 1, full, 0:E % P], d[E - E % P:E].rearrange("(o p) -> o p", o=1)).then_inc(eload, 16)
            sp.wait_ge(bsplit, 2 * BP - 1)
            for j in range(BP):
                for i in range(BP + 2):
                    at = (BP + 1) * j + i if i < BP + 1 else NR + j
                    col = max(i - BP + 1, 0)
                    sp.dma_start(bias0[at:at + 1, :], bparts[0:1, j, col * D:(col + 1) * D]).then_inc(bload, 16)
                sp.dma_start(bias1[j:j + 1, :], bparts[0:1, j, 3 * D:5 * D]).then_inc(bload, 16)
            sp.wait_ge(flagged, 1)
            general = sp.value_load(flag[0:1, 0:1], min_val=0, max_val=1)
            with sp.If(general > 0):
                for g in range(NG):
                    sp.dma_start(acc0_d[g * 512:(g + 1) * 512, :].rearrange("(t p) d -> p t d", p=P), zeros[:].unsqueeze(1).broadcast_to([P, TG, 2 * D])).then_inc(accz, 16)
                    sp.dma_start(acc1_d[g * 512:(g + 1) * 512, :].rearrange("(t p) d -> p t d", p=P), zeros[:, 0:W].unsqueeze(1).broadcast_to([P, TG, W])).then_inc(accz, 16)
                sp.dma_start(acc0_d[NPAD:NPAD + P, :], zeros[:, :]).then_inc(accz, 16)
                sp.dma_start(acc1_d[NPAD:NPAD + P, :], zeros[:, 0:W]).then_inc(accz, 16)
                sp.wait_ge(accz, 16 * (2 * NG + 2))
            for g in (0, 1):
                for a, b in group_parts(x_d, g, xg[:, g]):
                    sp.dma_start(b, a).then_inc(xl[g], 16)
            sp.wait_ge(statT_sb, 1)
            NB4 = -(-NT // P)
            sp.wait_ge(zeroed, 4)
            for j in range(BP):
                for b in range(NB4):
                    n = min(P, NT - b * P)
                    sp.dma_start(rows_d[(BP + 1) * j:(BP + 1) * (j + 1), b * P * P:(b * P + n) * P].rearrange("i (t p) -> t i p", p=P),
                                 statT[0:n, :, b, :]).then_inc(rows_st, 16)
            with sp.If(general > 0):
                sp.wait_ge(g_sct, 16 * NC)

            sp.wait_ge(rows_st, 16 * BP * NB4)

            def l0_load(g, s):
                sp.wait_ge(s1_ps, g - 1)
                for a, b in group_parts(x_d, g, xg[:, s]):
                    sp.dma_start(b, a).then_inc(xl[s], 16)

            def l0_load_rows(g, s):
                sp.dma_start(row0s[0:NR, s, :], rows_d[:, bass.ds(g * (P * TG), P * TG)]).then_inc(rl[s], 16)

            def acc_load(acc_d, width, g, base):
                with sp.If(general > 0):
                    if not (isinstance(g, int) and g + base == 0):
                        sp.wait_ge(acc_rd, g + base)
                    sp.dma_start(accg[:, :, 0:width],
                                 acc_d[bass.ds(g * (P * TG), P * TG), :].rearrange("(t p) d -> p t d", p=P)).then_inc(accl, 16)

            def l0_store(g, s, z_count=None):
                sp.wait_ge(h1_rdy, g + 1)
                if z_count is not None:
                    sp.wait_ge(z_ps, z_count)
                for a, b in group_parts(h1_d, g, h1g[:, s]):
                    sp.dma_start(a, b).then_inc(h1_st[s], 16)

            for g in (0, 1):
                acc_load(acc0_d, 2 * D, g, 0)
                l0_load_rows(g, g)
            l0_load(2, 0)
            acc_load(acc0_d, 2 * D, 2, 0)
            sp.wait_ge(z_ps, 1)
            l0_load_rows(2, 0)
            with sp.Fori(0, NG // 2 - 2) as i:
                for s in range(2):
                    l0_load(2 * i + (3 + s), 1 - s)
                    acc_load(acc0_d, 2 * D, 2 * i + (3 + s), 0)
                    l0_store(2 * i + s, s, 2 * i + (2 + s))
                    l0_load_rows(2 * i + (3 + s), 1 - s)
            l0_load(NG - 1, 1)
            acc_load(acc0_d, 2 * D, NG - 1, 0)
            l0_store(NG - 4, 0, NG - 2)
            l0_load_rows(NG - 1, 1)
            for g in (NG - 3, NG - 2, NG - 1):
                l0_store(g, g % 2)
            for s in range(2):
                sp.wait_ge(h1_st[s], 16 * (NG // 2 + (LAST_PARTS - 1) * s))
            with sp.If(general > 0):
                sp.wait_ge(g_sct, 16 * 2 * NC)

            def l1_load(g, s, first):
                if not first:
                    sp.wait_ge(own_rdy, g - 1)
                for a, b in group_parts(h1_d, g, h1g[:, s]):
                    sp.dma_start(b, a).then_inc(hl[s], 16)

            def l1_store(g, s):
                sp.wait_ge(out_rdy, g + 1)
                for a, b in group_parts(out_d, g, outg[:, s]):
                    sp.dma_start(a, b).then_inc(out_st[s], 16)

            def l1_step(g, s):
                l1_load(g, s, isinstance(g, int) and g < 2)
                acc_load(acc1_d, W, g, NG)

            for g in range(4):
                l1_step(g, g % 2)
            with sp.Fori(0, NG // 2 - 3) as i:
                for s in range(2):
                    l1_step(2 * i + (4 + s), s)
                    l1_store(2 * i + s, s)
            for g in range(NG - 6, NG):
                if g + 4 < NG:
                    l1_step(g + 4, g % 2)
                l1_store(g, g % 2)
            for s in range(2):
                sp.wait_ge(out_st[s], 16 * (NG // 2 + (LAST_PARTS - 1) * s))

        @block.gpsimd
        def _(pool):
            st = Steps(pool, pchain)
            last_node, last_row = pool.to_reg(N - 1), pool.to_reg(NPAD + P - 1)
            nc.gpsimd.memset(s_raw[:], N - 1).then_inc(zeroed, 1)
            nc.gpsimd.memset(d_raw[:], N - 1).then_inc(zeroed, 1)
            nc.gpsimd.memset(row0s[:], 1.0).then_inc(zeroed, 1)
            nc.gpsimd.memset(ones_row[:], 1.0).then_inc(zeroed, 1)
            nc.gpsimd.iota(iota_i[:], pattern=[[P, NCP]], base=0, channel_multiplier=1).then_inc(iotas, 1)
            nc.gpsimd.iota(tmp_i[:], pattern=[[1, NCP]], base=0, channel_multiplier=0).then_inc(iotas, 1)
            nc.gpsimd.memset(ones[:], 1.0).then_inc(pchain, 1)
            nc.gpsimd.memset(minus_half[:], -0.5)
            nc.gpsimd.memset(ones16[:], 1.0)
            nc.gpsimd.memset(all16[:], 1.0)
            nc.gpsimd.memset(zeros[:], 0.0)
            nc.gpsimd.memset(gx[:], 0.0)
            nc.gpsimd.memset(accg[:], 0.0)
            nc.gpsimd.memset(e_rows[:], 0.0)
            nc.gpsimd.memset(xg[:], 0.0)
            nc.gpsimd.memset(h1g[:], 0.0)
            pool.wait_ge(pchain, 1)
            st.n = 1
            st.mark(nc.gpsimd.affine_select(out=before[:], in_=ones[:], compare_op=ALU.is_gt, fill=0.0, base=0,
                                            pattern=[[1, P]], channel_multiplier=-1))
            st.mark(nc.gpsimd.affine_select(out=after[:], in_=ones[:], compare_op=ALU.is_gt, fill=0.0, base=0,
                                            pattern=[[-1, P]], channel_multiplier=1))
            st.mark(nc.gpsimd.affine_select(out=ident[:], in_=ones[:], compare_op=ALU.is_equal, fill=0.0, base=0,
                                            pattern=[[1, P]], channel_multiplier=-1))
            st.link(nc.gpsimd.affine_select(out=row0[:], in_=ones[:], compare_op=ALU.is_equal, fill=0.0, base=0,
                                            pattern=[[0, P]], channel_multiplier=1))
            nc.gpsimd.tensor_copy(before16[:], before[:]).then_inc(consts, 1)
            nc.gpsimd.tensor_copy(ident16[:], ident[:]).then_inc(consts, 1)
            nc.gpsimd.tensor_scalar(notbefore16[:], before[:], -1.0, 1.0, ALU.mult, ALU.add).then_inc(consts, 1)

            def src_onehots(i, s):
                pool.wait_ge(s_staged, i + 1)
                for c in range(CB):
                    if not (isinstance(i, int) and i == 0):
                        pool.wait_ge(s_done, CB * i + (c + 1 - CB))
                        nc.gpsimd.tensor_tensor(spare[0:1, c:c + 1], ones[0:1, 0:1], ones[0:1, 0:1], ALU.add)
                    nc.gpsimd.tensor_scalar(src_oh[:, c, :], iota[:], sort_s[:, s, c, 1:2], None, ALU.is_equal).then_inc(s_src, 1)
                col = bass.ds(i * CB, CB)
                nc.gpsimd.tensor_tensor(dinv[:, col], dinv[:, col], minus_half[:, 0:CB], ALU.pow).then_inc(dinv_rdy, 1)

            for i in range(2):
                src_onehots(i, i)
            with pool.Fori(1, NT // CB // 2) as i:
                for s in range(2):
                    src_onehots(2 * i + s, s)

            pool.wait_ge(flagged, 1)
            general = pool.value_load(flag[0:1, 0:1], min_val=0, max_val=1)

            with pool.If(general > 0):
                pool.wait_ge(gen_deg, 1)
                nc.gpsimd.tensor_tensor(dinv[:], slot_f[:], slot_hi[:], ALU.pow).then_inc(dinv_rdy, 1)

            def take(idx_count, count):
                if not isinstance(count, int):
                    pool.wait_ge(g_take, count)
                    pool.wait_ge(g_idx, idx_count)
                nc.gpsimd.tensor_tensor(spare[0:1, 2:3], ones[0:1, 0:1], ones[0:1, 0:1], ALU.add).then_inc(g_take, 1)

            def edge_rows(count, rows, width, acc, payload):
                take(count, count)
                for k, (table, col) in enumerate(rows):
                    nc.gpsimd.indirect_dma_start(out=e_rows[:, k, 0:width], out_offset=None, in_=table,
                                                 in_offset=bass.IndirectOffsetOnAxis(ap=e_idx[:, col:col + 1], axis=0),
                                                 bounds_check=last_node, oob_is_err=False).then_inc(g_gat, 16)

            with pool.If(general > 0):
                pool.wait_ge(accz, 16 * (2 * NG + 2))
                take(0, 0)
                with pool.Fori(0, NC) as k:
                    edge_rows(2 * k + 1, [(x_d, 0), (x_d, 1)], D, acc0_d, e_sum)
                    take(2 * k + 2, 2 * k + 2)
                    nc.gpsimd.indirect_dma_start(out=acc0_d, out_offset=bass.IndirectOffsetOnAxis(ap=e_tgti[:, 0:1], axis=0),
                                                 in_=e_sum[:, 0:2 * D], in_offset=None, bounds_check=last_row,
                                                 compute_op=ALU.add).then_inc(g_sct, 16)
                    pool.wait_ge(g_sct, 16 * k + 16)

            def gathers(g, s, table, width, sems, ready):
                pool.wait_ge(ready, g + 1)
                if not isinstance(g, int):
                    nc.gpsimd.tensor_tensor(spare[0:1, s:s + 1], ones[0:1, 0:1], ones[0:1, 0:1], ALU.add)
                for t in range(TG):
                    nc.gpsimd.indirect_dma_start(out=gx[:, s, t, 0:width], out_offset=None, in_=table,
                                                 in_offset=bass.IndirectOffsetOnAxis(ap=gidx[:, s, t:t + 1], axis=0),
                                                 bounds_check=last_node, oob_is_err=False).then_inc(sems[s], 16)

            def rstds(g, var, done):
                pool.wait_ge(var, g + 1)
                nc.gpsimd.tensor_tensor(rstd[:], vare[:], minus_half[:], ALU.pow).then_inc(done, 1)

            gathers(0, 0, x_d, D, gat, gidx_rdy)
            gathers(1, 1, x_d, D, gat, gidx_rdy)
            gathers(2, 0, x_d, D, gat, gidx_rdy)
            with pool.Fori(0, NG // 2 - 2) as i:
                for s in range(2):
                    rstds(2 * i + s, var0, rstd0)
                    gathers(2 * i + (3 + s), 1 - s, x_d, D, gat, gidx_rdy)
            rstds(NG - 4, var0, rstd0)
            gathers(NG - 1, 1, x_d, D, gat, gidx_rdy)
            for g in (NG - 3, NG - 2, NG - 1):
                rstds(g, var0, rstd0)

            for s in range(2):
                pool.wait_ge(h1_st[s], 16 * (NG // 2 + (LAST_PARTS - 1) * s))
            with pool.If(general > 0):
                with pool.Fori(0, NC) as k:
                    edge_rows(2 * k + (2 * NC + 1), [(h1_d, 0)], W, acc1_d, e_sum)
                    take(2 * k + (2 * NC + 2), 2 * k + (2 * NC + 2))
                    nc.gpsimd.indirect_dma_start(out=acc1_d, out_offset=bass.IndirectOffsetOnAxis(ap=e_tgti[:, 0:1], axis=0),
                                                 in_=e_sum[:, 0:W], in_offset=None, bounds_check=last_row,
                                                 compute_op=ALU.add).then_inc(g_sct, 16)
                    pool.wait_ge(g_sct, 16 * k + (16 * NC + 16))
            def own_sums(g, s):
                if not (isinstance(g, int) and g < 2):
                    pool.wait_ge(res_rdy, g - 1)
                pool.wait_ge(ay2_rdy, g + 1)
                nc.gpsimd.tensor_tensor(own_sum[:, s], ay[:, 2], h1g[:, s, :, 0:D], ALU.add).then_inc(own_rdy, 1)

            def all_sums(g, s):
                if not (isinstance(g, int) and g < 2):
                    pool.wait_ge(out_rdy, g - 1)
                pool.wait_ge(ay_rdy, g + 1)
                nc.gpsimd.tensor_tensor(total[s][:], ay[:, 0], ay[:, 1], ALU.add).then_inc(nb_rdy, 1)
                pool.wait_ge(nb_rdy, g + 1)
                pool.wait_ge(own_rdy, g + 1)
                nc.gpsimd.tensor_tensor(total[s][:], total[s][:], own_sum[:, s], ALU.add).then_inc(res_rdy, 1)

            for g in range(3):
                gathers(g, g % 2, h1_d, W, gat1, gidx1)

            def l1_step(g, s):
                own_sums(g, s)
                if not (isinstance(g, int) and g + 3 >= NG):
                    gathers(g + 3, 1 - s, h1_d, W, gat1, gidx1)
                all_sums(g, s)
                if not (isinstance(g, int) and g == 0):
                    rstds(g - 1, var1, rstd1)

            l1_step(0, 0)
            l1_step(1, 1)
            with pool.Fori(1, NG // 2 - 2) as i:
                for s in range(2):
                    l1_step(2 * i + s, s)
            for g in range(NG - 4, NG):
                l1_step(g, g % 2)
            rstds(NG - 1, var1, rstd1)

        @block.vector
        def _(dve):
            v = nc.vector
            st = Steps(dve, vchain)
            L = st.link
            G = Steps(dve, g_chain).link
            dve.wait_ge(iotas, 2)
            v.tensor_copy(iota[:], tmp_i[:, 0:P])
            v.tensor_copy(iota_t[:], tmp_i[:, 0:NT])
            v.tensor_copy(part[:], iota_i[:, 0:1])
            L(v.tensor_scalar(valid[:], iota_i[:], float(E), None, ALU.is_lt))
            dve.wait_ge(eload, 16 * 6)
            v.tensor_copy(s_nat[:], s_raw[:])
            v.tensor_scalar(t0_raw[:], d_raw[:, :, 0], 7, None, ALU.arith_shift_right)
            L(v.tensor_copy(d_nat[:], d_raw[:]))
            v.tensor_copy(t0_col[:, 0, :], t0_raw[:]).then_inc(nat, 1)
            dve.wait_ge(wT_ps, 1)
            v.tensor_copy(wnT[:], bank(4)[:, 0:D])
            v.tensor_tensor(wz[:, 0:D], bank(4)[:, D:2 * D], ident[:], ALU.add)
            v.tensor_copy(wx[:, 0:D], bank(4)[:, 3 * D:4 * D])
            v.tensor_scalar(wg[:, 0:D], bank(4)[:, 3 * D:4 * D], -1.0, None, ALU.mult)
            v.tensor_copy(wg[:, D:2 * D], bank(5)[:, 0:D])
            v.tensor_copy(wx[:, D:2 * D], bank(5)[:, D:2 * D])
            v.tensor_copy(wl2T[:], bank(4)[:, 2 * D:3 * D]).then_inc(wT_sb, 1)
            dve.wait_ge(wT_ps, 2)
            v.tensor_copy(wz[:, D:2 * D], bank(6)[:, 0:D])
            v.tensor_copy(wabs[:], bank(6)[:, 2 * D:3 * D])
            v.tensor_copy(wmid[:], bank(6)[:, D:2 * D]).then_inc(wT_sb, 1)
            dve.wait_ge(wT_ps, 3)
            v.tensor_copy(wsum[:], bank(7)[:, 0:D])
            v.tensor_scalar(vec[:, 0:D], bank(4)[:, 0:D], -1.0, None, ALU.mult)
            v.tensor_copy(vec[:, D:512], bank(4)[:, D:512])
            v.tensor_copy(vec[:, 512:5 * D + 3], bank(5)[:, 0:5 * D + 3 - 512])
            v.tensor_copy(brow[0:1, 0:2 * D], bank(7)[0:1, D:3 * D]).then_inc(wT_sb, 1)
            dve.wait_ge(wT_sb, 3)
            for j in range(BP):
                v.tensor_copy(bparts[0:1, j, :], brow[0:1, :]).then_inc(bsplit, 1)
                if j + 1 < BP:
                    dve.wait_ge(bsplit, 2 * j + 1)
                    v.tensor_tensor(brow[0:1, :], brow[0:1, :], bparts[0:1, j, :], ALU.subtract).then_inc(bsplit, 1)
                    dve.wait_ge(bsplit, 2 * j + 2)
            dve.wait_ge(edgeT, 1)
            v.memset(s_i[:], N - 1)
            L(v.memset(d_i[:], N - 1))
            v.tensor_copy(s_i[:, 0:NC], bank(0, 2)[:, 0:NC])
            L(v.tensor_copy(d_i[:, 0:NC], bank(2, 2)[:, 0:NC]))
            L(v.tensor_scalar(tmp_i[:], d_i[:], 7, None, ALU.arith_shift_right))
            v.tensor_copy(td[:], tmp_i[:]).then_inc(t_ready, 1)
            L(v.tensor_scalar(tmp2_i[:], d_i[:], 127, None, ALU.bitwise_and))
            v.tensor_copy(ld[:], tmp2_i[:])
            L(v.scalar_tensor_tensor(tmp2_i[:], s_i[:], 7, tmp2_i[:], ALU.logical_shift_left, ALU.bitwise_or))
            L(v.tensor_scalar(tmp_i[:], tmp2_i[:], 12, None, ALU.arith_shift_right))
            L(v.tensor_scalar(tmp2_i[:], tmp2_i[:], 4095, None, ALU.bitwise_and))
            v.tensor_scalar(hi[:], tmp_i[:], 1.0, None, ALU.add)
            v.tensor_scalar(lo[:], tmp2_i[:], -float(HALF), None, ALU.add)
            L(v.tensor_tensor(ta[:], s_i[:], d_i[:], ALU.is_equal))
            L(v.tensor_tensor(selfe[:], ta[:], valid[:], ALU.mult))
            v.tensor_tensor(other[:], valid[:], selfe[:], ALU.subtract)
            dve.wait_ge(t0_ps, 1)
            L(v.tensor_copy(t0[:], bank(0, 2)[:, 0:NCP]))
            L(v.tensor_tensor(ta[:], td[:], t0[:], ALU.subtract))
            v.scalar_tensor_tensor(in0[:], ta[:], 0.0, valid[:], ALU.is_equal, ALU.mult)
            L(v.scalar_tensor_tensor(in1[:], ta[:], 1.0, valid[:], ALU.is_equal, ALU.mult))
            v.tensor_tensor(tb[:], other[:], in0[:], ALU.mult).then_inc(masks, 1)
            dve.wait_ge(sums_ps, 1)
            v.tensor_copy(cols[:], bank(2, 2)[:, 0:NCP])
            v.tensor_copy(o_first[:], bank(4, 2)[:, 0:NCP])
            L(v.tensor_copy(n_first[:], bank(6, 2)[:, 0:NCP]))
            v.memset(ta[:], 1.0).then_inc(pre_rd, 1)
            dve.wait_ge(pre_rd, 1)
            L(v.tensor_tensor_scan(tb[:], ta[:], cols[:], 0.0, ALU.mult, ALU.add))
            L(v.tensor_tensor(pre[:], tb[:], cols[:], ALU.subtract))
            L(v.tensor_tensor(nxt[:], pre[:], o_first[:], ALU.add))
            L(v.memset(ta[:, 0:1], 0.0))
            L(v.tensor_tensor(ta[:, 1:NCP], t0[:, 1:NCP], t0[:, 0:NCP - 1], ALU.subtract))
            v.memset(start[:, 0:1], 0.0)
            L(v.scalar_tensor_tensor(start[:, 1:NCP], ta[:, 1:NCP], 1.0, nxt[:, 0:NCP - 1], ALU.is_equal, ALU.mult))
            L(v.scalar_tensor_tensor(tb[:], ta[:], 1.5, pre[:], ALU.is_gt, ALU.mult))
            L(v.tensor_tensor(start[:], start[:], tb[:], ALU.add))
            L(v.memset(tb[:], 0.0))
            L(v.tensor_tensor_scan(rank[:], tb[:], start[:], 0.0, ALU.add, ALU.max))
            L(v.tensor_copy(start[:], rank[:]))
            L(v.memset(bad[:], 0.0))
            L(v.tensor_scalar(tb[:, 0:NCP - 1], n_first[:, 0:NCP - 1], float(P), None, ALU.is_lt))
            L(v.tensor_tensor(bad[:, 1:NC], ta[:, 1:NC], tb[:, 0:NC - 1], ALU.is_lt))
            L(v.tensor_scalar(tb[:], n_first[:], part[:, 0:1], None, ALU.is_le))
            L(v.tensor_tensor(tb[:], tb[:], valid[:], ALU.mult))
            L(v.tensor_tensor(tb[:], tb[:], in1[:], ALU.not_equal))
            L(v.tensor_tensor(bad[:], bad[:], tb[:], ALU.add))
            L(v.tensor_tensor(tb[:], in0[:], in1[:], ALU.add))
            L(v.tensor_tensor(tb[:], tb[:], valid[:], ALU.not_equal))
            L(v.tensor_tensor(bad[:], bad[:], tb[:], ALU.add))
            dve.wait_ge(lower_ps, 1)
            L(v.tensor_tensor(rank[:], bank(0, 2)[:, 0:NCP], pre[:], ALU.add))
            L(v.tensor_tensor(rank[:], rank[:], start[:], ALU.subtract))
            L(v.tensor_tensor(tb[:], nxt[:], start[:], ALU.subtract))
            L(v.tensor_tensor(tb[:], tb[:], in1[:], ALU.mult))
            L(v.tensor_tensor(rank[:], rank[:], tb[:], ALU.subtract))
            L(v.scalar_tensor_tensor(tb[:], rank[:], float(P) - 0.5, other[:], ALU.is_gt, ALU.mult))
            L(v.tensor_tensor(bad[:], bad[:], tb[:], ALU.add))
            L(v.tensor_reduce(badsum[:, 0:1], bad[:], AX.X, ALU.add))
            L(v.tensor_tensor(ta[:], other[:], in0[:], ALU.mult))
            L(v.tensor_tensor(tb[:], other[:], in1[:], ALU.mult))
            v.tensor_tensor(place_v[:, :, 0], hi[:], ta[:], ALU.mult)
            v.tensor_tensor(place_v[:, :, 1], lo[:], ta[:], ALU.mult)
            v.tensor_tensor(place_v[:, :, 2], hi[:], tb[:], ALU.mult)
            v.tensor_tensor(place_v[:, :, 3], lo[:], tb[:], ALU.mult)
            v.tensor_tensor(count_v[:, :, 0], selfe[:], in0[:], ALU.mult)
            v.tensor_copy(count_v[:, :, 1], ta[:])
            v.tensor_tensor(count_v[:, :, 2], selfe[:], in1[:], ALU.mult)
            L(v.tensor_copy(count_v[:, :, 3], tb[:]))
            L(v.tensor_scalar(t0_col[:, 1, :], t0_col[:, 0, :], 1.0, None, ALU.add))

            def place_step(i, s):
                def wide(t):
                    return t[:, bass.ds(i * CB, CB)].unsqueeze(2).broadcast_to([P, CB, P])
                io = iota[:].unsqueeze(1).broadcast_to([P, CB, P])
                v.tensor_tensor(place_oh[:, s], io, wide(rank), ALU.is_equal)
                v.tensor_tensor(local_oh[:, s], io, wide(ld), ALU.is_equal).then_inc(place, 1)

            at = 0
            for b in range(NB):
                steps = min(P, NCP - b * P) // CB
                n2 = steps // 2
                if b == 0:
                    place_step(0, 0)
                    place_step(1, 1)
                with dve.Fori(1 if b == 0 else 0, n2) as i:
                    for s in range(2):
                        dve.wait_ge(placed, 2 * i + (at + s - 1))
                        place_step(2 * i + (at + s), s)
                at += 2 * n2
                if steps % 2:
                    dve.wait_ge(placed, at - 1)
                    place_step(at, at % 2)
                    at += 1
                if b:
                    dve.wait_ge(folded, b)
                v.tensor_scalar(fold[:, 0, :], iota_t[:], t0_col[:, 0, b:b + 1], None, ALU.is_equal)
                v.tensor_scalar(fold[:, 1, :], iota_t[:], t0_col[:, 1, b:b + 1], None, ALU.is_equal).then_inc(fold_rdy, 1)
                dve.wait_ge(fieldT, b + 1)
                v.tensor_copy(fieldsT[:], bank(2).bitcast(f16).rearrange("p (a n) -> p a n", a=8)).then_inc(fieldT_sb, 1)
            dve.wait_ge(folded, NB)
            v.tensor_copy(slot_hi[:], bank(4)[:, 0:NT])
            v.tensor_copy(slot_lo[:], bank(5)[:, 0:NT])
            v.tensor_copy(n_self[:], bank(6)[:, 0:NT])
            L(v.tensor_copy(n_in[:], bank(7)[:, 0:NT]))
            L(v.tensor_scalar(dinv[:], n_self[:], 1.0, None, ALU.add))
            L(v.tensor_tensor(dinv[:], dinv[:], n_in[:], ALU.add))

            def table(loc, idx, far_f):
                L(v.tensor_scalar(occ[:], slot_hi[:], 0.5, None, ALU.is_gt))
                L(v.tensor_scalar(slot_f[:], slot_lo[:], float(HALF - 2 * HALF), None, ALU.add))
                L(v.scalar_tensor_tensor(slot_f[:], slot_hi[:], float(2 * HALF), slot_f[:], ALU.mult, ALU.add))
                L(v.tensor_scalar(slot_f[:], slot_f[:], 0.0, None, ALU.max))
                L(v.tensor_copy(slot_i[:], slot_f[:]))
                v.tensor_scalar(slot_j[:], slot_i[:], 127, None, ALU.bitwise_and)
                L(v.tensor_scalar(slot_k[:], slot_i[:], 7, None, ALU.arith_shift_right))
                v.tensor_copy(far_f[:], slot_k[:])
                L(v.tensor_scalar(loc[:], slot_j[:], 1.0, None, ALU.add))
                L(v.tensor_tensor(loc[:], loc[:], occ[:], ALU.mult))
                L(v.tensor_scalar(loc[:], loc[:], -1.0, None, ALU.add))
                L(v.scalar_tensor_tensor(slot_f[:], far_f[:], float(OOB), occ[:], ALU.subtract, ALU.mult))
                L(v.tensor_scalar(slot_f[:], slot_f[:], float(OOB), None, ALU.add))
                v.tensor_copy(idx[:], slot_f[:])

            table(loc1, idx1, slot_lo)
            L(v.tensor_scalar(slot_j[:], slot_k[:], 7, None, ALU.arith_shift_right))
            L(v.tensor_copy(slot_f[:], slot_j[:]))
            L(v.tensor_scalar(slot_f[:], slot_f[:], -999.0, None, ALU.add))
            L(v.tensor_tensor(slot_f[:], slot_f[:], occ[:], ALU.mult))
            v.tensor_scalar(sort_f[:, :, 0], slot_f[:], 999.0, None, ALU.add)
            L(v.tensor_scalar(slot_j[:], slot_k[:], 127, None, ALU.bitwise_and))
            v.tensor_copy(sort_f[:, :, 1], slot_j[:])
            L(v.scalar_tensor_tensor(slot_f[:], iota_t[:], float(P), loc1[:], ALU.mult, ALU.add))
            L(v.tensor_tensor(slot_f[:], slot_f[:], occ[:], ALU.mult))
            L(v.tensor_copy(slot_i[:], slot_f[:]))
            L(v.scalar_tensor_tensor(slot_i[:], slot_i[:], 7, slot_j[:], ALU.logical_shift_left, ALU.bitwise_or))
            L(v.tensor_scalar(slot_k[:], slot_i[:], 12, None, ALU.arith_shift_right))
            L(v.tensor_scalar(slot_i[:], slot_i[:], 4095, None, ALU.bitwise_and))
            v.tensor_scalar(sort_f[:, :, 2], slot_k[:], 1.0, None, ALU.add)
            v.tensor_scalar(sort_f[:, :, 3], slot_i[:], -float(HALF), None, ALU.add).then_inc(tab1, 1)
            dve.wait_ge(tab1, 1)

            def tile_onehot(j, k):
                if not (isinstance(j, int) and j < 2 * CB):
                    dve.wait_ge(s_done, j - (2 * CB - 1))
                v.tensor_scalar(tile_oh(k), iota_t[:], sort_f[:, bass.ds(j, 1), 0:1].rearrange("p a b -> p (a b)"),
                                None, ALU.is_equal).then_inc(s_oh, 1)

            def sort_body(i, last=False):
                for c in range(0, 2 * CB, 2):
                    j = 2 * CB * i + c
                    for d in range(2):
                        at = rank_s[:, (c + d) // CB, (c + d) % CB:(c + d) % CB + 1]
                        dve.wait_ge(s_rankps, j + (d + 1))
                        v.tensor_tensor_reduce(out=junk[:, d, :], in0=tile_oh(c + d), in1=bank(4 * d)[:, 0:NT], scale=1.0, scalar=0.0,
                                               op0=ALU.mult, op1=ALU.add, accum_out=at).then_inc(s_rank, 1)
                    for d in range(2):
                        at = rank_s[:, (c + d) // CB, (c + d) % CB:(c + d) % CB + 1]
                        if not (isinstance(j, int) and j + d < CB):
                            dve.wait_ge(s_val, j + (d + 1 - CB))
                        dve.wait_ge(s_rank, j + (d + 1))
                        v.tensor_scalar(rank_oh[:, (c + d) % CB, :], iota[:], at, None, ALU.is_equal).then_inc(s_roh, 1)
                    for d in range(2):
                        if not (last and c + d + CB >= 2 * CB):
                            tile_onehot(j + (d + CB), (c + d + CB) % (2 * CB))
                    if c % CB == CB - 2:
                        v.tensor_copy(rank0[:, bass.ds(2 * CB * i + (c + 2 - CB), CB)], rank_s[:, c // CB, :]).then_inc(s_kept, 1)

            for j in range(CB):
                tile_onehot(j, j)
            sort_body(0)
            with dve.Fori(1, NT // (2 * CB) - 1) as i:
                sort_body(i)
            sort_body(NT // (2 * CB) - 1, last=True)
            dve.wait_ge(s_done, NT)
            v.tensor_copy(slot_hi[:], bank(1)[:, 0:NT])
            dve.wait_ge(s_kept, NT // CB)
            L(v.tensor_scalar(junk[:, 0, :], rank0[:], float(P) - 0.5, None, ALU.is_gt))
            L(v.tensor_reduce(badsum[:, 1:2], junk[:, 0, :], AX.X, ALU.add))
            L(v.tensor_tensor(badsum[:, 0:1], badsum[:, 0:1], badsum[:, 1:2], ALU.add))
            v.tensor_copy(slot_lo[:], bank(2)[:, 0:NT])
            v.tensor_copy(n_out[:], bank(3)[:, 0:NT]).then_inc(bad_rdy, 1)
            dve.wait_ge(bad_rdy, 1)
            table(loc0, idx0, slot_lo)
            dve.wait_ge(bad_ps, 1)
            L(v.tensor_scalar(okv[:], bank(0)[:, 0:1], 0.5, None, ALU.is_lt))
            L(v.tensor_scalar(badsum[:, 0:1], okv[:], -1.0, 1.0, ALU.mult, ALU.add))
            v.tensor_copy(flag[:], badsum[:, 0:1]).then_inc(flagged, 1)
            for loc, idx in ((loc0, idx0), (loc1, idx1)):
                L(v.tensor_scalar(loc[:], loc[:], 1.0, okv[:, 0:1], ALU.add, ALU.mult))
                L(v.tensor_scalar(loc[:], loc[:], -1.0, None, ALU.add))
                L(v.tensor_copy(slot_f[:], idx[:]))
                L(v.tensor_scalar(slot_f[:], slot_f[:], -float(OOB), okv[:, 0:1], ALU.add, ALU.mult))
                L(v.tensor_scalar(slot_f[:], slot_f[:], float(OOB), None, ALU.add))
                L(v.tensor_copy(idx[:], slot_f[:]))
            v.tensor_scalar(n_self[:], n_self[:], okv[:, 0:1], None, ALU.mult).then_inc(n_self_rdy, 1)
            dve.wait_ge(n_self_rdy, 1)

            def l0_indices(g, s):
                if not (isinstance(g, int) and g < 2):
                    dve.wait_ge(s1_ps, g - 1)
                v.tensor_copy(gidx[:, s, :], idx0[:, bass.ds(g * TG, TG)]).then_inc(gidx_rdy, 1)

            def l0_onehots(g, s):
                if not (isinstance(g, int) and g < 2):
                    dve.wait_ge(s2_ps, g - 1)
                v.tensor_tensor(oh[:, s], iota[:].unsqueeze(1).broadcast_to([P, TG, P]),
                                loc0[:, bass.ds(g * TG, TG)].unsqueeze(2).broadcast_to([P, TG, P]), ALU.is_equal).then_inc(oh_rdy, 1)

            for g in (0, 1):
                l0_indices(g, g)
                l0_onehots(g, g)
            dve.wait_ge(flagged, 1)
            general = dve.value_load(flag[0:1, 0:1], min_val=0, max_val=1)
            with dve.If(general > 0):
                G(v.tensor_scalar(tmp_i[:], s_i[:], 7, None, ALU.arith_shift_right))
                G(v.tensor_copy(ta[:], tmp_i[:]))
                G(v.tensor_scalar(tmp_i[:], s_i[:], 127, None, ALU.bitwise_and))
                G(v.tensor_copy(tb[:], tmp_i[:]))
                G(v.tensor_scalar(in0[:], valid[:], -999.0, 999.0, ALU.mult, ALU.add))
                G(v.tensor_tensor(ta[:], ta[:], in0[:], ALU.add))
                G(v.tensor_tensor(in1[:], td[:], in0[:], ALU.add))

                def count_onehots(k):
                    v.tensor_scalar(g_loh[:, 0, :], iota[:], tb[:, bass.ds(k, 1)], None, ALU.is_equal)
                    v.tensor_scalar(g_loh[:, 1, :], iota[:], ld[:, bass.ds(k, 1)], None, ALU.is_equal)
                    v.tensor_scalar(g_oh[:, 0, :], iota_t[:], ta[:, bass.ds(k, 1)], None, ALU.is_equal)
                    v.tensor_scalar(g_oh[:, 1, :], iota_t[:], in1[:, bass.ds(k, 1)], None, ALU.is_equal).then_inc(g_ohr, 1)

                count_onehots(0)
                with dve.Fori(1, NC) as k:
                    dve.wait_ge(g_cnt, k)
                    count_onehots(k)
                dve.wait_ge(g_cnt, NC)
                v.tensor_copy(n_out[:], bank(1)[:, 0:NT]).then_inc(g_v, 1)
                v.tensor_copy(n_in[:], bank(2)[:, 0:NT]).then_inc(g_v, 1)
                dve.wait_ge(g_v, 2)
            L(v.tensor_tensor(slot_f[:], n_out[:], n_self[:], ALU.add))
            v.tensor_scalar(some[:], slot_f[:], 1.0, None, ALU.min)
            L(v.tensor_scalar(slot_f[:], slot_f[:], 1.0, None, ALU.max))
            L(v.reciprocal(rc[:], slot_f[:]))
            part16 = junk[:, 0, :].bitcast(bf16)
            left, parts = rc, (slot_lo, occ, rank0)
            for j, rc_j in enumerate(parts):
                L(v.tensor_copy(part16, left[:]))
                L(v.tensor_copy(rc_j[:], part16))
                if j + 1 < BP:
                    L(v.tensor_tensor(slot_f[:], left[:], rc_j[:], ALU.subtract))
                    left = slot_f
            v.tensor_scalar(self_w[:], n_self[:], 1.0, None, ALU.add).then_inc(stat_rdy, 1)
            dve.wait_ge(stat_rdy, 1)
            dve.wait_ge(dinv_rdy, NT // CB)
            with dve.If(general > 0):
                v.memset(slot_hi[:], -0.5)
                v.tensor_tensor(slot_f[:], n_in[:], self_w[:], ALU.add).then_inc(gen_deg, 1)
                dve.wait_ge(dinv_rdy, NT // CB + 1)
            L(v.tensor_tensor(self_w[:], self_w[:], dinv[:], ALU.mult))
            dve.wait_ge(statT_ps, 1)
            rest = NT % P
            both = bank(4, BP + 1).rearrange("p (a b n) -> p a b n", a=BP + 1, b=4)
            v.tensor_copy(statT[:, :, 0:NT // P, :], both[:, :, 0:NT // P, :])
            v.tensor_copy(statT[0:rest, :, NT // P, :], both[0:rest, :, NT // P, :]).then_inc(statT_sb, 1)

            with dve.If(general > 0):
                with dve.Fori(0, NC) as k:
                    col = bass.ds(k, 1)

                    def own(j):
                        dve.wait_ge(g_v, 2 + 12 * k + j)
                    v.tensor_scalar(e_tgt[:], s_i[:, col], -float(OOB), valid[:, col], ALU.add, ALU.mult).then_inc(g_v, 1)
                    v.tensor_scalar(e_key[:], d_i[:, col], -float(OOB), valid[:, col], ALU.add, ALU.mult).then_inc(g_v, 1)
                    own(2)
                    v.tensor_scalar(e_idx[:, 0:1], e_tgt[:], float(OOB), None, ALU.add)
                    v.tensor_scalar(e_idx[:, 1:2], e_key[:], float(OOB), None, ALU.add).then_inc(g_idx, 1)
                    v.tensor_scalar(e_keyb[:], ones[:], e_tgt[:, 0:1], None, ALU.mult).then_inc(g_dif, 1)
                    dve.wait_ge(g_gat, 32 * k + 32)
                    v.tensor_tensor(e_diff[:], e_rows[:, 0, 0:D], e_rows[:, 1, 0:D], ALU.subtract).then_inc(g_dif, 1)
                    v.tensor_copy(e_pay[:, 0:D], e_rows[:, 1, 0:D])
                    dve.wait_ge(g_pe, 4 * k + 1)
                    v.tensor_scalar(e_same[:], bank(0)[:, 0:P], e_tgt[:, 0:1], None, ALU.is_equal).then_inc(g_v, 1)
                    dve.wait_ge(g_pe, 4 * k + 2)
                    v.tensor_copy(e_diffT[:], bank(1)[:, 0:D]).then_inc(g_dif, 1)
                    own(3)
                    v.tensor_tensor(e_junk[:], e_same[:], after[:], ALU.mult).then_inc(g_v, 1)
                    own(4)
                    v.tensor_reduce(e_prev[:], e_junk[:], AX.X, ALU.add).then_inc(g_v, 1)
                    own(5)
                    v.tensor_scalar(e_prev[:], e_prev[:], 0.5, None, ALU.is_lt).then_inc(g_v, 1)
                    own(6)
                    v.tensor_tensor(e_lead[:], e_prev[:], valid[:, col], ALU.mult).then_inc(g_v, 1)
                    v.tensor_scalar(e_key[:], part[:], float(NPAD - OOB), None, ALU.add).then_inc(g_v, 1)
                    own(8)
                    v.tensor_tensor(e_tgt[:], e_tgt[:], e_key[:], ALU.subtract).then_inc(g_v, 1)
                    own(9)
                    v.scalar_tensor_tensor(e_tgt[:], e_tgt[:], e_lead[:, 0:1], e_key[:], ALU.mult, ALU.add).then_inc(g_v, 1)
                    own(10)
                    v.tensor_scalar(e_tgti[:], e_tgt[:], float(OOB), None, ALU.add)
                    dve.wait_ge(g_pe, 4 * k + 3)
                    v.tensor_scalar(e_junk[:], bank(2)[:, 0:D], -1.0, None, ALU.mult).then_inc(g_v, 1)
                    own(11)
                    v.tensor_tensor(e_pay[:, D:2 * D], bank(2)[:, 0:D], e_junk[:], ALU.max).then_inc(g_dif, 1)
                    dve.wait_ge(g_pe, 4 * k + 4)
                    v.tensor_copy(e_sum[:], bank(3)[:, 0:2 * D]).then_inc(g_v, 1)
                    own(12)
                    v.tensor_copy(e_prev[:], e_prev[:]).then_inc(g_idx, 1)
                    dve.wait_ge(g_sct, 16 * k + 16)

            def row_stats(rows, own):
                for t in range(TG):
                    v.bn_stats(stats[:, t, :], rows[:, t, :]).then_inc(own, 1)

            def means(g, own, var):
                dve.wait_ge(own, 2 * TG * g + TG)
                v.memset(spare[0:1, 3:4], 0.0)
                for t in range(TG):
                    v.bn_aggr(mv[:, t, :], stats[:, t, :]).then_inc(own, 1)
                dve.wait_ge(own, 2 * TG * g + 2 * TG)
                v.tensor_scalar(vare[:], mv[:, :, 1], EPS, None, ALU.add).then_inc(var, 1)

            def l0_abs_copy(g):
                dve.wait_ge(s2_ps, g + 1)
                if not (isinstance(g, int) and g == 0):
                    dve.wait_ge(z_ps, g)
                v.tensor_copy(s2T[:], bank(5).rearrange("p (t n) -> p t n", t=TG)).then_inc(s2_sb, 1)

            def l0_differences(g):
                dve.wait_ge(gxT_sb, g + 1)
                dve.wait_ge(dT_ps, g + 1)
                if not (isinstance(g, int) and g == 0):
                    dve.wait_ge(hd_ps, g)
                v.tensor_tensor(dT[:], bank(2).rearrange("p (t n) -> p t n", t=TG), hd[:],
                                ALU.subtract).then_inc(dT_sb, 1)

            def l0_residual(g):
                if not (isinstance(g, int) and g == 0):
                    dve.wait_ge(h1_rdy, g)
                dve.wait_ge(p2_sb, g + 1)
                v.tensor_tensor(res[:], bank(6, 2).rearrange("p (t c n) -> p t c n", t=TG, c=2)[:, :, 0, :],
                                p2[:], ALU.add).then_inc(z_rd, 1)
                dve.wait_ge(z_rd, g + 1)
                row_stats(res, stats0)
                means(g, stats0, var0)

            def l0_apply(g, s, stores):
                if stores is not None:
                    dve.wait_ge(h1_st[s], stores)
                v.tensor_copy(h1g[:, s, :, D], dinv[:, bass.ds(g * TG, TG)])
                dve.wait_ge(rstd0, g + 1)
                for t in range(TG):
                    last = v.tensor_scalar(h1g[:, s, t, 0:D], res[:, t, :], mv[:, t, 0:1], rstd[:, t:t + 1],
                                           ALU.subtract, ALU.mult)
                last.then_inc(h1_rdy, 1)

            def l0_step(g, s, stores):
                whole = isinstance(g, int)
                if not (whole and g + 2 >= NG):
                    l0_indices(g + 2, s)
                l0_abs_copy(g)
                if not (whole and g + 2 >= NG):
                    l0_onehots(g + 2, s)
                if not (whole and g == 0):
                    l0_apply(g - 1, 1 - s, stores)
                if not (whole and g + 1 >= NG):
                    l0_differences(g + 1)
                l0_residual(g)

            l0_differences(0)
            l0_step(0, 0, None)
            l0_step(1, 1, None)
            l0_step(2, 0, None)
            with dve.Fori(1, NG // 2 - 2) as i:
                l0_step(2 * i + 1, 1, 16 * i)
                l0_step(2 * i + 2, 0, 16 * i)
            for g in (NG - 3, NG - 2, NG - 1):
                l0_step(g, g % 2, 16 * ((g - 1) // 2))
            l0_apply(NG - 1, 1, 16 * (NG // 2 - 1))

            with dve.If(general > 0):
                with dve.Fori(0, NC) as k:
                    col = bass.ds(k, 1)
                    vb = 2 + 12 * NC

                    def own(j):
                        dve.wait_ge(g_v, (vb + j) + 12 * k)
                    v.tensor_scalar(e_key[:], s_i[:, col], -float(OOB), valid[:, col], ALU.add, ALU.mult).then_inc(g_v, 1)
                    v.tensor_scalar(e_tgt[:], d_i[:, col], -float(OOB), valid[:, col], ALU.add, ALU.mult).then_inc(g_v, 1)
                    own(2)
                    v.tensor_scalar(e_idx[:, 0:1], e_key[:], float(OOB), None, ALU.add).then_inc(g_idx, 1)
                    v.tensor_scalar(e_keyb[:], ones[:], e_tgt[:, 0:1], None, ALU.mult).then_inc(g_dif, 1)
                    dve.wait_ge(g_gat, 16 * k + (32 * NC + 16))
                    v.tensor_scalar(e_pay[:, 0:D], e_rows[:, 0, 0:D], e_rows[:, 0, D:W], None, ALU.mult)
                    v.tensor_copy(e_pay[:, D:W], e_rows[:, 0, D:W]).then_inc(g_v, 1)
                    dve.wait_ge(g_pe, 2 * k + (4 * NC + 1))
                    v.tensor_scalar(e_same[:], bank(0)[:, 0:P], e_tgt[:, 0:1], None, ALU.is_equal).then_inc(g_dif, 1)
                    dve.wait_ge(g_dif, 4 * NC + 2 * k + 2)
                    v.tensor_tensor(e_junk[:], e_same[:], after[:], ALU.mult).then_inc(g_v, 1)
                    own(4)
                    v.tensor_reduce(e_prev[:], e_junk[:], AX.X, ALU.add).then_inc(g_v, 1)
                    own(5)
                    v.tensor_scalar(e_prev[:], e_prev[:], 0.5, None, ALU.is_lt).then_inc(g_v, 1)
                    own(6)
                    v.tensor_tensor(e_lead[:], e_prev[:], valid[:, col], ALU.mult).then_inc(g_v, 1)
                    v.tensor_scalar(e_key[:], part[:], float(NPAD - OOB), None, ALU.add).then_inc(g_v, 1)
                    own(8)
                    v.tensor_tensor(e_tgt[:], e_tgt[:], e_key[:], ALU.subtract).then_inc(g_v, 1)
                    own(9)
                    v.scalar_tensor_tensor(e_tgt[:], e_tgt[:], e_lead[:, 0:1], e_key[:], ALU.mult, ALU.add).then_inc(g_v, 1)
                    own(10)
                    v.tensor_scalar(e_tgti[:], e_tgt[:], float(OOB), None, ALU.add).then_inc(g_v, 1)
                    dve.wait_ge(g_pe, 2 * k + (4 * NC + 2))
                    v.tensor_copy(e_sum[:, 0:W], bank(3)[:, 0:W]).then_inc(g_v, 1)
                    own(12)
                    v.tensor_copy(e_prev[:], e_prev[:]).then_inc(g_idx, 1)
                    dve.wait_ge(g_sct, 16 * k + (16 * NC + 16))

            def l1_indices(g, s):
                if not (isinstance(g, int) and g < 2):
                    dve.wait_ge(yT_ps, g - 1)
                v.tensor_copy(gidx[:, s, :], idx1[:, bass.ds(g * TG, TG)]).then_inc(gidx1, 1)

            def l1_onehots(g, s, half):
                if not (isinstance(g, int) and g < 2):
                    dve.wait_ge(yT_ps, g - 1)
                dve.wait_ge(gat1[s], (half + 1) * (16 * TG))
                for t in range(TG):
                    last = v.tensor_scalar(oh[:, s, t, :], iota[:], loc1[:, bass.ds(g * TG + t, 1)], gx[:, s, t, D:W],
                                           ALU.is_equal, ALU.mult)
                last.then_inc(oh1, 1)

            def l1_gamma(g):
                dve.wait_ge(yT_ps, g + 1)
                v.tensor_tensor(gam[:], bank(3)[:, 0:TG], self_w[:, bass.ds(g * TG, TG)], ALU.add).then_inc(gam_sum, 1)

            def l1_gamma_scale(g):
                dve.wait_ge(gam_sum, g + 1)
                v.tensor_tensor(gam[:], gam[:], dinv[:, bass.ds(g * TG, TG)], ALU.mult).then_inc(gam_rd, 1)

            xh = bank(6).rearrange("p (t n) -> p t n", t=TG)
            xi = bank(7).rearrange("p (t n) -> p t n", t=TG)

            def l1_dots(g, k, part_of, done):
                for t in range(TG):
                    last = v.scalar_tensor_tensor(dot_junk[:, k, t, :], part_of(t), 0.0, vec[:, (2 + k) * D:(3 + k) * D],
                                                  ALU.max, ALU.mult, accum_out=dots[:, k, t:t + 1])
                if done is not None:
                    last.then_inc(done, 1)

            def l1_gate(g, s):
                first = isinstance(g, int) and g == 0
                dve.wait_ge(xi_ps, g + 1)
                if not first:
                    dve.wait_ge(gate2_rdy, g)
                l1_dots(g, 2, lambda t: xi[:, t, :], dots2_rdy)
                if not (isinstance(g, int) and g < 2):
                    dve.wait_ge(ay_rdy, g - 1)
                dve.wait_ge(gam_rd, g + 1)
                dve.wait_ge(g_sb, g + 1)
                for t in range(TG):
                    last = v.scalar_tensor_tensor(q[:, s, t, :], vec[:, 0:2 * D], gam[:, t:t + 1], gs[:, t, :], ALU.mult, ALU.add)
                last.then_inc(q_rdy, 1)
                dve.wait_ge(q_rdy, g + 1)
                dve.wait_ge(xh_ps, g + 1)
                v.tensor_tensor(q[:, s, :, 0:D], xh, q[:, s, :, 0:D], ALU.add).then_inc(x_rd, 1)
                if not first:
                    dve.wait_ge(gate_rdy, g)
                l1_dots(g, 1, lambda t: q[:, s, t, D:2 * D], None)
                dve.wait_ge(x_rd, g + 1)
                l1_dots(g, 0, lambda t: q[:, s, t, 0:D], dots_rdy)
                if not (isinstance(g, int) and g + 3 >= NG):
                    l1_indices(g + 3, 1 - s)

            def l1_stats(g, s):
                dve.wait_ge(res_rdy, g + 1)
                row_stats(total[s], stats1)

            def l1_means(g):
                if not (isinstance(g, int) and g == 0):
                    dve.wait_ge(out_rdy, g)
                means(g, stats1, var1)

            def l1_apply(g, s, stores):
                if stores is not None:
                    dve.wait_ge(out_st[s], stores)
                dve.wait_ge(rstd1, g + 1)
                for t in range(TG):
                    last = v.tensor_scalar(outg[:, s, t, :], total[s][:, t, :], mv[:, t, 0:1], rstd[:, t:t + 1],
                                           ALU.subtract, ALU.mult)
                last.then_inc(out_rdy, 1)

            def l1_step(g, s, half):
                whole = isinstance(g, int)
                l1_gate(g, s)
                if not (whole and g + 1 >= NG):
                    l1_gamma(g + 1)
                if not (whole and g + 2 >= NG):
                    l1_onehots(g + 2, s, half + 1)
                if not (whole and g + 1 >= NG):
                    l1_gamma_scale(g + 1)
                if not (whole and g == 0):
                    l1_stats(g - 1, 1 - s)
                if not (whole and g < 2):
                    l1_apply(g - 2, s, None if whole and g < 4 else (half - 1) * 16)
                if not (whole and g == 0):
                    l1_means(g - 1)

            l1_indices(0, 0)
            l1_indices(1, 1)
            l1_onehots(0, 0, 0)
            l1_onehots(1, 1, 0)
            l1_indices(2, 0)
            l1_gamma(0)
            l1_gamma_scale(0)
            for g in range(4):
                l1_step(g, g % 2, g // 2)
            with dve.Fori(2, NG // 2 - 2) as i:
                for s in range(2):
                    l1_step(2 * i + s, s, i)
            for g in range(NG - 4, NG):
                l1_step(g, g % 2, g // 2)
            l1_apply(NG - 2, 0, 16 * (NG // 2 - 1))
            l1_stats(NG - 1, 1)
            l1_means(NG - 1)
            l1_apply(NG - 1, 1, 16 * (NG // 2 - 1))

        @block.tensor
        def _(pe):
            mm = nc.tensor.matmul

            def wide_mm(b, lhsT, rhs, start=True, stop=True):
                mm(psum[:, 512 * b:512 * b + 512], lhsT, rhs[:, 0:512], start=start, stop=stop)
                return mm(psum[:, 512 * b + 512:512 * b + NCP], lhsT, rhs[:, 512:NCP], start=start, stop=stop)

            pe.wait_ge(consts, 3)
            pe.wait_ge(wload, 16 * 19)
            for k, w in enumerate((wn[:], wl[:, 0:D], wl[:, D:2 * D], w1[:, 0, :])):
                nc.tensor.transpose(bank(4)[:, k * D:(k + 1) * D], w, ident[:])
            nc.tensor.transpose(bank(5)[:, 0:D], w1[:, 1, :], ident[:])
            nc.tensor.transpose(bank(5)[:, D:2 * D], w1[:, 2, :], ident[:]).then_inc(wT_ps, 1)
            pe.wait_ge(wT_sb, 1)
            mm(bank(6)[:, 0:D], wn[:], wl2T[:], start=True, stop=True)
            mm(bank(6)[:, D:2 * D], we[:, 0:D], wl2T[:], start=True, stop=True)
            mm(bank(6)[:, 2 * D:3 * D], we[:, D:2 * D], wl2T[:], start=True, stop=True).then_inc(wT_ps, 1)
            pe.wait_ge(wT_sb, 2)
            mm(bank(7)[:, 0:D], wn[:], wmid[:], start=True, stop=True)
            mm(bank(7)[0:1, D:2 * D], bcol[:, 0:1], wl2T[:], start=True, stop=True)
            mm(bank(7)[0:1, 2 * D:3 * D], bcol[:, 1:2], wl2T[:], start=True, stop=False)
            mm(bank(7)[0:1, 2 * D:3 * D], bcol[:, 0:1], wmid[:], start=False, stop=True)
            mm(bank(4), ones_row[0:1, :], vec_row[0:1, 0:512], start=True, stop=True)
            mm(bank(5)[:, 0:5 * D + 3 - 512], ones_row[0:1, :], vec_row[0:1, 512:5 * D + 3], start=True, stop=True).then_inc(wT_ps, 1)

            pe.wait_ge(nat, 1)
            for b in range(NB):
                n = min(P, NC - b * P)
                nc.tensor.transpose(psum[:, b * P:b * P + n], s_nat[0:n, b, :], ident[0:n, 0:n])
                last = nc.tensor.transpose(psum[:, 1024 + b * P:1024 + b * P + n], d_nat[0:n, b, :], ident[0:n, 0:n])
            last.then_inc(edgeT, 1)
            pe.wait_ge(t_ready, 1)
            wide_mm(0, row0[:], td).then_inc(t0_ps, 1)
            pe.wait_ge(masks, 1)
            pe.wait_ge(wT_sb, 3)
            wide_mm(2, ones[:], other)
            wide_mm(4, ones[:], tb)
            wide_mm(6, ones[:], in0).then_inc(sums_ps, 1)
            wide_mm(0, before[:], other).then_inc(lower_ps, 1)

            def place_step(i, s):
                pe.wait_ge(place, i + 1)
                pe.wait_ge(p_staged, i + 1)
                if not (isinstance(i, int) and i < 2):
                    pe.wait_ge(p_copied, i - 1)
                o = bank(s)[:, 0:2 * 4 * CB].rearrange("p (a f c) -> p a f c", a=2, f=4)
                for c in range(CB):
                    mm(o[:, 0, :, c], place_oh[:, s, c, :], step_v[:, s, c, 0, :], start=True, stop=True)
                    last = mm(o[:, 1, :, c], local_oh[:, s, c, :], step_v[:, s, c, 1, :], start=True, stop=True)
                last.then_inc(placed, 1)

            at = 0
            for b in range(NB):
                n = min(P, NCP - b * P)
                steps = n // CB
                n2 = steps // 2
                if b == 0:
                    place_step(0, 0)
                    place_step(1, 1)
                with pe.Fori(1 if b == 0 else 0, n2) as i:
                    for s in range(2):
                        place_step(2 * i + (at + s), s)
                at += 2 * n2
                if steps % 2:
                    place_step(at, at % 2)
                    at += 1
                pe.wait_ge(p_copied, at)
                if b:
                    pe.wait_ge(fieldT_sb, b)
                fT = bank(2).bitcast(f16).rearrange("p (a n) -> p a n", a=8)
                for f in range(8):
                    last = nc.tensor.transpose(fT[0:n, f, :], fields[:, f, 0:n], ident16[:])
                last.then_inc(fieldT, 1)
                pe.wait_ge(fold_rdy, b + 1)
                pe.wait_ge(fieldT_sb, b + 1)
                for f in range(8):
                    which, i1 = 2 * (f // 4) + f % 2, (f % 4) // 2
                    last = mm(bank(4 + which)[:, 0:NT], fieldsT[0:n, f, :], fold[0:n, i1, :],
                              start=(b == 0 and i1 == 0), stop=(b == NB - 1 and i1 == 1), skip_group_check=True)
                last.then_inc(folded, 1)

            pe.wait_ge(tab1, 1)

            def count(b, lhsT, k, start=False):
                return mm(bank(b)[:, 0:NT], lhsT[:], tile_oh(k % (2 * CB)), start=start, stop=True, skip_group_check=True)

            def advance(j, k):
                pe.wait_ge(s_rank, j + 1)
                count(0, notbefore16, k)
                count(0, all16, k + 1)
                pe.wait_ge(s_oh, j + 3)
                count(0, before16, k + 2).then_inc(s_rankps, 1)
                pe.wait_ge(s_rank, j + 2)
                count(4, notbefore16, k + 1)
                count(4, all16, k + 2)
                pe.wait_ge(s_oh, j + 4)
                count(4, before16, k + 3).then_inc(s_rankps, 1)

            def slots_mm(j, k, first=False):
                t = tile_oh(k)
                pe.wait_ge(s_src, j + 1)
                mm(bank(3)[:, 0:NT], src_oh[:, k % CB, :], t, start=first, stop=True, skip_group_check=True)
                pe.wait_ge(s_val, j + 1)
                mm(bank(1)[:, 0:NT], hi_oh[:, k % CB, :], t, start=first, stop=True, skip_group_check=True)
                mm(bank(2)[:, 0:NT], lo_oh[:, k % CB, :], t, start=first, stop=True, skip_group_check=True).then_inc(s_done, 1)

            def sort_body(i, first=False, last=False):
                for k in range(0, 2 * CB, 2):
                    j = 2 * CB * i + k
                    if not (last and k == 2 * CB - 2):
                        advance(j, k)
                    if not (first and k == 0):
                        slots_mm(j - 2, (k - 2) % (2 * CB), first and k == 2)
                        slots_mm(j - 1, (k - 1) % (2 * CB))

            pe.wait_ge(s_oh, 1)
            count(0, before16, 0, start=True).then_inc(s_rankps, 1)
            count(4, all16, 0, start=True)
            pe.wait_ge(s_oh, 2)
            count(4, before16, 1).then_inc(s_rankps, 1)
            sort_body(0, first=True)
            with pe.Fori(1, NT // (2 * CB) - 1) as i:
                sort_body(i)
            sort_body(NT // (2 * CB) - 1, last=True)
            for j in (NT - 2, NT - 1):
                slots_mm(j, j % (2 * CB))
            pe.wait_ge(bad_rdy, 1)
            mm(bank(0)[:, 0:1], ones[:], badsum[:, 0:1], start=True, stop=True).then_inc(bad_ps, 1)
            pe.wait_ge(flagged, 1)
            general = pe.value_load(flag[0:1, 0:1], min_val=0, max_val=1)
            with pe.If(general > 0):
                def count_mm(j, first):
                    pe.wait_ge(g_ohr, j + 1)
                    mm(bank(1)[:, 0:NT], g_loh[:, 0, :], g_oh[:, 0, :], start=first, stop=True, skip_group_check=True)
                    mm(bank(2)[:, 0:NT], g_loh[:, 1, :], g_oh[:, 1, :], start=first, stop=True, skip_group_check=True).then_inc(g_cnt, 1)
                count_mm(0, True)
                with pe.Fori(1, NC) as k:
                    count_mm(k, False)
            pe.wait_ge(stat_rdy, 1)
            NB4 = -(-NT // P)
            for k, t in enumerate((slot_lo, occ, rank0, some)):
                for b in range(NB4):
                    n = min(P, NT - b * P)
                    last = nc.tensor.transpose(psum[0:n, 2048 + 512 * k + P * b:2048 + 512 * k + P * (b + 1)], t[:, b * P:b * P + n], ident[:])
            last.then_inc(statT_ps, 1)

            with pe.If(general > 0):
                with pe.Fori(0, NC) as k:
                    pe.wait_ge(g_dif, 4 * k + 1)
                    nc.tensor.transpose(bank(0)[:, 0:P], e_keyb[:], ident[:]).then_inc(g_pe, 1)
                    pe.wait_ge(g_dif, 4 * k + 2)
                    nc.tensor.transpose(bank(1)[:, 0:P], e_diff[:], ident[:]).then_inc(g_pe, 1)
                    pe.wait_ge(g_dif, 4 * k + 3)
                    mm(bank(2)[:, 0:D], e_diffT[:], wnT[:], start=True, stop=True).then_inc(g_pe, 1)
                    pe.wait_ge(g_dif, 4 * k + 4)
                    mm(bank(3)[:, 0:2 * D], e_same[:], e_pay[:], start=True, stop=True).then_inc(g_pe, 1)
                pe.wait_ge(g_idx, 2 * NC)

            pe.wait_ge(bload, 16 * BP * (BP + 3))
            pe.wait_ge(statT_sb, 1)

            def landed(g, s, per, half):
                if isinstance(g, int):
                    return per * ((g - s) // 2 + 1) + (per * (LAST_PARTS - 1) if g == NG - 1 and per == 16 else 0)
                return half * per

            def transposes(g, s, half):
                pe.wait_ge(xl[s], landed(g, s, 16, half))
                pe.wait_ge(oh_rdy, g + 1)
                if not (isinstance(g, int) and g == 0):
                    pe.wait_ge(xT_sb, g)
                    pe.wait_ge(ohT_sb, g)
                for t in range(TG):
                    nc.tensor.transpose(bank(0)[:, t * P:(t + 1) * P], xg[:, s, t, :], ident[:])
                for t in range(TG):
                    nc.tensor.transpose(bank(1)[:, t * P:(t + 1) * P], oh[:, s, t, :], ident[:])
                pe.wait_ge(gat[s], landed(g, s, 16 * TG, half))
                if not (isinstance(g, int) and g == 0):
                    pe.wait_ge(hd_sb, g)
                for t in range(TG):
                    last = nc.tensor.transpose(bank(3)[:, t * P:(t + 1) * P], gx[:, s, t, 0:D], ident[:])
                last.then_inc(trans, 1)

            def differences(g, s, half):
                pe.wait_ge(ohT_sb, g + 1)
                if not (isinstance(g, int) and g == 0):
                    pe.wait_ge(dT_sb, g)
                for t in range(TG):
                    last = mm(bank(2)[:, t * P:(t + 1) * P], xg[:, s, t, :], ohT[:, t, :], start=True, stop=True)
                last.then_inc(dT_ps, 1)

            def edge_products(g, s):
                pe.wait_ge(dT_sb, g + 1)
                if not (isinstance(g, int) and g == 0):
                    pe.wait_ge(hd_sb, g)
                for t in range(TG):
                    last = mm(bank(3)[:, t * P:(t + 1) * P], dT[:, t, :], wnT[:], start=True, stop=True)
                last.then_inc(hd_ps, 1)

            def sums(g, s, add):
                pe.wait_ge(diag0, g + 1)
                if not (isinstance(g, int) and g == 0):
                    pe.wait_ge(s1_sb, g)
                parts = [(gx[:, s, t, 0:D], oh[:, s, t, :], t) for t in range(TG)] + [(xg[:, s, t, :], diag[:, s, t, :], t) for t in range(TG)]
                for k, (l, r, t) in enumerate(parts):
                    last = mm(bank(4)[:, t * P:(t + 1) * P], l, r, start=(k == 0), stop=True, skip_group_check=True)
                    if k == 0:
                        with pe.If(general > 0):
                            pe.wait_ge(accl, 16 * g + 16)
                            for u in range(TG):
                                mm(bank(4)[:, u * P:(u + 1) * P], accg[:, u, 0:D], ident[:], start=False, stop=True, skip_group_check=True)
                last.then_inc(s1_ps, 1)

            def abs_sums(g, s):
                pe.wait_ge(hd_sb, g + 1)
                if not (isinstance(g, int) and g == 0):
                    pe.wait_ge(s2_sb, g)
                for t in range(TG):
                    last = mm(bank(5)[:, t * P:(t + 1) * P], hd[:, t, :], oh[:, s, t, :], start=(t == 0), stop=True,
                              skip_group_check=True)
                    if t == 0:
                        with pe.If(general > 0):
                            pe.wait_ge(accl, 16 * g + 16)
                            for u in range(TG):
                                acc = mm(bank(5)[:, u * P:(u + 1) * P], accg[:, u, D:2 * D], ident[:], start=False, stop=True,
                                         skip_group_check=True)
                            acc.then_inc(acc_rd, 1)
                last.then_inc(s2_ps, 1)

            def z_x(g, s, half):
                pe.wait_ge(xT_sb, g + 1)
                pe.wait_ge(s1_sb, g + 1)
                pe.wait_ge(rl[s], landed(g, s, 16, half) if not (isinstance(g, int) and g == NG - 1) else 16 * (NG // 2))
                if not (isinstance(g, int) and g == 0):
                    pe.wait_ge(z_rd, g)
                def z(t):
                    return psum[:, 3072 + 256 * t:3072 + 256 * (t + 1)]

                for t in range(TG):
                    mm(z(t)[:, 0:D], row0s[:, s, t * P:(t + 1) * P], bias0[:, :], start=(t % 2 == 0), stop=True, skip_group_check=True)
                for t in range(TG):
                    mm(z(t), xT[s][:, t, :], wz[:], start=False, stop=True, skip_group_check=True)
                    mm(z(t)[:, D:2 * D], s1T[:, t, :], wsum[:], start=False, stop=True, skip_group_check=True)

            def z_abs(g, s):
                pe.wait_ge(s2_sb, g + 1)
                for t in range(TG):
                    o = psum[:, 3072 + 256 * t + D:3072 + 256 * (t + 1)]
                    last = mm(o, s2T[:, t, :], wabs[:], start=False, stop=True, skip_group_check=True)
                last.then_inc(z_ps, 1)

            def l0_step(g, s, half, nxt_half, more=True):
                abs_sums(g, s)
                if more:
                    transposes(g + 1, 1 - s, nxt_half)
                z_x(g, s, half)
                if more:
                    differences(g + 1, 1 - s, nxt_half)
                z_abs(g, s)
                if more:
                    edge_products(g + 1, 1 - s)
                    sums(g + 1, 1 - s, None)

            transposes(0, 0, None)
            differences(0, 0, None)
            edge_products(0, 0)
            sums(0, 0, None)
            l0_step(0, 0, None, None)
            l0_step(1, 1, None, None)
            with pe.Fori(1, NG // 2 - 1) as i:
                l0_step(2 * i, 0, i + 1, i + 1)
                l0_step(2 * i + 1, 1, i + 1, i + 2)
            l0_step(NG - 2, 0, None, None)
            l0_step(NG - 1, 1, None, None, more=False)

            with pe.If(general > 0):
                pe.wait_ge(z_rd, NG)
                with pe.Fori(0, NC) as k:
                    pe.wait_ge(g_dif, 2 * k + (4 * NC + 1))
                    nc.tensor.transpose(bank(0)[:, 0:P], e_keyb[:], ident[:]).then_inc(g_pe, 1)
                    pe.wait_ge(g_dif, 2 * k + (4 * NC + 2))
                    mm(bank(3)[:, 0:W], e_same[:], e_pay[:, 0:W], start=True, stop=True).then_inc(g_pe, 1)
                pe.wait_ge(g_idx, 4 * NC)

            def l1_sums(g, s):
                first = isinstance(g, int) and g == 0
                pe.wait_ge(oh1, g + 1)
                pe.wait_ge(diag_rdy, g + 1)
                if not first:
                    pe.wait_ge(yT_sb, g)
                    pe.wait_ge(gam_rd, g)
                for t in range(TG):
                    o = bank(0)[:, t * P:(t + 1) * P]
                    mm(bank(3)[:, t:t + 1], oh[:, s, t, :], ones[:, 0:1], start=(t == 0), stop=True, skip_group_check=True)
                    mm(o, gx[:, s, t, 0:D], oh[:, s, t, :], start=(t == 0), stop=True, skip_group_check=True)
                    if t == 0:
                        with pe.If(general > 0):
                            pe.wait_ge(accl, 16 * g + (16 * NG + 16))
                            for u in range(TG):
                                mm(bank(0)[:, u * P:(u + 1) * P], accg[:, u, 0:D], ident[:], start=False, stop=True, skip_group_check=True)
                                acc = mm(bank(3)[:, u:u + 1], ident[:], accg[:, u, D:W], start=False, stop=True, skip_group_check=True)
                            acc.then_inc(acc_rd, 1)
                    last = mm(o, h1g[:, s, t, 0:D], diag[:, s, t, :], start=False, stop=True, skip_group_check=True)
                last.then_inc(yT_ps, 1)

            def l1_transposes(g, s, half):
                first = isinstance(g, int) and g == 0
                pe.wait_ge(hl[s], landed(g, s, 16, half))
                if not first:
                    pe.wait_ge(hT_sb, g)
                for t in range(TG):
                    last = nc.tensor.transpose(bank(1)[:, t * P:(t + 1) * P], h1g[:, s, t, 0:D], ident[:])
                last.then_inc(hT_ps, 1)

            def l1_g(g, s):
                pe.wait_ge(yT_sb, g + 1)
                if not (isinstance(g, int) and g == 0):
                    pe.wait_ge(g_sb, g)
                for t in range(TG):
                    last = mm(psum[:, 2048 + 256 * t:2048 + 256 * (t + 1)], yT(t), wg[:], start=(t % 2 == 0), stop=True, skip_group_check=True)
                last.then_inc(g_ps, 1)

            def yT(t):
                return s1T[:, t, :]

            def l1_x(g, b, used, done):
                k = b - 6
                if not (isinstance(g, int) and g == 0):
                    pe.wait_ge(used, g)
                mm(bank(b), ones16[:, :], bias1[:, k * D:(k + 1) * D].unsqueeze(1).broadcast_to([BP, TG, D]),
                   start=True, stop=True, skip_group_check=True)
                for t in range(TG):
                    last = mm(bank(b)[:, t * P:(t + 1) * P], xT[0][:, t, :], wx[:, k * D:(k + 1) * D],
                              start=False, stop=True, skip_group_check=True)
                last.then_inc(done, 1)

            def l1_step(g, s, half):
                l1_transposes(g, s, half)
                l1_sums(g, s)
                pe.wait_ge(hT_sb, g + 1)
                l1_x(g, 7, ay2_rdy, xi_ps)
                l1_g(g, s)
                l1_x(g, 6, x_rd, xh_ps)

            l1_step(0, 0, None)
            l1_step(1, 1, None)
            with pe.Fori(1, NG // 2 - 1) as i:
                l1_step(2 * i, 0, i + 1)
                l1_step(2 * i + 1, 1, i + 1)
            l1_step(NG - 2, 0, None)
            l1_step(NG - 1, 1, None)

        @block.scalar
        def _(act):
            a = nc.scalar
            def place_stage(i, s):
                a.copy(step_v[:, s], chunk_v[:, bass.ds(i * CB, CB)]).then_inc(p_staged, 1)

            def place_copy(i, s, b):
                act.wait_ge(placed, i + 1)
                if NCP // CB > 2 and not (isinstance(i, int) and i + 2 >= NCP // CB):
                    place_stage(i + 2, s)
                a.copy(fields[:, :, bass.ds(i * CB - b * P, CB)],
                       bank(s)[:, 0:2 * 4 * CB].rearrange("p (f c) -> p f c", f=8)).then_inc(p_copied, 1)

            act.wait_ge(place, 1)
            place_stage(0, 0)
            place_stage(1, 1)
            at = 0
            for b in range(NB):
                steps = min(P, NCP - b * P) // CB
                n2 = steps // 2 - (b == NB - 1)
                if b:
                    act.wait_ge(fieldT, b)
                with act.Fori(0, n2) as i:
                    for s in range(2):
                        place_copy(2 * i + (at + s), s, b)
                for i in range(at + 2 * n2, at + steps):
                    place_copy(i, i % 2, b)
                at += steps
            act.wait_ge(tab1, 1)

            def sort_stage(i, s, first=False):
                if not first:
                    act.wait_ge(s_src, CB * i - CB)
                a.copy(sort_s[:, s], sort_f[:, bass.ds(i * CB, CB), :]).then_inc(s_staged, 1)

            def sort_values(i, s):
                for c in range(CB):
                    col = bass.ds(CB * i + c, 1)
                    if not (isinstance(i, int) and i == 0):
                        act.wait_ge(s_done, CB * i + (c + 1 - CB))
                    act.wait_ge(s_roh, CB * i + (c + 1))
                    a.activation(hi_oh[:, c, :], rank_oh[:, c, :], ACT.Copy, scale=sort_f[:, col, 2:3].rearrange("p a b -> p (a b)"))
                    a.activation(lo_oh[:, c, :], rank_oh[:, c, :], ACT.Copy, scale=sort_f[:, col, 3:4].rearrange("p a b -> p (a b)")).then_inc(s_val, 1)

            sort_stage(0, 0, True)
            sort_stage(1, 1, True)
            sort_values(0, 0)
            sort_stage(2, 0)
            sort_values(1, 1)
            sort_stage(3, 1)
            with act.Fori(1, NT // CB // 2 - 1) as i:
                for s in range(2):
                    sort_values(2 * i + s, s)
                    sort_stage(2 * i + (2 + s), s)
            for i in (NT // CB - 2, NT // CB - 1):
                sort_values(i, i % 2)

            def copy4(dst, b, func=ACT.Copy):
                return a.activation(dst, bank(b).rearrange("p (t n) -> p t n", t=TG), func)

            def l0_front(g, s):
                act.wait_ge(trans, g + 1)
                if not (isinstance(g, int) and g == 0):
                    act.wait_ge(dT_ps, g)
                copy4(ohT[:], 1).then_inc(ohT_sb, 1)
                copy4(hd[:], 3).then_inc(gxT_sb, 1)
                if not (isinstance(g, int) and g < 2):
                    act.wait_ge(z_ps, g - 1)
                copy4(xT[s], 0).then_inc(xT_sb, 1)

            def l0_sum_copy(g):
                act.wait_ge(s1_ps, g + 1)
                if not (isinstance(g, int) and g == 0):
                    act.wait_ge(z_ps, g)
                copy4(s1T[:], 4).then_inc(s1_sb, 1)

            def l0_abs(g):
                act.wait_ge(hd_ps, g + 1)
                if not (isinstance(g, int) and g == 0):
                    act.wait_ge(s2_ps, g)
                copy4(hd[:], 3, ACT.Abs).then_inc(hd_sb, 1)

            def l0_p2(g):
                act.wait_ge(z_ps, g + 1)
                if not (isinstance(g, int) and g == 0):
                    act.wait_ge(z_rd, g)
                for t in range(TG):
                    last = a.activation(p2[:, t, :], psum[:, 3072 + 256 * t + D:3072 + 256 * (t + 1)], ACT.Copy,
                                        scale=rc[:, bass.ds(TG * g + t, 1)])
                last.then_inc(p2_sb, 1)

            def l0_diag(g, s, first):
                if not first:
                    act.wait_ge(s1_ps, g - 1)
                for t in range(TG):
                    last = a.activation(diag[:, s, t, :], ident[:], ACT.Copy, scale=n_self[:, bass.ds(TG * g + t, 1)])
                last.then_inc(diag0, 1)

            def l0_step(g, s, more=2):
                if more > 0:
                    l0_front(g + 1, 1 - s)
                l0_p2(g)
                if more > 0:
                    l0_abs(g + 1)
                    l0_sum_copy(g + 1)
                if more > 1:
                    l0_diag(g + 2, s, False)

            act.wait_ge(n_self_rdy, 1)
            l0_diag(0, 0, True)
            l0_front(0, 0)
            l0_abs(0)
            l0_sum_copy(0)
            l0_diag(1, 1, True)
            l0_step(0, 0)
            l0_step(1, 1)
            with act.Fori(1, NG // 2 - 1) as i:
                for s in range(2):
                    l0_step(2 * i + s, s)
            l0_step(NG - 2, 0, 1)
            l0_step(NG - 1, 1, 0)

            def l1_diag(g, s):
                if not (isinstance(g, int) and g < 2):
                    act.wait_ge(yT_ps, g - 1)
                for t in range(TG):
                    last = a.activation(diag[:, s, t, :], ident[:], ACT.Copy, scale=self_w[:, bass.ds(TG * g + t, 1)])
                last.then_inc(diag_rdy, 1)

            def l1_copyh(g):
                first = isinstance(g, int) and g == 0
                act.wait_ge(hT_ps, g + 1)
                if not first:
                    act.wait_ge(xh_ps, g)
                copy4(xT[0], 1).then_inc(hT_sb, 1)

            def l1_copyy(g):
                first = isinstance(g, int) and g == 0
                act.wait_ge(yT_ps, g + 1)
                if not first:
                    act.wait_ge(g_ps, g)
                copy4(s1T[:], 0).then_inc(yT_sb, 1)

            def l1_scale(g):
                act.wait_ge(g_ps, g + 1)
                if not (isinstance(g, int) and g == 0):
                    act.wait_ge(q_rdy, g)
                for t in range(TG):
                    last = a.activation(gs[:, t, :], psum[:, 2048 + 256 * t:2048 + 256 * (t + 1)], ACT.Copy,
                                        scale=dinv[:, bass.ds(TG * g + t, 1)])
                last.then_inc(g_sb, 1)

            def gate(k):
                return a.activation(gates[:, k, :], dots[:, k, :], ACT.Sigmoid, bias=vec[:, 5 * D + k:5 * D + k + 1])

            def l1_own_gate(g):
                act.wait_ge(dots2_rdy, g + 1)
                gate(2).then_inc(gate2_rdy, 1)
                act.wait_ge(gate2_rdy, g + 1)
                if not (isinstance(g, int) and g == 0):
                    act.wait_ge(own_rdy, g)
                for t in range(TG):
                    last = a.activation(ay[:, 2, t, :], bank(7)[:, t * P:(t + 1) * P], ACT.Relu,
                                        scale=gates[:, 2, t:t + 1])
                last.then_inc(ay2_rdy, 1)

            def l1_gates(g, s):
                act.wait_ge(dots_rdy, g + 1)
                gate(0)
                gate(1).then_inc(gate_rdy, 1)
                act.wait_ge(gate_rdy, g + 1)
                if not (isinstance(g, int) and g == 0):
                    act.wait_ge(nb_rdy, g)
                for k in range(2):
                    for t in range(TG):
                        last = a.activation(ay[:, k, t, :], q[:, s, t, k * D:(k + 1) * D], ACT.Relu, scale=gates[:, k, t:t + 1])
                last.then_inc(ay_rdy, 1)

            def l1_step(g, s, more=2):
                l1_scale(g)
                l1_own_gate(g)
                if more > 0:
                    l1_copyh(g + 1)
                    l1_copyy(g + 1)
                if more > 1:
                    l1_diag(g + 2, s)
                l1_gates(g, s)

            l1_diag(0, 0)
            l1_diag(1, 1)
            l1_copyh(0)
            l1_copyy(0)
            l1_step(0, 0)
            l1_step(1, 1)
            with act.Fori(1, NG // 2 - 1) as i:
                for s in range(2):
                    l1_step(2 * i + s, s)
            l1_step(NG - 2, 0, 1)
            l1_step(NG - 1, 1, 0)


_INS = ['x', 'src', 'dst', 'L0_gnn_W_neigh', 'L0_gnn_b_neigh', 'L0_gnn_W_edge', 'L0_gnn_b_edge', 'L0_gnn_W_lin',
        'L0_gnn_b_lin', 'L1_gnn_W_hp', 'L1_gnn_b_hp', 'L1_gnn_W_lp', 'L1_gnn_b_lp', 'L1_gnn_W_i', 'L1_gnn_b_i',
        'L1_gnn_wlin_h', 'L1_gnn_blin_h', 'L1_gnn_wlin_l', 'L1_gnn_blin_l', 'L1_gnn_wlin_i', 'L1_gnn_blin_i']


def kernel(**inputs):
    import numpy as np
    import concourse.bacc as bacc
    from concourse import mybir
    from concourse.bass_utils import run_bass_kernel_spmd

    nc = bacc.Bacc("TRN2", target_bir_lowering=False, num_devices=1)
    arrays, args = {}, []
    for name in _INS:
        a = np.ascontiguousarray(inputs[name])
        a = a.reshape(a.shape if a.ndim else (1,))
        arrays[f"in_{name}"] = a
        args.append(nc.dram_tensor(f"in_{name}", a.shape, mybir.dt.from_np(a.dtype), kind="ExternalInput").ap())
    out = nc.dram_tensor("out", inputs["x"].shape, mybir.dt.float32, kind="ExternalOutput").ap()
    build(nc, *args, out)
    r = run_bass_kernel_spmd(nc, [arrays], core_ids=[0])
    return r.results[0]["out"]
```
